# Optimizing a Trainium2 kernel written in Bass

```python
import numpy as np
import jax
import jax.numpy as jnp

def _softmax(x, axis=-1):
    return jax.nn.softmax(x, axis=axis)

def _gelu(x):
    return jax.nn.gelu(x, approximate=True)

def _silu(x):
    return jax.nn.silu(x)

def _sigmoid(x):
    return jax.nn.sigmoid(x)

def _layernorm(x, axis=-1, eps=1e-05):
    m = jnp.mean(x, axis=axis, keepdims=True)
    v = jnp.var(x, axis=axis, keepdims=True)
    return (x - m) / jnp.sqrt(v + eps)

def _scatter_add(tgt, idx, src, axis=0):
    return tgt.at[idx].add(src)

def _segment_sum(src, seg, n):
    return jax.ops.segment_sum(src, seg, n)
kernel_name = 'mk_decoder_preln_d4_seqx_r8_8d0b15'

def setup_inputs(seed: int=0):
    np.random.seed(seed)
    _w = jnp.asarray

    def _rec_inputs():
        import jax
        import jax.numpy as jnp
        _rk = jax.random.key(seed)
        x = 4.136e-05 + 0.9999 * jax.random.normal(jax.random.fold_in(_rk, 1), (4, 256, 256), jnp.float32)
        _lenS = 256 - jax.random.randint(jax.random.fold_in(_rk, 7), (4,), 0, max(1, 256 // 4) + 1, jnp.int32)
        _lenS2 = 256 - jax.random.randint(jax.random.fold_in(_rk, 8), (4,), 0, max(1, 256 // 4) + 1, jnp.int32)
        _ctx_1024P = jax.random.normal(jax.random.fold_in(_rk, 11), (4, 16, 128), jnp.float32)
        _ctx_1024c = jax.random.dirichlet(jax.random.fold_in(_rk, 511), 0.3 * jnp.ones((16,), jnp.float32), (4, 256))
        _ctx_1024t = jnp.einsum('bsk,bkd->bsd', _ctx_1024c, _ctx_1024P)
        _ctx_1024t = _ctx_1024t * jax.lax.rsqrt(jnp.mean(jnp.square(_ctx_1024t)) + 1e-12) * 0.953939
        ctx_1024 = -0.000292821 + 1.00034 * (_ctx_1024t + 0.3 * jax.random.normal(jax.random.fold_in(_rk, 611), (4, 256, 128), jnp.float32))
        fside_BxSx2_0 = jax.random.uniform(jax.random.fold_in(_rk, 12), (4, 256, 2), jnp.float32, 0.0, 0.999707)
        return (x, ctx_1024, fside_BxSx2_0)
    x, ctx_1024, fside_BxSx2_0 = _rec_inputs()

    def _L0_attn_setup():
        import jax, jax.numpy as jnp
        import numpy as np
        B, L, D, H = (4, 512, 256, 16)
        HD = D // H
        EPS = 1e-09

        def phi(x):
            return jax.nn.elu(x) + 1.0
        key = jax.random.key(seed)
        k1, k2, k3 = jax.random.split(key, 3)
        x = jax.random.normal(k1, (B, L, D), dtype=jnp.float32)
        W_qkv = jax.random.normal(k2, (3 * D, D), dtype=jnp.float32) * D ** (-0.5)
        W_out = jax.random.normal(k3, (D, D), dtype=jnp.float32) * D ** (-0.5)
        return {'x': x, 'W_qkv': W_qkv, 'W_out': W_out}
    _L0_attn_all = _L0_attn_setup()
    _L0_attn_in = {k: v for k, v in _L0_attn_all.items() if k in ('W_qkv', 'W_out')}
    del _L0_attn_all

    def _L0_xattn_setup():
        import jax, jax.numpy as jnp
        import numpy as np
        import math
        B, L, DM = (2, 256, 128)
        DS, DC, EXP = (16, 4, 2)
        DI = EXP * DM
        DR = math.ceil(DM / 16)
        DT_MIN, DT_MAX, DT_FLOOR = (0.001, 0.1, 0.0001)

        def _ssm_forward(hidden_states, z, in_proj_w, conv_w, conv_b, x_proj_w, dt_proj_w, dt_proj_b, A_log, D):
            b = hidden_states.shape[0]
            x = jnp.einsum('ed,bld->bel', in_proj_w, hidden_states)
            xp = jnp.pad(x, ((0, 0), (0, 0), (DC - 1, 0)))
            xc = jax.lax.conv_general_dilated(xp, conv_w[:, None, :], window_strides=(1,), padding='VALID', dimension_numbers=('NCH', 'OIH', 'NCH'), feature_group_count=DI)
            u = jax.nn.silu(xc + conv_b[None, :, None])
            x_dbl = jnp.einsum('ke,bel->bkl', x_proj_w, u)
            dt_lo = x_dbl[:, :DR]
            Bm = x_dbl[:, DR:DR + DS]
            Cm = x_dbl[:, DR + DS:]
            delta = jax.nn.softplus(jnp.einsum('er,brl->bel', dt_proj_w, dt_lo) + dt_proj_b[None, :, None])
            A = -jnp.exp(A_log)

            def step(state, xs):
                d_t, B_t, C_t, u_t = xs
                dA = jnp.exp(d_t[..., None] * A)
                state = state * dA + (d_t * u_t)[..., None] * B_t[:, None, :]
                y_t = jnp.einsum('ben,bn->be', state, C_t)
                return (state, y_t)
            xs = (jnp.moveaxis(delta, -1, 0), jnp.moveaxis(Bm, -1, 0), jnp.moveaxis(Cm, -1, 0), jnp.moveaxis(u, -1, 0))
            state0 = jnp.zeros((b, DI, DS), delta.dtype)
            _, ys = jax.lax.scan(step, state0, xs)
            y = jnp.moveaxis(ys, 0, -1)
            y = y + D[None, :, None] * u
            y = y * jax.nn.silu(z)
            return jnp.swapaxes(y, 1, 2)
        key = jax.random.key(seed)
        ks = jax.random.split(key, 8)
        hidden_states = jax.random.normal(ks[0], (B, L, DM), jnp.float32)
        z = jax.random.normal(ks[1], (B, DI, L), jnp.float32)
        in_proj_w = jax.random.normal(ks[2], (DI, DM), jnp.float32) * DM ** (-0.5)
        conv_w = jax.random.normal(ks[3], (DI, DC), jnp.float32) * DC ** (-0.5)
        conv_b = jnp.zeros((DI,), jnp.float32)
        x_proj_w = jax.random.normal(ks[4], (DR + 2 * DS, DI), jnp.float32) * DI ** (-0.5)
        dt_std = DR ** (-0.5)
        dt_proj_w = jax.random.uniform(ks[5], (DI, DR), jnp.float32, -dt_std, dt_std)
        dt = jnp.exp(jax.random.uniform(ks[6], (DI,), jnp.float32) * (math.log(DT_MAX) - math.log(DT_MIN)) + math.log(DT_MIN))
        dt = jnp.clip(dt, DT_FLOOR)
        dt_proj_b = dt + jnp.log(-jnp.expm1(-dt))
        A_log = jnp.log(jnp.broadcast_to(jnp.arange(1, DS + 1, dtype=jnp.float32), (DI, DS)))
        D = jnp.ones((DI,), jnp.float32)
        return dict(hidden_states=hidden_states, z=z, in_proj_w=in_proj_w, conv_w=conv_w, conv_b=conv_b, x_proj_w=x_proj_w, dt_proj_w=dt_proj_w, dt_proj_b=dt_proj_b, A_log=A_log, D=D)
    _L0_xattn_all = _L0_xattn_setup()
    _L0_xattn_in = {k: v for k, v in _L0_xattn_all.items() if k in ('in_proj_w', 'conv_w', 'conv_b', 'x_proj_w', 'dt_proj_w', 'dt_proj_b', 'A_log', 'D')}
    del _L0_xattn_all

    def _L0_ffn_setup():
        import jax, jax.numpy as jnp
        import numpy as np
        B, S, D = (2, 256, 256)
        MOE_D = 176
        E = 16
        K = 6
        ALPHA = 0.001

        def _moe_forward(x, gate_w, w_gate, w_up, w_down):
            b, s, d = x.shape
            T = b * s
            h = x.reshape(T, d)
            logits = h @ gate_w.T
            scores = jax.nn.softmax(logits.astype(jnp.float32), axis=-1)
            topk_w, topk_idx = jax.lax.top_k(scores, K)
            cw = jnp.zeros((T, E), jnp.float32)
            cw = cw.at[jnp.arange(T)[:, None], topk_idx].add(topk_w)
            y = jnp.zeros((T, d), x.dtype)
            for e in range(E):
                g = h @ w_gate[e].T
                u = h @ w_up[e].T
                out = jax.nn.silu(g) * u @ w_down[e].T
                y = y + cw[:, e:e + 1].astype(x.dtype) * out
            counts = jnp.sum(jax.nn.one_hot(topk_idx.reshape(b, s * K), E, dtype=jnp.float32), axis=1)
            ce = counts * (E / (s * K))
            scores_bse = scores.reshape(b, s, E)
            aux = jnp.mean(jnp.sum(ce * scores_bse.mean(axis=1), axis=1)) * ALPHA
            return (y.reshape(b, s, d), aux)
        key = jax.random.key(seed)
        ks = jax.random.split(key, 5)
        sd = 1.0 / np.sqrt(D)
        sm = 1.0 / np.sqrt(MOE_D)
        return {'x': jax.random.normal(ks[0], (B, S, D), jnp.float32), 'gate_w': jax.random.normal(ks[1], (E, D), jnp.float32) * sd, 'w_gate': jax.random.normal(ks[2], (E, MOE_D, D), jnp.float32) * sd, 'w_up': jax.random.normal(ks[3], (E, MOE_D, D), jnp.float32) * sd, 'w_down': jax.random.normal(ks[4], (E, D, MOE_D), jnp.float32) * sm}
    _L0_ffn_all = _L0_ffn_setup()
    _L0_ffn_in = {k: v for k, v in _L0_ffn_all.items() if k in ('gate_w', 'w_gate', 'w_up', 'w_down')}
    del _L0_ffn_all

    def _L1_attn_setup():
        import jax, jax.numpy as jnp
        import numpy as np
        D_MODEL = 256
        NUM_HEADS = 16
        D_K = D_MODEL // NUM_HEADS
        SEQ = 256
        BATCH = 2
        THETA = 10000.0

        def _rope_tables(seq_len, d_k, theta, dtype):
            pos = jnp.arange(seq_len, dtype=dtype)[:, None]
            inv = theta ** (-(jnp.arange(0, d_k, 2, dtype=dtype) / d_k))
            ang = pos * inv
            sin = jnp.repeat(jnp.sin(ang), 2, axis=1)
            cos = jnp.repeat(jnp.cos(ang), 2, axis=1)
            return (sin, cos)

        def _apply_rope(x, sin, cos):
            xp = x.reshape(x.shape[:-1] + (x.shape[-1] // 2, 2))
            swapped = jnp.stack((-xp[..., 1], xp[..., 0]), axis=-1).reshape(x.shape)
            return x * cos + swapped * sin
        key = jax.random.key(seed)
        ks = jax.random.split(key, 5)
        s = 1.0 / np.sqrt(D_MODEL)
        return {'x': jax.random.normal(ks[0], (BATCH, SEQ, D_MODEL), jnp.float32), 'wq': jax.random.normal(ks[1], (D_MODEL, D_MODEL), jnp.float32) * s, 'wk': jax.random.normal(ks[2], (D_MODEL, D_MODEL), jnp.float32) * s, 'wv': jax.random.normal(ks[3], (D_MODEL, D_MODEL), jnp.float32) * s, 'wo': jax.random.normal(ks[4], (D_MODEL, D_MODEL), jnp.float32) * s}
    _L1_attn_all = _L1_attn_setup()
    _L1_attn_in = {k: v for k, v in _L1_attn_all.items() if k in ('wq', 'wk', 'wv', 'wo')}
    del _L1_attn_all

    def _L1_xattn_setup():
        import jax, jax.numpy as jnp
        import numpy as np
        B_, L_, D_MODEL = (4, 256, 128)
        D_STATE, D_CONV, EXPAND = (16, 4, 2)
        D_INNER = EXPAND * D_MODEL
        DT_RANK = (D_MODEL + 15) // 16

        def silu(x):
            return x * jax.nn.sigmoid(x)
        key = jax.random.key(seed)
        ks = jax.random.split(key, 10)
        f32 = jnp.float32
        hidden_states = jax.random.normal(ks[0], (B_, L_, D_MODEL), dtype=f32)
        z = jax.random.normal(ks[1], (B_, D_INNER, L_), dtype=f32)
        in_proj_w = jax.random.normal(ks[2], (D_INNER, D_MODEL), dtype=f32) * 0.02
        conv_w = jax.random.normal(ks[3], (D_INNER, 1, D_CONV), dtype=f32) * 0.1
        conv_b = jax.random.normal(ks[4], (D_INNER,), dtype=f32) * 0.02
        x_proj_w = jax.random.normal(ks[5], (DT_RANK + 2 * D_STATE, D_INNER), dtype=f32) * 0.02
        dt_proj_w = jax.random.uniform(ks[6], (D_INNER, DT_RANK), dtype=f32, minval=-DT_RANK ** (-0.5), maxval=DT_RANK ** (-0.5))
        dt = jnp.exp(jax.random.uniform(ks[7], (D_INNER,), dtype=f32, minval=np.log(0.001), maxval=np.log(0.1)))
        dt_proj_b = jnp.log(jnp.expm1(dt))
        A_log = jnp.log(jnp.broadcast_to(jnp.arange(1, D_STATE + 1, dtype=f32), (D_INNER, D_STATE)))
        D = jnp.ones((D_INNER,), f32)
        return {'hidden_states': hidden_states, 'z': z, 'in_proj_w': in_proj_w, 'conv_w': conv_w, 'conv_b': conv_b, 'x_proj_w': x_proj_w, 'dt_proj_w': dt_proj_w, 'dt_proj_b': dt_proj_b, 'A_log': A_log, 'D': D}
    _L1_xattn_all = _L1_xattn_setup()
    _L1_xattn_in = {k: v for k, v in _L1_xattn_all.items() if k in ('in_proj_w', 'conv_w', 'conv_b', 'x_proj_w', 'dt_proj_w', 'dt_proj_b', 'A_log', 'D')}
    del _L1_xattn_all

    def _L1_ffn_setup():
        import jax, jax.numpy as jnp
        import numpy as np
        _FP8_MAX = 448.0
        _BLOCK = 32
        _EPS = 1e-30

        def _mx_dequant(t):
            rows, feat = t.shape
            blocks = t.reshape(rows, feat // _BLOCK, _BLOCK)
            max_abs = jnp.max(jnp.abs(blocks), axis=-1)
            scales = jnp.maximum(max_abs / _FP8_MAX, _EPS)
            q = (blocks / scales[..., None]).astype(jnp.float8_e4m3fn).astype(jnp.float32)
            return (q * scales[..., None]).reshape(rows, feat)

        def _mx_linear(x2d, w):
            return _mx_dequant(x2d) @ _mx_dequant(w).T
        key = jax.random.key(seed)
        k1, k2, k3, k4 = jax.random.split(key, 4)
        B, S, H, I = (2, 128, 256, 1024)
        return {'x': jax.random.normal(k1, (B, S, H), dtype=jnp.float32), 'gate_w': jax.random.normal(k2, (I, H), dtype=jnp.float32) * 0.02, 'up_w': jax.random.normal(k3, (I, H), dtype=jnp.float32) * 0.02, 'down_w': jax.random.normal(k4, (H, I), dtype=jnp.float32) * 0.02}
    _L1_ffn_all = _L1_ffn_setup()
    _L1_ffn_in = {k: v for k, v in _L1_ffn_all.items() if k in ('gate_w', 'up_w', 'down_w')}
    del _L1_ffn_all

    def _L2_attn_setup():
        import math
        import jax, jax.numpy as jnp
        import numpy as np
        HID = 256
        H = 16
        HKV = 8
        D = HID // H
        F = D
        SEQ = 256
        BATCH = 2
        THETA = 10000.0

        def _rotate_half(x):
            x1, x2 = (x[..., :x.shape[-1] // 2], x[..., x.shape[-1] // 2:])
            return jnp.concatenate((-x2, x1), axis=-1)

        def _softmax_kernel(x, R):
            n = jnp.sqrt(jnp.sum(x * x, axis=-1, keepdims=True))
            x = x / jnp.maximum(n, 1e-06)
            p = jnp.einsum('...d,ed->...e', x, R)
            feats = jnp.concatenate([jnp.sin(p), jnp.cos(p)], axis=-1)
            return feats / math.sqrt(F)
        key = jax.random.key(seed)
        ks = jax.random.split(key, 10)
        s = lambda k, shape, scale=0.02: jax.random.normal(k, shape, dtype=jnp.float32) * scale
        return {'hidden_states': jax.random.normal(ks[0], (BATCH, SEQ, HID), dtype=jnp.float32), 'Wq': s(ks[1], (HID, HID)), 'bq': s(ks[2], (HID,)), 'Wk': s(ks[3], (HKV * D, HID)), 'bk': s(ks[4], (HKV * D,)), 'Wv': s(ks[5], (HKV * D, HID)), 'bv': s(ks[6], (HKV * D,)), 'Wo': s(ks[7], (HID, HID)), 'bo': s(ks[8], (HID,)), 'rand_matrix': jax.random.normal(ks[9], (F // 2, D), dtype=jnp.float32)}
    _L2_attn_all = _L2_attn_setup()
    _L2_attn_in = {k: v for k, v in _L2_attn_all.items() if k in ('Wq', 'bq', 'Wk', 'bk', 'Wv', 'bv', 'Wo', 'bo', 'rand_matrix')}
    del _L2_attn_all

    def _L2_xattn_setup():
        import jax, jax.numpy as jnp
        import numpy as np
        key = jax.random.key(seed)
        ks = jax.random.split(key, 6)
        B, L, N, C, D = (8, 64, 256, 128, 128)
        return {'teacher_logits': jax.random.normal(ks[0], (B, L, N), dtype=jnp.float32), 'teacher_features': jax.random.normal(ks[1], (B, N, C), dtype=jnp.float32), 'Wq': jax.random.normal(ks[2], (D, C), dtype=jnp.float32) * (1.0 / np.sqrt(C)), 'bq': jnp.zeros((D,), dtype=jnp.float32), 'Wk': jax.random.normal(ks[3], (D, C), dtype=jnp.float32) * (1.0 / np.sqrt(C)), 'bk': jnp.zeros((D,), dtype=jnp.float32)}
    _L2_xattn_all = _L2_xattn_setup()
    _L2_xattn_in = {k: v for k, v in _L2_xattn_all.items() if k in ('Wq', 'bq', 'Wk', 'bk')}
    del _L2_xattn_all

    def _L2_ffn_setup():
        import jax, jax.numpy as jnp
        import numpy as np
        B, S, H = (2, 128, 256)
        E, K = (8, 2)
        I = 176
        IS = 704
        WSCALE = 0.02
        key = jax.random.key(seed)
        ks = jax.random.split(key, 9)
        f32 = jnp.float32
        return {'hidden_states': jax.random.normal(ks[0], (B, S, H), dtype=f32), 'gate_w': jax.random.normal(ks[1], (E, H), dtype=f32) * WSCALE, 'w_gate': jax.random.normal(ks[2], (E, H, I), dtype=f32) * WSCALE, 'w_up': jax.random.normal(ks[3], (E, H, I), dtype=f32) * WSCALE, 'w_down': jax.random.normal(ks[4], (E, I, H), dtype=f32) * WSCALE, 'sw_gate': jax.random.normal(ks[5], (H, IS), dtype=f32) * WSCALE, 'sw_up': jax.random.normal(ks[6], (H, IS), dtype=f32) * WSCALE, 'sw_down': jax.random.normal(ks[7], (IS, H), dtype=f32) * WSCALE, 'shared_gate_w': jax.random.normal(ks[8], (H, 1), dtype=f32) * WSCALE}
    _L2_ffn_all = _L2_ffn_setup()
    _L2_ffn_in = {k: v for k, v in _L2_ffn_all.items() if k in ('gate_w', 'w_gate', 'w_up', 'w_down', 'sw_gate', 'sw_up', 'sw_down', 'shared_gate_w')}
    del _L2_ffn_all

    def _L3_attn_setup():
        import jax, jax.numpy as jnp
        import numpy as np
        B, S, D = (4, 512, 256)
        DECAY_BIAS_INIT = -4.0
        W_SCALE = 0.02
        key = jax.random.key(seed)
        ks = jax.random.split(key, 6)
        return {'x': jax.random.normal(ks[0], (B, S, D), dtype=jnp.float32), 'W_in': jax.random.normal(ks[1], (D, D), dtype=jnp.float32) * W_SCALE, 'b_in': jnp.zeros((D,), jnp.float32), 'W_decay': jax.random.normal(ks[2], (D, D), dtype=jnp.float32) * W_SCALE, 'b_decay': jnp.zeros((D,), jnp.float32), 'W_gate': jax.random.normal(ks[3], (D, D), dtype=jnp.float32) * W_SCALE, 'b_gate': jnp.zeros((D,), jnp.float32), 'W_out': jax.random.normal(ks[4], (D, D), dtype=jnp.float32) * W_SCALE, 'b_out': jnp.zeros((D,), jnp.float32), 'decay_bias': jnp.full((D,), DECAY_BIAS_INIT, jnp.float32)}
    _L3_attn_all = _L3_attn_setup()
    _L3_attn_in = {k: v for k, v in _L3_attn_all.items() if k in ('W_in', 'b_in', 'W_decay', 'b_decay', 'W_gate', 'b_gate', 'W_out', 'b_out', 'decay_bias')}
    del _L3_attn_all

    def _L3_xattn_setup():
        import jax, jax.numpy as jnp
        import numpy as np
        DIM = 256
        CTX_DIM = 128
        N_HEADS = 32
        HEAD_DIM = DIM // N_HEADS
        POS_DIM = 2
        B, N, CTXN = (2, 256, 256)
        ROPE_BASE = 10000.0

        def apply_axial_rope(x, pos):
            b, n, h, d = x.shape
            p = pos.shape[-1]
            dpa = d // p
            half = dpa // 2
            freqs = ROPE_BASE ** (-jnp.arange(half, dtype=x.dtype) / half)
            ang = pos[..., :, None] * freqs
            cos = jnp.cos(ang)[:, :, None, :, :]
            sin = jnp.sin(ang)[:, :, None, :, :]
            xr = x.reshape(b, n, h, p, half, 2)
            x1, x2 = (xr[..., 0], xr[..., 1])
            out = jnp.stack([x1 * cos - x2 * sin, x1 * sin + x2 * cos], axis=-1)
            return out.reshape(b, n, h, d)
        key = jax.random.key(seed)
        ks = jax.random.split(key, 8)
        x = jax.random.normal(ks[0], (B, N, DIM), jnp.float32)
        ctx = jax.random.normal(ks[1], (B, CTXN, CTX_DIM), jnp.float32)
        pos_map = jax.random.uniform(ks[2], (B, N, POS_DIM), jnp.float32)
        ctx_pos_map = jax.random.uniform(ks[3], (B, CTXN, POS_DIM), jnp.float32)
        Wq = jax.random.normal(ks[4], (DIM, DIM), jnp.float32) / np.sqrt(DIM)
        Wkv = jax.random.normal(ks[5], (CTX_DIM, 2 * DIM), jnp.float32) / np.sqrt(CTX_DIM)
        Wout = jax.random.normal(ks[6], (DIM, DIM), jnp.float32) / np.sqrt(DIM)
        bout = jnp.zeros((DIM,), jnp.float32)
        return {'x': x, 'ctx': ctx, 'pos_map': pos_map, 'ctx_pos_map': ctx_pos_map, 'Wq': Wq, 'Wkv': Wkv, 'Wout': Wout, 'bout': bout}
    _L3_xattn_all = _L3_xattn_setup()
    _L3_xattn_in = {k: v for k, v in _L3_xattn_all.items() if k in ('Wq', 'Wkv', 'Wout', 'bout')}
    del _L3_xattn_all

    def _L3_ffn_setup():
        import jax, jax.numpy as jnp
        import numpy as np
        K_SKIP = 4
        NORM_TOPK = True
        key = jax.random.key(seed)
        k1, k2, k3, k4 = jax.random.split(key, 4)
        B, S, H, I, E = (1, 128, 256, 96, 64)
        hidden_states = jax.random.normal(k1, (B, S, H), dtype=jnp.float32)
        gate_weight = jax.random.normal(k2, (E, H), dtype=jnp.float32) * 0.02
        gate_up_proj = jax.random.normal(k3, (E, 2 * I, H), dtype=jnp.float32) * 0.02
        down_proj = jax.random.normal(k4, (E, H, I), dtype=jnp.float32) * 0.02
        return {'hidden_states': hidden_states, 'gate_weight': gate_weight, 'gate_up_proj': gate_up_proj, 'down_proj': down_proj}
    _L3_ffn_all = _L3_ffn_setup()
    _L3_ffn_in = {k: v for k, v in _L3_ffn_all.items() if k in ('gate_weight', 'gate_up_proj', 'down_proj')}
    del _L3_ffn_all
    return {'x': x, 'ctx_1024': ctx_1024, 'fside_BxSx2_0': fside_BxSx2_0, 'L0_attn_W_qkv': _L0_attn_in['W_qkv'], 'L0_attn_W_out': _L0_attn_in['W_out'], 'L0_xattn_in_proj_w': _L0_xattn_in['in_proj_w'], 'L0_xattn_conv_w': _L0_xattn_in['conv_w'], 'L0_xattn_conv_b': _L0_xattn_in['conv_b'], 'L0_xattn_x_proj_w': _L0_xattn_in['x_proj_w'], 'L0_xattn_dt_proj_w': _L0_xattn_in['dt_proj_w'], 'L0_xattn_dt_proj_b': _L0_xattn_in['dt_proj_b'], 'L0_xattn_A_log': _L0_xattn_in['A_log'], 'L0_xattn_D': _L0_xattn_in['D'], 'L0_ffn_gate_w': _L0_ffn_in['gate_w'], 'L0_ffn_w_gate': _L0_ffn_in['w_gate'], 'L0_ffn_w_up': _L0_ffn_in['w_up'], 'L0_ffn_w_down': _L0_ffn_in['w_down'], 'L1_attn_wq': _L1_attn_in['wq'], 'L1_attn_wk': _L1_attn_in['wk'], 'L1_attn_wv': _L1_attn_in['wv'], 'L1_attn_wo': _L1_attn_in['wo'], 'L1_xattn_in_proj_w': _L1_xattn_in['in_proj_w'], 'L1_xattn_conv_w': _L1_xattn_in['conv_w'], 'L1_xattn_conv_b': _L1_xattn_in['conv_b'], 'L1_xattn_x_proj_w': _L1_xattn_in['x_proj_w'], 'L1_xattn_dt_proj_w': _L1_xattn_in['dt_proj_w'], 'L1_xattn_dt_proj_b': _L1_xattn_in['dt_proj_b'], 'L1_xattn_A_log': _L1_xattn_in['A_log'], 'L1_xattn_D': _L1_xattn_in['D'], 'L1_ffn_gate_w': _L1_ffn_in['gate_w'], 'L1_ffn_up_w': _L1_ffn_in['up_w'], 'L1_ffn_down_w': _L1_ffn_in['down_w'], 'L2_attn_Wq': _L2_attn_in['Wq'], 'L2_attn_bq': _L2_attn_in['bq'], 'L2_attn_Wk': _L2_attn_in['Wk'], 'L2_attn_bk': _L2_attn_in['bk'], 'L2_attn_Wv': _L2_attn_in['Wv'], 'L2_attn_bv': _L2_attn_in['bv'], 'L2_attn_Wo': _L2_attn_in['Wo'], 'L2_attn_bo': _L2_attn_in['bo'], 'L2_attn_rand_matrix': _L2_attn_in['rand_matrix'], 'L2_xattn_Wq': _L2_xattn_in['Wq'], 'L2_xattn_bq': _L2_xattn_in['bq'], 'L2_xattn_Wk': _L2_xattn_in['Wk'], 'L2_xattn_bk': _L2_xattn_in['bk'], 'L2_ffn_gate_w': _L2_ffn_in['gate_w'], 'L2_ffn_w_gate': _L2_ffn_in['w_gate'], 'L2_ffn_w_up': _L2_ffn_in['w_up'], 'L2_ffn_w_down': _L2_ffn_in['w_down'], 'L2_ffn_sw_gate': _L2_ffn_in['sw_gate'], 'L2_ffn_sw_up': _L2_ffn_in['sw_up'], 'L2_ffn_sw_down': _L2_ffn_in['sw_down'], 'L2_ffn_shared_gate_w': _L2_ffn_in['shared_gate_w'], 'L3_attn_W_in': _L3_attn_in['W_in'], 'L3_attn_b_in': _L3_attn_in['b_in'], 'L3_attn_W_decay': _L3_attn_in['W_decay'], 'L3_attn_b_decay': _L3_attn_in['b_decay'], 'L3_attn_W_gate': _L3_attn_in['W_gate'], 'L3_attn_b_gate': _L3_attn_in['b_gate'], 'L3_attn_W_out': _L3_attn_in['W_out'], 'L3_attn_b_out': _L3_attn_in['b_out'], 'L3_attn_decay_bias': _L3_attn_in['decay_bias'], 'L3_xattn_Wq': _L3_xattn_in['Wq'], 'L3_xattn_Wkv': _L3_xattn_in['Wkv'], 'L3_xattn_Wout': _L3_xattn_in['Wout'], 'L3_xattn_bout': _L3_xattn_in['bout'], 'L3_ffn_gate_weight': _L3_ffn_in['gate_weight'], 'L3_ffn_gate_up_proj': _L3_ffn_in['gate_up_proj'], 'L3_ffn_down_proj': _L3_ffn_in['down_proj']}

def reference(x, ctx_1024, fside_BxSx2_0, L0_attn_W_qkv, L0_attn_W_out, L0_xattn_in_proj_w, L0_xattn_conv_w, L0_xattn_conv_b, L0_xattn_x_proj_w, L0_xattn_dt_proj_w, L0_xattn_dt_proj_b, L0_xattn_A_log, L0_xattn_D, L0_ffn_gate_w, L0_ffn_w_gate, L0_ffn_w_up, L0_ffn_w_down, L1_attn_wq, L1_attn_wk, L1_attn_wv, L1_attn_wo, L1_xattn_in_proj_w, L1_xattn_conv_w, L1_xattn_conv_b, L1_xattn_x_proj_w, L1_xattn_dt_proj_w, L1_xattn_dt_proj_b, L1_xattn_A_log, L1_xattn_D, L1_ffn_gate_w, L1_ffn_up_w, L1_ffn_down_w, L2_attn_Wq, L2_attn_bq, L2_attn_Wk, L2_attn_bk, L2_attn_Wv, L2_attn_bv, L2_attn_Wo, L2_attn_bo, L2_attn_rand_matrix, L2_xattn_Wq, L2_xattn_bq, L2_xattn_Wk, L2_xattn_bk, L2_ffn_gate_w, L2_ffn_w_gate, L2_ffn_w_up, L2_ffn_w_down, L2_ffn_sw_gate, L2_ffn_sw_up, L2_ffn_sw_down, L2_ffn_shared_gate_w, L3_attn_W_in, L3_attn_b_in, L3_attn_W_decay, L3_attn_b_decay, L3_attn_W_gate, L3_attn_b_gate, L3_attn_W_out, L3_attn_b_out, L3_attn_decay_bias, L3_xattn_Wq, L3_xattn_Wkv, L3_xattn_Wout, L3_xattn_bout, L3_ffn_gate_weight, L3_ffn_gate_up_proj, L3_ffn_down_proj):
    import jax
    import jax.numpy as jnp

    def _L0_attn_ref(x, W_qkv, W_out):
        import jax, jax.numpy as jnp
        import numpy as np
        B, L, D, H = (4, 512, 256, 16)
        HD = D // H
        EPS = 1e-09

        def phi(x):
            return jax.nn.elu(x) + 1.0
        b, l, d = x.shape
        qkv = x @ W_qkv.T
        q, k, v = jnp.split(qkv, 3, axis=-1)
        q = q.reshape(b, l, H, HD).transpose(0, 2, 1, 3)
        k = k.reshape(b, l, H, HD).transpose(0, 2, 1, 3)
        v = v.reshape(b, l, H, HD).transpose(0, 2, 1, 3)
        q = phi(q)
        k = phi(k)
        kv_cumsum = jnp.cumsum(k * v, axis=2)
        k_cumsum = jnp.cumsum(k, axis=2)
        out = q * kv_cumsum / (q * k_cumsum + EPS)
        out = out.transpose(0, 2, 1, 3).reshape(b, l, d)
        return out @ W_out.T * HD ** (-0.5)

    def _L0_xattn_ref(hidden_states, z, in_proj_w, conv_w, conv_b, x_proj_w, dt_proj_w, dt_proj_b, A_log, D):
        import jax, jax.numpy as jnp
        import numpy as np
        import math
        B, L, DM = (2, 256, 128)
        DS, DC, EXP = (16, 4, 2)
        DI = EXP * DM
        DR = math.ceil(DM / 16)
        DT_MIN, DT_MAX, DT_FLOOR = (0.001, 0.1, 0.0001)

        def _ssm_forward(hidden_states, z, in_proj_w, conv_w, conv_b, x_proj_w, dt_proj_w, dt_proj_b, A_log, D):
            b = hidden_states.shape[0]
            x = jnp.einsum('ed,bld->bel', in_proj_w, hidden_states)
            xp = jnp.pad(x, ((0, 0), (0, 0), (DC - 1, 0)))
            xc = jax.lax.conv_general_dilated(xp, conv_w[:, None, :], window_strides=(1,), padding='VALID', dimension_numbers=('NCH', 'OIH', 'NCH'), feature_group_count=DI)
            u = jax.nn.silu(xc + conv_b[None, :, None])
            x_dbl = jnp.einsum('ke,bel->bkl', x_proj_w, u)
            dt_lo = x_dbl[:, :DR]
            Bm = x_dbl[:, DR:DR + DS]
            Cm = x_dbl[:, DR + DS:]
            delta = jax.nn.softplus(jnp.einsum('er,brl->bel', dt_proj_w, dt_lo) + dt_proj_b[None, :, None])
            A = -jnp.exp(A_log)

            def step(state, xs):
                d_t, B_t, C_t, u_t = xs
                dA = jnp.exp(d_t[..., None] * A)
                state = state * dA + (d_t * u_t)[..., None] * B_t[:, None, :]
                y_t = jnp.einsum('ben,bn->be', state, C_t)
                return (state, y_t)
            xs = (jnp.moveaxis(delta, -1, 0), jnp.moveaxis(Bm, -1, 0), jnp.moveaxis(Cm, -1, 0), jnp.moveaxis(u, -1, 0))
            state0 = jnp.zeros((b, DI, DS), delta.dtype)
            _, ys = jax.lax.scan(step, state0, xs)
            y = jnp.moveaxis(ys, 0, -1)
            y = y + D[None, :, None] * u
            y = y * jax.nn.silu(z)
            return jnp.swapaxes(y, 1, 2)
        return _ssm_forward(hidden_states, z, in_proj_w, conv_w, conv_b, x_proj_w, dt_proj_w, dt_proj_b, A_log, D)

    def _L0_ffn_ref(x, gate_w, w_gate, w_up, w_down):
        import jax, jax.numpy as jnp
        import numpy as np
        B, S, D = (2, 256, 256)
        MOE_D = 176
        E = 16
        K = 6
        ALPHA = 0.001

        def _moe_forward(x, gate_w, w_gate, w_up, w_down):
            b, s, d = x.shape
            T = b * s
            h = x.reshape(T, d)
            logits = h @ gate_w.T
            scores = jax.nn.softmax(logits.astype(jnp.float32), axis=-1)
            topk_w, topk_idx = jax.lax.top_k(scores, K)
            cw = jnp.zeros((T, E), jnp.float32)
            cw = cw.at[jnp.arange(T)[:, None], topk_idx].add(topk_w)
            y = jnp.zeros((T, d), x.dtype)
            for e in range(E):
                g = h @ w_gate[e].T
                u = h @ w_up[e].T
                out = jax.nn.silu(g) * u @ w_down[e].T
                y = y + cw[:, e:e + 1].astype(x.dtype) * out
            counts = jnp.sum(jax.nn.one_hot(topk_idx.reshape(b, s * K), E, dtype=jnp.float32), axis=1)
            ce = counts * (E / (s * K))
            scores_bse = scores.reshape(b, s, E)
            aux = jnp.mean(jnp.sum(ce * scores_bse.mean(axis=1), axis=1)) * ALPHA
            return (y.reshape(b, s, d), aux)
        y, _aux = _moe_forward(x, gate_w, w_gate, w_up, w_down)
        return y

    def _L1_attn_ref(x, wq, wk, wv, wo):
        import jax, jax.numpy as jnp
        import numpy as np
        D_MODEL = 256
        NUM_HEADS = 16
        D_K = D_MODEL // NUM_HEADS
        SEQ = 256
        BATCH = 2
        THETA = 10000.0

        def _rope_tables(seq_len, d_k, theta, dtype):
            pos = jnp.arange(seq_len, dtype=dtype)[:, None]
            inv = theta ** (-(jnp.arange(0, d_k, 2, dtype=dtype) / d_k))
            ang = pos * inv
            sin = jnp.repeat(jnp.sin(ang), 2, axis=1)
            cos = jnp.repeat(jnp.cos(ang), 2, axis=1)
            return (sin, cos)

        def _apply_rope(x, sin, cos):
            xp = x.reshape(x.shape[:-1] + (x.shape[-1] // 2, 2))
            swapped = jnp.stack((-xp[..., 1], xp[..., 0]), axis=-1).reshape(x.shape)
            return x * cos + swapped * sin
        B, S, D = x.shape
        H, dk = (NUM_HEADS, D_K)
        q = jnp.einsum('bsd,hkd->bhsk', x, wq.reshape(H, dk, D))
        k = jnp.einsum('bsd,hkd->bhsk', x, wk.reshape(H, dk, D))
        v = jnp.einsum('bsd,hkd->bhsk', x, wv.reshape(H, dk, D))
        sin, cos = _rope_tables(S, dk, THETA, x.dtype)
        q = _apply_rope(q, sin, cos)
        k = _apply_rope(k, sin, cos)
        scores = jnp.einsum('bhqk,bhsk->bhqs', q, k) / jnp.sqrt(jnp.asarray(dk, x.dtype))
        causal = jnp.triu(jnp.ones((S, S), dtype=bool), k=1)
        scores = jnp.where(causal, -jnp.inf, scores)
        attn = jax.nn.softmax(scores, axis=-1)
        out = jnp.einsum('bhqs,bhsv->bqhv', attn, v).reshape(B, S, H * dk)
        return jnp.einsum('bsf,df->bsd', out, wo)

    def _L1_xattn_ref(hidden_states, z, in_proj_w, conv_w, conv_b, x_proj_w, dt_proj_w, dt_proj_b, A_log, D):
        import jax, jax.numpy as jnp
        import numpy as np
        B_, L_, D_MODEL = (4, 256, 128)
        D_STATE, D_CONV, EXPAND = (16, 4, 2)
        D_INNER = EXPAND * D_MODEL
        DT_RANK = (D_MODEL + 15) // 16

        def silu(x):
            return x * jax.nn.sigmoid(x)
        Bsz, L, _ = hidden_states.shape
        d_inner, _, d_conv = conv_w.shape
        dt_rank = dt_proj_w.shape[1]
        d_state = A_log.shape[1]
        x = jnp.einsum('bld,ed->bel', hidden_states, in_proj_w)
        xc = jax.lax.conv_general_dilated(x, conv_w, window_strides=(1,), padding=[(d_conv - 1, 0)], feature_group_count=d_inner, dimension_numbers=('NCH', 'OIH', 'NCH'))
        x = silu(xc + conv_b[None, :, None])
        x_dbl = jnp.einsum('bdl,ed->bel', x, x_proj_w)
        dt_low, Bm, Cm = jnp.split(x_dbl, [dt_rank, dt_rank + d_state], axis=1)
        dt = jnp.einsum('brl,dr->bdl', dt_low, dt_proj_w)
        dt = jax.nn.softplus(dt + dt_proj_b[None, :, None])
        A = -jnp.exp(A_log)
        dt_t = jnp.moveaxis(dt, -1, 0)
        B_t = jnp.moveaxis(Bm, -1, 0)
        C_t = jnp.moveaxis(Cm, -1, 0)
        u_t = jnp.moveaxis(x, -1, 0)

        def step(state, inp):
            d, b, c, u = inp
            dA = jnp.exp(d[..., None] * A)
            state = state * dA + (d * u)[..., None] * b[:, None, :]
            y = jnp.einsum('bdn,bn->bd', state, c)
            return (state, y)
        state0 = jnp.zeros((Bsz, d_inner, d_state), x.dtype)
        _, ys = jax.lax.scan(step, state0, (dt_t, B_t, C_t, u_t))
        y = jnp.moveaxis(ys, 0, 2)
        y = y + D[None, :, None] * x
        y = y * silu(z)
        return jnp.swapaxes(y, 1, 2)

    def _L1_ffn_ref(x, gate_w, up_w, down_w):
        import jax, jax.numpy as jnp
        import numpy as np
        _FP8_MAX = 448.0
        _BLOCK = 32
        _EPS = 1e-30

        def _mx_dequant(t):
            rows, feat = t.shape
            blocks = t.reshape(rows, feat // _BLOCK, _BLOCK)
            max_abs = jnp.max(jnp.abs(blocks), axis=-1)
            scales = jnp.maximum(max_abs / _FP8_MAX, _EPS)
            q = (blocks / scales[..., None]).astype(jnp.float8_e4m3fn).astype(jnp.float32)
            return (q * scales[..., None]).reshape(rows, feat)

        def _mx_linear(x2d, w):
            return _mx_dequant(x2d) @ _mx_dequant(w).T
        B, S, H = x.shape
        x2d = x.reshape(B * S, H)
        gate = _mx_linear(x2d, gate_w)
        up = _mx_linear(x2d, up_w)
        h = jax.nn.silu(gate) * up
        out = _mx_linear(h, down_w)
        return out.reshape(B, S, H)

    def _L2_attn_ref(hidden_states, Wq, bq, Wk, bk, Wv, bv, Wo, bo, rand_matrix):
        import math
        import jax, jax.numpy as jnp
        import numpy as np
        HID = 256
        H = 16
        HKV = 8
        D = HID // H
        F = D
        SEQ = 256
        BATCH = 2
        THETA = 10000.0

        def _rotate_half(x):
            x1, x2 = (x[..., :x.shape[-1] // 2], x[..., x.shape[-1] // 2:])
            return jnp.concatenate((-x2, x1), axis=-1)

        def _softmax_kernel(x, R):
            n = jnp.sqrt(jnp.sum(x * x, axis=-1, keepdims=True))
            x = x / jnp.maximum(n, 1e-06)
            p = jnp.einsum('...d,ed->...e', x, R)
            feats = jnp.concatenate([jnp.sin(p), jnp.cos(p)], axis=-1)
            return feats / math.sqrt(F)
        b, s, _ = hidden_states.shape
        q = (hidden_states @ Wq.T + bq).reshape(b, s, H, D).transpose(0, 2, 1, 3)
        k = (hidden_states @ Wk.T + bk).reshape(b, s, HKV, D).transpose(0, 2, 1, 3)
        v = (hidden_states @ Wv.T + bv).reshape(b, s, HKV, D).transpose(0, 2, 1, 3)
        inv_freq = 1.0 / THETA ** (jnp.arange(0, D, 2, dtype=jnp.float32) / D)
        freqs = jnp.arange(s, dtype=jnp.float32)[:, None] * inv_freq[None, :]
        emb = jnp.concatenate((freqs, freqs), axis=-1)
        cos = jnp.cos(emb)[None, None, :, :]
        sin = jnp.sin(emb)[None, None, :, :]
        q = q * cos + _rotate_half(q) * sin
        k = k * cos + _rotate_half(k) * sin
        rep = H // HKV
        k = jnp.repeat(k, rep, axis=1)
        v = jnp.repeat(v, rep, axis=1)
        qp = _softmax_kernel(q, rand_matrix)
        kp = _softmax_kernel(k, rand_matrix)
        kv = jnp.einsum('bhsf,bhsd->bsfd', kp, v)
        out = jnp.einsum('bhsf,bsfd->bhsd', qp, kv)
        out = out.reshape(b, s, HID)
        return out @ Wo.T + bo

    def _L2_xattn_ref(teacher_logits, teacher_features, Wq, bq, Wk, bk):
        import jax, jax.numpy as jnp
        import numpy as np
        query = jnp.einsum('bnc,dc->bnd', teacher_features, Wq) + bq
        key = jnp.einsum('bnc,dc->bnd', teacher_features, Wk) + bk
        energy = jnp.einsum('bnd,bmd->bnm', query, key)
        attention = jax.nn.softmax(energy, axis=-1)
        x_m = jnp.einsum('bln,bmn->blm', teacher_logits, attention)
        return x_m

    def _L2_ffn_ref(hidden_states, gate_w, w_gate, w_up, w_down, sw_gate, sw_up, sw_down, shared_gate_w):
        import jax, jax.numpy as jnp
        import numpy as np
        B, S, H = (2, 128, 256)
        E, K = (8, 2)
        I = 176
        IS = 704
        WSCALE = 0.02
        x = hidden_states
        logits = jnp.einsum('bsh,eh->bse', x, gate_w)
        probs = jax.nn.softmax(logits, axis=-1)
        top_w, top_i = jax.lax.top_k(probs, K)
        top_w = top_w / jnp.sum(top_w, axis=-1, keepdims=True)
        onehot = jax.nn.one_hot(top_i, E, dtype=x.dtype)
        combine = jnp.einsum('bsk,bske->bse', top_w, onehot)
        g = jnp.einsum('bsh,ehi->besi', x, w_gate)
        u = jnp.einsum('bsh,ehi->besi', x, w_up)
        h = jax.nn.silu(g) * u
        expert_out = jnp.einsum('besi,eih->besh', h, w_down)
        moe_out = jnp.einsum('besh,bse->bsh', expert_out, combine)
        sh = jax.nn.silu(x @ sw_gate) * (x @ sw_up)
        shared_out = sh @ sw_down
        shared_gate = jax.nn.sigmoid(x @ shared_gate_w)
        return moe_out + shared_out * shared_gate

    def _L3_attn_ref(x, W_in, b_in, W_decay, b_decay, W_gate, b_gate, W_out, b_out, decay_bias):
        import jax, jax.numpy as jnp
        import numpy as np
        B, S, D = (4, 512, 256)
        DECAY_BIAS_INIT = -4.0
        W_SCALE = 0.02
        inp = jax.nn.silu(jnp.einsum('bsd,de->bse', x, W_in) + b_in).astype(jnp.float32)
        decay = jax.nn.sigmoid(jnp.einsum('bsd,de->bse', x, W_decay) + b_decay + decay_bias)
        gate = jax.nn.sigmoid(jnp.einsum('bsd,de->bse', x, W_gate) + b_gate)

        def step(state, di):
            d, i = di
            state = d * state + (1.0 - d) * i
            return (state, state)
        init = jnp.zeros((x.shape[0], x.shape[2]), jnp.float32)
        _, states = jax.lax.scan(step, init, (jnp.swapaxes(decay, 0, 1), jnp.swapaxes(inp, 0, 1)))
        y = gate * jnp.swapaxes(states, 0, 1)
        y = y.astype(x.dtype)
        return jnp.einsum('bsd,de->bse', y, W_out) + b_out

    def _L3_xattn_ref(x, ctx, pos_map, ctx_pos_map, Wq, Wkv, Wout, bout):
        import jax, jax.numpy as jnp
        import numpy as np
        DIM = 256
        CTX_DIM = 128
        N_HEADS = 32
        HEAD_DIM = DIM // N_HEADS
        POS_DIM = 2
        B, N, CTXN = (2, 256, 256)
        ROPE_BASE = 10000.0

        def apply_axial_rope(x, pos):
            b, n, h, d = x.shape
            p = pos.shape[-1]
            dpa = d // p
            half = dpa // 2
            freqs = ROPE_BASE ** (-jnp.arange(half, dtype=x.dtype) / half)
            ang = pos[..., :, None] * freqs
            cos = jnp.cos(ang)[:, :, None, :, :]
            sin = jnp.sin(ang)[:, :, None, :, :]
            xr = x.reshape(b, n, h, p, half, 2)
            x1, x2 = (xr[..., 0], xr[..., 1])
            out = jnp.stack([x1 * cos - x2 * sin, x1 * sin + x2 * cos], axis=-1)
            return out.reshape(b, n, h, d)
        b, n, _ = x.shape
        ctx_n = ctx.shape[1]
        q = (x @ Wq).reshape(b, n, N_HEADS, HEAD_DIM)
        k, v = jnp.split(ctx @ Wkv, 2, axis=-1)
        k = k.reshape(b, ctx_n, N_HEADS, HEAD_DIM)
        v = v.reshape(b, ctx_n, N_HEADS, HEAD_DIM)
        q = apply_axial_rope(q, pos_map)
        k = apply_axial_rope(k, ctx_pos_map)
        scale = 1.0 / np.sqrt(HEAD_DIM).astype(np.float32)
        logits = jnp.einsum('bqhd,bkhd->bhqk', q, k) * scale
        w = jax.nn.softmax(logits, axis=-1)
        attn = jnp.einsum('bhqk,bkhd->bqhd', w, v)
        attn = attn.reshape(b, n, N_HEADS * HEAD_DIM)
        return attn @ Wout + bout

    def _L3_ffn_ref(hidden_states, gate_weight, gate_up_proj, down_proj):
        import jax, jax.numpy as jnp
        import numpy as np
        K_SKIP = 4
        NORM_TOPK = True
        B, S, H = hidden_states.shape
        E = gate_weight.shape[0]
        x = hidden_states.reshape(-1, H)
        T = x.shape[0]
        router_logits = x @ gate_weight.T
        router_probs = jax.nn.softmax(router_logits.astype(jnp.float32), axis=-1)
        router_probs = router_probs.astype(router_logits.dtype)
        top_v, top_i = jax.lax.top_k(router_probs, K_SKIP)
        if NORM_TOPK:
            top_v = top_v / jnp.clip(top_v.sum(axis=-1, keepdims=True), 1e-12)
        combine = jnp.zeros((T, E), dtype=top_v.dtype).at[jnp.arange(T)[:, None], top_i].add(top_v)

        def body(acc, expert):
            w1, w2, we = expert
            gate, up = jnp.split(x @ w1.T, 2, axis=-1)
            h = jax.nn.silu(gate) * up @ w2.T
            return (acc + h * we[:, None], None)
        out, _ = jax.lax.scan(body, jnp.zeros_like(x), (gate_up_proj, down_proj, combine.T))
        return out.reshape(B, S, H)
    x = x + _L0_attn_ref(_layernorm(x, axis=-1), L0_attn_W_qkv, L0_attn_W_out)
    x = x + _L0_xattn_ref(ctx_1024, _layernorm(x, axis=-1), L0_xattn_in_proj_w, L0_xattn_conv_w, L0_xattn_conv_b, L0_xattn_x_proj_w, L0_xattn_dt_proj_w, L0_xattn_dt_proj_b, L0_xattn_A_log, L0_xattn_D)
    x = x + _L0_ffn_ref(_layernorm(x, axis=-1), L0_ffn_gate_w, L0_ffn_w_gate, L0_ffn_w_up, L0_ffn_w_down)
    x = x + _L1_attn_ref(_layernorm(x, axis=-1), L1_attn_wq, L1_attn_wk, L1_attn_wv, L1_attn_wo)
    x = x + _L1_xattn_ref(ctx_1024, _layernorm(x, axis=-1), L1_xattn_in_proj_w, L1_xattn_conv_w, L1_xattn_conv_b, L1_xattn_x_proj_w, L1_xattn_dt_proj_w, L1_xattn_dt_proj_b, L1_xattn_A_log, L1_xattn_D)
    x = x + _L1_ffn_ref(_layernorm(x, axis=-1), L1_ffn_gate_w, L1_ffn_up_w, L1_ffn_down_w)
    x = x + _L2_attn_ref(_layernorm(x, axis=-1), L2_attn_Wq, L2_attn_bq, L2_attn_Wk, L2_attn_bk, L2_attn_Wv, L2_attn_bv, L2_attn_Wo, L2_attn_bo, L2_attn_rand_matrix)
    x = x + _L2_xattn_ref(_layernorm(x, axis=-1), ctx_1024, L2_xattn_Wq, L2_xattn_bq, L2_xattn_Wk, L2_xattn_bk)
    x = x + _L2_ffn_ref(_layernorm(x, axis=-1), L2_ffn_gate_w, L2_ffn_w_gate, L2_ffn_w_up, L2_ffn_w_down, L2_ffn_sw_gate, L2_ffn_sw_up, L2_ffn_sw_down, L2_ffn_shared_gate_w)
    x = x + _L3_attn_ref(_layernorm(x, axis=-1), L3_attn_W_in, L3_attn_b_in, L3_attn_W_decay, L3_attn_b_decay, L3_attn_W_gate, L3_attn_b_gate, L3_attn_W_out, L3_attn_b_out, L3_attn_decay_bias)
    x = x + _L3_xattn_ref(_layernorm(x, axis=-1), ctx_1024, fside_BxSx2_0, fside_BxSx2_0, L3_xattn_Wq, L3_xattn_Wkv, L3_xattn_Wout, L3_xattn_bout)
    x = x + _L3_ffn_ref(_layernorm(x, axis=-1), L3_ffn_gate_weight, L3_ffn_gate_up_proj, L3_ffn_down_proj)
    return x

_drawn_inputs = setup_inputs


def setup_inputs(seed=0):
    import zlib

    import numpy as np

    out = dict(_drawn_inputs(seed))
    spreads = {'L0_xattn_conv_b': (0.0, 0.1),
     'L0_xattn_D': (1.0, 0.2),
     'L1_xattn_D': (1.0, 0.6),
     'L2_xattn_bq': (0.0, 0.1),
     'L2_xattn_bk': (0.0, 2.0),
     'L3_attn_b_in': (0.0, 0.8),
     'L3_attn_b_decay': (0.0, 2.0),
     'L3_attn_b_gate': (0.0, 2.0),
     'L3_attn_b_out': (0.0, 0.366),
     'L3_attn_decay_bias': (-4.0, 0.6),
     'L3_xattn_bout': (0.0, 0.427)}
    factors = {'L0_xattn_dt_proj_w': 5.437,
     'L1_xattn_in_proj_w': 5.069,
     'L1_xattn_conv_w': 5.27,
     'L1_xattn_conv_b': 8.0,
     'L1_xattn_x_proj_w': 8.0,
     'L1_xattn_dt_proj_w': 8.0,
     'L1_xattn_dt_proj_b': 8.0,
     'L1_xattn_A_log': 8.0,
     'L2_attn_bq': 8.0,
     'L2_attn_bk': 8.0,
     'L2_attn_bv': 8.0,
     'L2_attn_bo': 3.557,
     'L2_ffn_gate_w': 8.0,
     'L2_ffn_w_gate': 8.0,
     'L2_ffn_w_up': 8.0,
     'L2_ffn_w_down': 8.0,
     'L2_ffn_sw_gate': 5.844,
     'L2_ffn_sw_up': 5.788,
     'L2_ffn_sw_down': 5.784,
     'L2_ffn_shared_gate_w': 8.0,
     'L3_attn_W_in': 3.3,
     'L3_attn_W_decay': 21.912,
     'L3_attn_W_gate': 8.0,
     'L3_attn_W_out': 3.11,
     'L3_ffn_gate_weight': 8.0,
     'L3_ffn_gate_up_proj': 8.0,
     'L3_ffn_down_proj': 8.0,
     'fside_BxSx2_0': 4.379}
    for name, (base, spread) in spreads.items():
        noise = np.random.default_rng([zlib.crc32(name.encode()), seed]).standard_normal(out[name].shape)
        drawn = base * np.exp(spread * noise) if base else spread * noise
        out[name] = jnp.asarray(drawn.astype(out[name].dtype))
    for name, factor in factors.items():
        out[name] = (out[name] * factor).astype(out[name].dtype)
    return out
```

```python
from contextlib import ExitStack

import numpy as np

import concourse.bass as bass
from concourse import mybir

F32 = mybir.dt.float32
I32 = mybir.dt.int32
ALU = mybir.AluOpType
ACT = mybir.ActivationFunctionType
AX_X = mybir.AxisListType.X

P = 128
B, S, D = 4, 256, 256
CTX = 128
T = B * S
TILES = T // P
KD = D // P
HALF = T // 2
PAIR = 1024
NORMS = 12
EPS = 1e-5
TWO_PI = 2.0 * np.pi
SIN_SCALE = float(np.float32(TWO_PI * (1 - 2e-7)))
ROUND = 1.5 * 2.0 ** 23
N_STATE, D_CONV, DT_RANK = 16, 4, 8
X_DBL = DT_RANK + 2 * N_STATE
MX_BLOCK, FP8_MAX = 32, 448.0


STAGE_SEMS = 64


class Order:

    def __init__(self, sem):
        self.sem, self.made, self.turn = sem, 0, None

    def mark(self, ins):
        self.made += 1
        ins.then_inc(self.sem, 1)

    def wait(self, eng):
        eng.wait_ge(self.sem, self.made if self.turn is None else self.turn + self.made)

    def link(self, eng, ins):
        self.mark(ins)
        self.wait(eng)


class Machine:

    def __init__(self, nc, ctx, dram):
        self.nc, self.ctx, self.dram = nc, ctx, dram
        self.stage_sems = None
        self.resid = self.sb("resid", [P, TILES, D])
        self.h = self.sb("h", [P, TILES, D])
        self.hT = self.sb("hT", [P, KD, T])
        self.stats = self.sb("stats", [P, TILES, 6])
        self.moments = self.sb("moments", [P, TILES, 2])
        self.rstd = self.sb("rstd", [P, 2, TILES])
        self.minus_half = self.sb("minus_half", [P, TILES])
        self.psum = ctx.enter_context(nc.psum_tensor("psum", [P, 4 * PAIR], F32))
        self.w = {}
        self.w_loaded = {}
        self.moments_ready = self.sem("moments_ready")
        self.rstd_ready = self.sem("rstd_ready")
        self.h_ready = self.sem("h_ready")
        self.turned = self.sem("turned")
        self.hT_ready = self.sem("hT_ready")
        self.dve_order = Order(self.sem("dve_order"))
        self.act_order = Order(self.sem("act_order"))
        self.pool_order = Order(self.sem("pool_order"))
        self.norm = -1

    def sb(self, name, shape, dt=F32):
        return self.ctx.enter_context(self.nc.sbuf_tensor(name, shape, dt))

    def sem(self, name):
        if self.stage_sems is None:
            return self.ctx.enter_context(self.nc.semaphore(name))
        self.stage_sems += 1
        assert self.stage_sems <= STAGE_SEMS
        return self.ctx.enter_context(self.nc.semaphore(name, num=self.first_stage_sem + self.stage_sems - 1))

    def pair(self, i, rows=P):
        return self.psum[0:rows, i * PAIR:(i + 1) * PAIR]

    def weight(self, group, name, shape):
        self.w[name] = self.sb("w_" + name, shape)
        if group not in self.w_loaded:
            self.w_loaded[group] = [self.sem("loaded_" + group), 0, []]
        self.w_loaded[group][1] += 16
        self.w_loaded[group][2].append(name)

    def wait_weights(self, eng, group):
        eng.wait_ge(self.w_loaded[group][0], self.w_loaded[group][1])



def norm_vector(m, dve, n):
    nc, o = m.nc, m.dve_order
    for t in range(TILES):
        o.mark(nc.vector.bn_stats(m.stats[:, t, :], m.resid[:, t, :]))
    for t in range(TILES):
        dve.wait_ge(o.sem, o.made - TILES + 1 + t)
        ins = nc.vector.bn_aggr(m.moments[:, t, :], m.stats[:, t, :])
    ins.then_inc(m.moments_ready, 1)
    dve.wait_ge(m.rstd_ready, n + 1)
    for t in range(TILES):
        nc.vector.tensor_scalar(m.h[:, t, :], m.resid[:, t, :], m.moments[:, t, 0:1], m.rstd[:, 1, t:t + 1],
                                ALU.subtract, ALU.mult).then_inc(m.h_ready, 1)


def norm_gpsimd(m, pool, n):
    nc = m.nc
    pool.wait_ge(m.moments_ready, n + 1)
    m.pool_order.link(pool, nc.gpsimd.tensor_scalar(m.rstd[:, 0, :], m.moments[:, :, 1], EPS, None, ALU.add))
    nc.gpsimd.tensor_tensor(m.rstd[:, 1, :], m.rstd[:, 0, :], m.minus_half[:], ALU.pow).then_inc(m.rstd_ready, 1)


def norm_tensor(m, pe, n):
    nc = m.nc
    for t in range(TILES):
        pe.wait_ge(m.h_ready, TILES * n + t + 1)
        for k in range(KD):
            at = k * PAIR + t * P
            ins = nc.tensor.transpose(m.psum[:, at:at + P], m.h[:, t, k * P:(k + 1) * P], m.ident[:])
        if t % 4 == 3:
            ins.then_inc(m.turned, 1)


def norm_scalar(m, act, j):
    nc = m.nc
    for half in range(2):
        act.wait_ge(m.turned, 2 * j + half + 1)
        for k in range(KD):
            cols = slice(half * HALF, (half + 1) * HALF)
            nc.scalar.activation(m.hT[:, k, cols], m.pair(k)[:, cols], ACT.Copy).then_inc(m.hT_ready, 1)


def wait_hT(m, eng, j, half=1):
    eng.wait_ge(m.hT_ready, 4 * j + 2 * (half + 1))


class Jobs:

    def __init__(self, m, label, first, jobs):
        self.m, self.first = m, first
        self.names = [n for n, _ in jobs]
        self.takers = [k for _, k in jobs]
        self.filled = m.sem(label + "_filled")
        self.emptied = {k: m.sem(label + "_emptied_" + k) for k in sorted(set(self.takers))}

    def at(self, name):
        return self.names.index(name)

    def pair(self, name, rows=P):
        return self.m.pair((self.first + self.at(name)) % 4, rows)

    def wait_room(self, eng, name):
        i = self.at(name) - 4
        if i >= 0:
            k = self.takers[i]
            eng.wait_ge(self.emptied[k], self.takers[:i + 1].count(k))

    def wait_filled(self, eng, name):
        eng.wait_ge(self.filled, self.at(name) + 1)

    def empty(self, name):
        return self.emptied[self.takers[self.at(name)]]


def project(m, pe, jobs, name, w, rhs, chunks, rows=P):
    nc = m.nc
    jobs.wait_room(pe, name)
    out = jobs.pair(name, rows)
    for half in range(2):
        cols = slice(half * HALF, (half + 1) * HALF)
        for k in range(chunks):
            ins = nc.tensor.matmul(out[:, cols], lhsT=w(k), rhs=rhs(k, cols), start=(k == 0), stop=(k == chunks - 1))
    ins.then_inc(jobs.filled, 1)


def project_tokens(m, pe, jobs, names, lhs, rhs, chunks):
    nc = m.nc
    for q, name in enumerate(names):
        jobs.wait_room(pe, name)
        out = jobs.pair(name)
        for j in range(4):
            t = 4 * q + j
            for k in range(chunks):
                ins = nc.tensor.matmul(out[:, j * D:(j + 1) * D], lhsT=lhs(k, t), rhs=rhs(k, t),
                                       start=(k == 0), stop=(k == chunks - 1))
        ins.then_inc(jobs.filled, 1)


def add_tokens(m, dve, jobs, names, scale=1.0, bias=None):
    nc = m.nc
    for q, name in enumerate(names):
        jobs.wait_filled(dve, name)
        r = m.resid[:, 4 * q:4 * q + 4, :]
        ps = jobs.pair(name).rearrange("p (t d) -> p t d", d=D)
        if bias is not None:
            m.dve_order.link(dve, nc.vector.tensor_tensor(r, r, bias.unsqueeze(1).to_broadcast([P, 4, D]), ALU.add))
        nc.vector.scalar_tensor_tensor(out=r, in0=ps, scalar=scale, in1=r, op0=ALU.mult,
                                       op1=ALU.add).then_inc(jobs.empty(name), 1)


def wcols(w, c):
    return lambda k: w[:, k, c * P:(c + 1) * P]


def feature_rhs(x):
    return lambda k, cols: x[:, k, cols]



def linear_attention(m, n, j):
    nc = m.nc
    w = m.w["l0_qkv"]
    jobs = Jobs(m, "l0a", 2, [(x + str(c), "vector" if x == "v" else "scalar") for c in range(KD) for x in "qkv"]
                + [("out0", "vector"), ("out1", "vector")])
    e = [m.sb(f"l0_exp{i}", [P, T]) for i in range(2)]
    r = [m.sb(f"l0_relu{i}", [P, T]) for i in range(2)]
    sums = [m.sb(f"l0_sum{i}", [P, T]) for i in range(2)]
    att = m.sb("l0_att", [P, KD, T])
    phi_in = m.sem("l0_phi_in")
    chunk_done = m.sem("l0_chunk_done")
    with nc.Block(name="l0_attn") as block:
        @block.gpsimd
        def _(pool):
            norm_gpsimd(m, pool, n)

        @block.tensor
        def _(pe):
            m.wait_weights(pe, "consts")
            norm_tensor(m, pe, n)
            wait_hT(m, pe, j)
            m.wait_weights(pe, "l0_attn")
            for c in range(KD):
                for i, x in enumerate("qkv"):
                    project(m, pe, jobs, x + str(c), wcols(w, KD * i + c), feature_rhs(m.hT), KD)
            pe.wait_ge(chunk_done, KD)
            project_tokens(m, pe, jobs, ("out0", "out1"), lambda k, t: att[:, k, t * P:(t + 1) * P],
                           lambda k, t: m.w["l0_out"][:, k, :], KD)

        @block.scalar
        def _(act):
            norm_scalar(m, act, j)
            for c in range(KD):
                for i, x in enumerate("qk"):
                    name = x + str(c)
                    jobs.wait_filled(act, name)
                    if c:
                        act.wait_ge(chunk_done, c)
                    nc.scalar.activation(e[i][:], jobs.pair(name), ACT.Exp).then_inc(phi_in, 1)
                    nc.scalar.activation(r[i][:], jobs.pair(name), ACT.Relu).then_inc(jobs.empty(name), 1)

        @block.vector
        def _(dve):
            o = m.dve_order
            m.wait_weights(dve, "consts")
            norm_vector(m, dve, n)
            for c in range(KD):
                dve.wait_ge(jobs.emptied["scalar"], 2 * c + 2)
                for i in range(2):
                    o.mark(nc.vector.scalar_tensor_tensor(out=e[i][:], in0=e[i][:], scalar=1.0, in1=r[i][:],
                                                          op0=ALU.min, op1=ALU.add))
                o.wait(dve)
                name = "v" + str(c)
                jobs.wait_filled(dve, name)
                ins = nc.vector.tensor_tensor(r[1][:], e[1][:], jobs.pair(name), ALU.mult)
                ins.then_inc(jobs.empty(name), 1)
                dve.wait_ge(jobs.empty(name), c + 1)
                o.mark(nc.vector.tensor_tensor_scan(sums[0][:], m.w["carry"][:], r[1][:], 0.0, ALU.mult, ALU.add))
                o.mark(nc.vector.tensor_tensor_scan(sums[1][:], m.w["carry"][:], e[1][:], 0.0, ALU.mult, ALU.add))
                o.wait(dve)
                for i in range(2):
                    o.mark(nc.vector.tensor_tensor(sums[i][:], e[0][:], sums[i][:], ALU.mult))
                o.wait(dve)
                o.link(dve, nc.vector.tensor_scalar(sums[1][:], sums[1][:], 1e-9, None, ALU.add))
                o.link(dve, nc.vector.reciprocal(sums[1][:], sums[1][:]))
                nc.vector.tensor_tensor(att[:, c, :], sums[0][:], sums[1][:], ALU.mult).then_inc(chunk_done, 1)
            add_tokens(m, dve, jobs, ("out0", "out1"), scale=16 ** -0.5)



def state_space(m, layer, n):
    nc = m.nc
    g = f"l{layer}s_"
    w = {k: m.w[g + k] for k in ("in", "conv", "conv_b", "x", "dt", "dt_b", "a", "d")}
    xpad = m.sb(g + "xpad", [P, KD, B, D_CONV - 1 + S])
    conv = m.sb(g + "conv_out", [P, KD, T])
    u = m.sb(g + "u", [P, KD, T])
    xdbl = m.sb(g + "xdbl", [X_DBL, T])
    t_abs = m.sb(g + "t_abs", [P, KD, T])
    t_sq = m.sb(g + "t_sq", [P, KD, T])
    relu = m.sb(g + "relu", [P, KD, T])
    du = m.sb(g + "du", [P, KD, T])
    skip = m.hT
    gate = m.sb(g + "gate", [P, TILES, S])
    decay = [t_sq[:, i, :] for i in range(2)]
    drive = [xpad[:, i, :, :].rearrange("p b s -> p (b s)")[:, 0:T] for i in range(2)]
    state = [relu[:, i, :] for i in range(2)]
    read = [conv[:, i, :] for i in range(2)]
    SLOTS = 4
    bc = [m.sb(g + f"bc{i}", [P, 2, T]) for i in range(SLOTS)]
    scratch = nc.dram_tensor(g + "scratch", (X_DBL, T), F32).ap()
    delta = t_abs
    (x_filled, pads, x_out, conv_done, u_ready, xdbl_filled, xdbl_ready, stored, dt_filled, act_dt, delta0_ready, delta1_ready,
     du_ready, gate_ready, decay_ready, drive_ready, scanned, read_ready, summed, product, turned,
     skip_ready, ratio_ready) = (m.sem(g + s) for s in (
         "x_filled", "pads", "x_out", "conv_done", "u_ready", "xdbl_filled", "xdbl_ready", "stored", "dt_filled",
         "act_dt", "delta0_ready", "delta1_ready", "du_ready", "gate_ready", "decay_ready", "drive_ready", "scanned", "read_ready",
         "summed", "product", "turned", "skip_ready", "ratio_ready"))
    bc_in = [m.sem(g + f"bc_in{i}") for i in range(SLOTS)]
    GROUPS = N_STATE // SLOTS

    with nc.Block(name=g + "block") as block:
        @block.sync
        def _(sp):
            sp.wait_ge(xdbl_ready, 1)
            sp.dma_start(scratch, xdbl[:]).then_inc(stored, 16)
            sp.wait_ge(stored, 16)
            rows = scratch[DT_RANK:X_DBL, :].rearrange("(a n) t -> n a t", n=N_STATE)
            for s in range(SLOTS):
                sp.dma_start(bc[s][:], rows[s].partition_broadcast(P)).then_inc(bc_in[s], 16)
            with sp.Fori(1, GROUPS) as i:
                for s in range(SLOTS):
                    sp.wait_ge(read_ready, (i * SLOTS + s - SLOTS + 1) * KD)
                    src = rows[bass.ds(i * SLOTS + s, 1)].rearrange("o a t -> (o a) t")
                    sp.dma_start(bc[s][:], src.partition_broadcast(P)).then_inc(bc_in[s], 16)

        @block.gpsimd
        def _(pool):
            o = m.pool_order
            nc.gpsimd.memset(xpad[:], 0.0).then_inc(pads, 1)
            norm_gpsimd(m, pool, n)
            pool.wait_ge(ratio_ready, 2)
            softplus_tail(pool, nc.gpsimd, o, t_abs[:, 1, :], t_sq[:, 1, :], conv[:, 1, :], relu[:, 1, :],
                          delta[:, 1, :], delta1_ready, fused=False)
            pool.wait_ge(u_ready, KD)
            pool.wait_ge(delta0_ready, 1)
            pool.wait_ge(delta1_ready, 1)
            for c in range(KD):
                o.mark(nc.gpsimd.tensor_tensor(du[:, c, :], delta[:, c, :], u[:, c, :], ALU.mult))
            o.wait(pool)
            for c in range(KD):
                first = delta[:, c, :].rearrange("p (b s) -> p b s", s=S)[:, :, 0:1]
                ins = nc.gpsimd.memset(first, 1e25)
            ins.then_inc(du_ready, 1)

            def group(i, q0):
                for s in range(SLOTS):
                    pool.wait_ge(bc_in[s], (i + 1) * 16)
                    for c in range(KD):
                        pool.wait_ge(scanned, q0 + s * KD + c + 1)
                        nc.gpsimd.tensor_tensor(drive[c], du[:, c, :], bc[s][:, 0, :],
                                                ALU.mult).then_inc(drive_ready, 1)
            with pool.Fori(0, GROUPS) as i:
                group(i, i * (SLOTS * KD))

        @block.tensor
        def _(pe):
            m.wait_weights(pe, g)
            for c in range(KD):
                for half in range(2):
                    cols = slice(half * HALF, (half + 1) * HALF)
                    ins = nc.tensor.matmul(m.pair(c)[:, cols], lhsT=w["in"][:, c * P:(c + 1) * P], rhs=m.ctxT[:, cols],
                                           start=True, stop=True)
                ins.then_inc(x_filled, 1)
            pe.wait_ge(u_ready, KD)
            for half in range(2):
                cols = slice(half * HALF, (half + 1) * HALF)
                for k in range(KD):
                    ins = nc.tensor.matmul(m.pair(2, X_DBL)[:, cols], lhsT=w["x"][:, k, :], rhs=u[:, k, cols],
                                           start=(k == 0), stop=(k == KD - 1))
            ins.then_inc(xdbl_filled, 1)
            pe.wait_ge(xdbl_ready, 1)
            for c in range(KD):
                for half in range(2):
                    cols = slice(half * HALF, (half + 1) * HALF)
                    ins = nc.tensor.matmul(m.pair(c)[:, cols], lhsT=w["dt"][:, c * P:(c + 1) * P],
                                           rhs=xdbl[0:DT_RANK, cols], start=True, stop=True)
                ins.then_inc(dt_filled, 1)
            pe.wait_ge(skip_ready, KD)

            def add(c, rhs, start, stop):
                for half in range(2):
                    cols = slice(half * HALF, (half + 1) * HALF)
                    ins = nc.tensor.matmul(m.pair(2 + c)[:, cols], lhsT=m.ident[:], rhs=rhs[:, cols], start=start,
                                           stop=stop, skip_group_check=True)
                return ins

            for c in range(KD):
                add(c, skip[:, c, :], True, False)

            def group(q0, last):
                for s in range(SLOTS):
                    for c in range(KD):
                        pe.wait_ge(read_ready, q0 + s * KD + c + 1)
                        add(c, read[c], False, last and s == SLOTS - 1).then_inc(summed, 1)
            with pe.Fori(0, GROUPS - 1) as i:
                group(i * (SLOTS * KD), False)
            group((GROUPS - 1) * SLOTS * KD, True)
            pe.wait_ge(product, KD)
            for q in range(2):
                for b in range(2 * q, 2 * q + 2):
                    for lh in range(2):
                        for c in range(KD):
                            at = q * PAIR + (2 * (b % 2) + lh) * D + c * P
                            src = conv[:, c, b * S + lh * P:b * S + (lh + 1) * P]
                            ins = nc.tensor.transpose(m.psum[:, at:at + P], src, m.ident[:])
                ins.then_inc(turned, 1)

        @block.scalar
        def _(act):
            act.wait_ge(pads, 1)
            for c in range(KD):
                act.wait_ge(x_filled, c + 1)
                nc.scalar.activation(xpad[:, c, :, D_CONV - 1:], m.pair(c).rearrange("p (b s) -> p b s", s=S),
                                     ACT.Copy).then_inc(x_out, 1)
            for c in range(KD):
                act.wait_ge(conv_done, c + 1)
                nc.scalar.activation(u[:, c, :], conv[:, c, :], ACT.Silu, bias=w["conv_b"][:, c:c + 1]).then_inc(u_ready, 1)
            act.wait_ge(m.h_ready, TILES * (n + 1))
            nc.scalar.activation(gate[:], m.h[:], ACT.Silu).then_inc(gate_ready, 1)
            act.wait_ge(u_ready, KD)
            for c in range(KD):
                nc.scalar.activation(skip[:, c, :], u[:, c, :], ACT.Copy, scale=w["d"][:, c:c + 1]).then_inc(skip_ready, 1)
            act.wait_ge(xdbl_filled, 1)
            nc.scalar.activation(xdbl[:], m.pair(2, X_DBL), ACT.Copy).then_inc(xdbl_ready, 1)
            for c in range(KD):
                act.wait_ge(dt_filled, c + 1)
                m.act_order.link(act, nc.scalar.activation(t_abs[:, c, :], m.pair(c), ACT.Abs, bias=w["dt_b"][:, c:c + 1]))
                nc.scalar.activation(relu[:, c, :], m.pair(c), ACT.Relu, bias=w["dt_b"][:, c:c + 1])
                nc.scalar.activation(t_abs[:, c, :], t_abs[:, c, :], ACT.Exp, scale=-1.0).then_inc(act_dt, 1)
            m.act_order.link(act, nc.scalar.activation(w["a"][:], w["a"][:], ACT.Exp))
            m.act_order.link(act, nc.scalar.mul(w["a"][:], w["a"][:], -1.0))
            act.wait_ge(du_ready, 1)
            with act.Fori(0, GROUPS) as i:
                for s in range(SLOTS):
                    for c in range(KD):
                        act.wait_ge(scanned, i * (SLOTS * KD) + s * KD + c + 1)
                        at = i * SLOTS + s
                        nc.scalar.activation(decay[c], delta[:, c, :], ACT.Exp,
                                             scale=w["a"][:, c, bass.ds(at, 1)]).then_inc(decay_ready, 1)

        @block.vector
        def _(dve):
            o = m.dve_order
            dve.sem_inc(scanned, KD)
            norm_vector(m, dve, n)
            m.wait_weights(dve, g)
            for c in range(KD):
                dve.wait_ge(x_out, c + 1)
                out = conv[:, c, :].rearrange("p (b s) -> p b s", s=S)
                o.link(dve, nc.vector.tensor_scalar(out, xpad[:, c, :, 0:S], w["conv"][:, c, 0:1], None, ALU.mult))
                for k in range(1, D_CONV):
                    ins = nc.vector.scalar_tensor_tensor(out=out, in0=xpad[:, c, :, k:k + S], scalar=w["conv"][:, c, k:k + 1],
                                                         in1=out, op0=ALU.mult, op1=ALU.add)
                    if k < D_CONV - 1:
                        o.link(dve, ins)
                ins.then_inc(conv_done, 1)
            for c in range(KD):
                dve.wait_ge(act_dt, c + 1)
                softplus_ratio(m, dve, c, t_abs[:, c, :], t_sq[:, c, :], ratio_ready)
            softplus_tail(dve, nc.vector, o, t_abs[:, 0, :], t_sq[:, 0, :], conv[:, 0, :], relu[:, 0, :],
                          delta[:, 0, :], delta0_ready, fused=True)

            def unit(q, c, s, i):
                dve.wait_ge(decay_ready, q + 1)
                dve.wait_ge(drive_ready, q + 1)
                nc.vector.tensor_tensor_scan(state[c], decay[c], drive[c], 0.0, ALU.mult,
                                             ALU.add).then_inc(scanned, 1)
                dve.wait_ge(scanned, q + 1 + KD)
                dve.wait_ge(summed, q + 1)
                nc.vector.tensor_tensor(read[c], state[c], bc[s][:, 1, :], ALU.mult).then_inc(read_ready, 1)

            dve.sem_inc(summed, KD)
            with dve.Fori(0, GROUPS) as i:
                for s in range(SLOTS):
                    for c in range(KD):
                        unit(i * (SLOTS * KD) + s * KD + c, c, s, i)
            dve.wait_ge(summed, KD + N_STATE * KD)
            dve.wait_ge(gate_ready, 1)
            for c in range(KD):
                y = m.pair(2 + c).rearrange("p (b s) -> p b s", s=S)
                z = gate[:].rearrange("p (b c) s -> p b c s", c=KD)[:, :, c, :]
                nc.vector.tensor_tensor(conv[:, c, :].rearrange("p (b s) -> p b s", s=S), y, z,
                                        ALU.mult).then_inc(product, 1)
            for q in range(2):
                dve.wait_ge(turned, q + 1)
                r = m.resid[:, 4 * q:4 * q + 4, :]
                o.link(dve, nc.vector.tensor_tensor(r, m.pair(q).rearrange("p (t d) -> p t d", d=D), r, ALU.add))


def softplus_ratio(m, dve, c, e, q, ratio_ready):
    nc, o = m.nc, m.dve_order
    o.link(dve, nc.vector.tensor_scalar(q, e, 2.0, None, ALU.add))
    o.link(dve, nc.vector.reciprocal(q, q))
    nc.vector.tensor_tensor(e, e, q, ALU.mult).then_inc(ratio_ready, 1)
    dve.wait_ge(ratio_ready, c + 1)


def softplus_tail(eng, ops, o, s, sq, p, relu, delta, delta_ready, fused):
    def times(p, scalar, by, op0, op1, out=None):
        out = p if out is None else out
        if fused:
            return ops.scalar_tensor_tensor(out=out, in0=p, scalar=scalar, in1=by, op0=op0, op1=op1)
        o.link(eng, ops.tensor_scalar(p, p, scalar, None, op0))
        return ops.tensor_tensor(out, p, by, op1)

    o.link(eng, ops.tensor_tensor(sq, s, s, ALU.mult))
    o.link(eng, ops.tensor_scalar(p, sq, 1 / 11, None, ALU.mult))
    for odd in (9, 7, 5, 3):
        o.link(eng, times(p, 1 / odd, sq, ALU.add, ALU.mult))
    o.link(eng, times(p, 1.0, s, ALU.add, ALU.mult))
    times(p, 2.0, relu, ALU.mult, ALU.add, out=delta).then_inc(delta_ready, 1)



def experts(m, n, j, tag, routed, top, rows, chunks, shared=0, normalize=False, floor=None):
    nc = m.nc
    E = routed + shared
    R = routed + (1 if shared else 0)
    F = rows * chunks
    PAD = 8 - top
    SLOTS = 4
    GROUPS = E // SLOTS
    STEPS = 2 * SLOTS
    UNITS = STEPS * chunks
    sb, sem = m.sb, lambda s: m.sem(tag + s)
    router = m.w[tag + "router"]
    w_in = [sb(tag + f"w_in{s}", [P, KD, 2 * F]) for s in range(SLOTS)]
    w_down = [sb(tag + f"w_down{s}", [rows, chunks, D]) for s in range(SLOTS)]
    silu = [sb(tag + f"silu{i}", [rows, HALF]) for i in range(2)]
    act_in = [sb(tag + f"gated{i}", [rows, chunks, HALF]) for i in range(2)]
    combine = sb(tag + "combine", [P, TILES, E])
    probs = sb(tag + "probs", [P, TILES, routed + PAD])
    rest = sb(tag + "rest", [P, TILES, routed + PAD])
    best = sb(tag + "best", [P, TILES, 8])
    row = sb(tag + "row", [P, TILES])
    logits = m.pair(2)[:, 0:TILES * R].rearrange("p (t e) -> p t e", e=R)
    routed_ready, less_max, exps, combine_ready, shared_ready = (
        sem(s) for s in ("logits", "less_max", "exps", "combine", "shared"))
    filled, silu_done, gated, down_done, accumulated = (
        sem(s) for s in ("filled", "silu", "gated", "down", "accumulated"))
    loaded = [sem(f"loaded{s}") for s in range(SLOTS)]

    def src(name, e):
        return m.dram[tag + name][bass.ds(e, 1)].rearrange("o p x -> (o p) x")

    def load(sp, s, e):
        sp.dma_start(w_in[s][:].rearrange("p k f -> p (k f)"), src("w_in", e)).then_inc(loaded[s], 16)
        sp.dma_start(w_down[s][:].rearrange("p c d -> p (c d)"), src("w_down", e)).then_inc(loaded[s], 16)

    with nc.Block(name=tag + "block") as block:
        @block.sync
        def _(sp):
            for s in range(SLOTS):
                load(sp, s, s)
            with sp.Fori(1, GROUPS) as i:
                for s in range(SLOTS):
                    sp.wait_ge(down_done, (i * SLOTS + s - SLOTS + 1) * TILES + 2 * 4)
                    load(sp, s, i * SLOTS + s)

        @block.gpsimd
        def _(pool):
            norm_gpsimd(m, pool, n)

        @block.tensor
        def _(pe):
            norm_tensor(m, pe, n)
            wait_hT(m, pe, j)
            m.wait_weights(pe, tag)
            for t in range(TILES):
                for k in range(KD):
                    ins = nc.tensor.matmul(logits[:, t, :], lhsT=m.hT[:, k, t * P:(t + 1) * P], rhs=router[:, k, :],
                                           start=(k == 0), stop=(k == KD - 1))
            ins.then_inc(routed_ready, 1)
            pe.wait_ge(combine_ready, 1)
            pe.sem_inc(down_done, 2 * 4)

            with pe.Fori(0, GROUPS) as i:
                def up(s, half):
                    if half == 0:
                        pe.wait_ge(loaded[s], (i + 1) * 32)
                    for c in range(chunks):
                        q = (2 * s + half) * chunks + c
                        pe.wait_ge(gated, i * UNITS + (q + 1))
                        ps = m.pair(q % 2, rows)
                        for part in range(2):
                            for k in range(KD):
                                at = part * F + c * rows
                                ins = nc.tensor.matmul(ps[:, part * HALF:(part + 1) * HALF],
                                                       lhsT=w_in[s][:, k, at:at + rows],
                                                       rhs=m.hT[:, k, half * HALF:(half + 1) * HALF],
                                                       start=(k == 0), stop=(k == KD - 1))
                        ins.then_inc(filled, 1)

                def down(s, half):
                    step = 2 * s + half
                    pe.wait_ge(gated, i * UNITS + ((step + 1) * chunks + 2))
                    pe.wait_ge(accumulated, i * (4 * STEPS) + (4 * step + 4))
                    for tt in range(4):
                        for c in range(chunks):
                            ins = nc.tensor.matmul(m.pair(2 + half)[:, tt * D:(tt + 1) * D],
                                                   lhsT=act_in[half][:, c, tt * P:(tt + 1) * P],
                                                   rhs=w_down[s][:, c, :], start=(c == 0), stop=(c == chunks - 1))
                        ins.then_inc(down_done, 1)

                for step in range(STEPS):
                    up(step // 2, step % 2)
                    if step:
                        down((step - 1) // 2, (step - 1) % 2)
                down(SLOTS - 1, 1)

        @block.scalar
        def _(act):
            norm_scalar(m, act, j)
            act.wait_ge(less_max, 1)
            nc.scalar.activation(probs[:, :, 0:routed], probs[:, :, 0:routed], ACT.Exp).then_inc(exps, 1)
            if shared:
                gate = logits[:, :, routed:R].to_broadcast([P, TILES, shared])
                nc.scalar.activation(combine[:, :, routed:E], gate, ACT.Sigmoid).then_inc(shared_ready, 1)
            with act.Fori(0, GROUPS) as i:
                for q in range(UNITS):
                    act.wait_ge(filled, i * UNITS + (q + 1))
                    act.wait_ge(gated, i * UNITS + (q + 1))
                    nc.scalar.activation(silu[q % 2][:], m.pair(q % 2, rows)[:, 0:HALF], ACT.Silu).then_inc(silu_done, 1)

        @block.vector
        def _(dve):
            o = m.dve_order
            norm_vector(m, dve, n)
            o.mark(nc.vector.memset(probs[:, :, routed:], -1.0))
            dve.wait_ge(routed_ready, 1)
            o.link(dve, nc.vector.tensor_reduce(row[:], logits[:, :, 0:routed], AX_X, ALU.max))
            nc.vector.tensor_tensor(probs[:, :, 0:routed], logits[:, :, 0:routed],
                                    row[:].unsqueeze(2).to_broadcast([P, TILES, routed]), ALU.subtract).then_inc(less_max, 1)
            dve.wait_ge(exps, 1)
            o.link(dve, nc.vector.tensor_reduce(row[:], probs[:, :, 0:routed], AX_X, ALU.add))
            o.link(dve, nc.vector.reciprocal(row[:], row[:]))
            o.link(dve, nc.vector.tensor_tensor(probs[:, :, 0:routed], probs[:, :, 0:routed],
                                                row[:].unsqueeze(2).to_broadcast([P, TILES, routed]), ALU.mult))
            for t in range(TILES):
                o.mark(nc.vector.max(best[:, t, :], probs[:, t, :]))
            o.wait(dve)
            o.link(dve, nc.vector.memset(best[:, :, top:], -1.0))
            for t in range(TILES):
                o.mark(nc.vector.match_replace(out=rest[:, t, :], in_to_replace=best[:, t, :], in_values=probs[:, t, :],
                                               imm_value=0.0))
            o.wait(dve)
            o.link(dve, nc.vector.tensor_tensor(combine[:, :, 0:routed], probs[:, :, 0:routed], rest[:, :, 0:routed],
                                                ALU.subtract))
            if normalize:
                o.link(dve, nc.vector.tensor_reduce(row[:], combine[:, :, 0:routed], AX_X, ALU.add))
                if floor is not None:
                    o.link(dve, nc.vector.tensor_scalar(row[:], row[:], floor, None, ALU.max))
                o.link(dve, nc.vector.reciprocal(row[:], row[:]))
                o.link(dve, nc.vector.tensor_tensor(combine[:, :, 0:routed], combine[:, :, 0:routed],
                                                    row[:].unsqueeze(2).to_broadcast([P, TILES, routed]), ALU.mult))
            if shared:
                dve.wait_ge(shared_ready, 1)
            dve.sem_inc(combine_ready, 1)
            dve.sem_inc(gated, 2)
            dve.sem_inc(accumulated, 2 * 4)

            with dve.Fori(0, GROUPS) as i:
                def gate(step):
                    for c in range(chunks):
                        q = step * chunks + c
                        dve.wait_ge(silu_done, i * UNITS + (q + 1))
                        dve.wait_ge(down_done, i * (4 * STEPS) + (4 * step + 4))
                        nc.vector.tensor_tensor(act_in[step % 2][:, c, :], silu[q % 2][:],
                                                m.pair(q % 2, rows)[:, HALF:T], ALU.mult).then_inc(gated, 1)

                def accumulate(step):
                    s, half = step // 2, step % 2
                    for tt in range(4):
                        done = 4 * step + tt + 1
                        dve.wait_ge(down_done, i * (4 * STEPS) + (4 * step + tt // 2 * 2 + 2 + 8))
                        dve.wait_ge(accumulated, i * (4 * STEPS) + done)
                        r = m.resid[:, 4 * half + tt, :]
                        nc.vector.scalar_tensor_tensor(out=r, in0=m.pair(2 + half)[:, tt * D:(tt + 1) * D],
                                                       scalar=combine[:, 4 * half + tt, bass.ds(i * SLOTS + s, 1)],
                                                       in1=r, op0=ALU.mult, op1=ALU.add).then_inc(accumulated, 1)

                for step in range(STEPS):
                    gate(step)
                    if step:
                        accumulate(step - 1)
                accumulate(STEPS - 1)



def rotate(m, dve, jobs, name, swapped, cos, sin, tmp, out, bias=(None, None)):
    nc, o = m.nc, m.dve_order
    for x, table, t, b in ((name, cos, tmp[0], bias[0]), (swapped, sin, tmp[1], bias[1])):
        jobs.wait_filled(dve, x)
        src = jobs.pair(x).rearrange("p (b s) -> p b s", s=S)
        if b is None:
            ins = nc.vector.tensor_tensor(t, src, table, ALU.mult)
        else:
            ins = nc.vector.scalar_tensor_tensor(out=t, in0=src, scalar=b, in1=table, op0=ALU.add, op1=ALU.mult)
        ins.then_inc(jobs.empty(x), 1)
        dve.wait_ge(jobs.empty(x), jobs.takers[:jobs.at(x) + 1].count("vector"))
    o.link(dve, nc.vector.tensor_tensor(out, tmp[0], tmp[1], ALU.add))



class Attention:

    def __init__(self, m, tag, heads, causal):
        self.m, self.causal = m, causal
        self.hpc = heads // KD
        self.hd = D // heads
        self.units = self.hpc
        sb, sem = m.sb, lambda s: m.sem(tag + s)
        self.q = sb(tag + "q", [P, B, KD, S])
        self.k = sb(tag + "k", [P, B, KD, S])
        self.v = sb(tag + "v", [P, B * KD, 2, P])
        self.k_head = [sb(tag + f"k_head{i}", [P, S]) for i in range(2)]
        self.prob = [sb(tag + f"prob{i}", [P, 2, S]) for i in range(2)]
        self.probT = [sb(tag + f"probT{i}", [P, 2, 2, P]) for i in range(2)]
        self.neg_max = [sb(tag + f"neg_max{i}", [P, 2]) for i in range(2)]
        self.sums = [sb(tag + f"sums{i}", [P, 2, self.hpc]) for i in range(2)]
        self.out = sb(tag + "out", [P, B, KD, 2, P])
        self.q_now = sb(tag + "q_now", [P, S])
        self.k_now = sb(tag + "k_now", [P, S])
        self.q_ready = sem("q_ready")
        self.mask = m.w[tag + "head_mask"]
        (self.inputs, self.k_ready, self.scored, self.max_ready, self.exp_done, self.turned, self.probT_ready,
         self.mixed, self.out_ready, self.outT_filled, self.outT_ready) = (sem(s) for s in (
             "inputs", "k_ready", "scored", "max_ready", "exp_done", "turned", "probT_ready", "mixed", "out_ready",
             "outT_filled", "outT_ready"))

    def bank(self, i):
        return self.m.psum[:, i * 512:(i + 1) * 512]

    def mask_keys(self, pool):
        nc, n = self.m.nc, self.units
        with pool.Fori(0, B * KD) as i:
            pool.wait_ge(self.scored, i * n + 2)
            q = self.q[:].rearrange("p b c s -> p (b c) s")[:, bass.ds(i, 1), :].rearrange("p o s -> p (o s)")
            nc.gpsimd.tensor_copy(self.q_now[:], q).then_inc(self.q_ready, 1)
            k = self.k[:].rearrange("p b c s -> p (b c) s")[:, bass.ds(i, 1), :].rearrange("p o s -> p (o s)")
            nc.gpsimd.tensor_copy(self.k_now[:], k).then_inc(self.q_ready, 1)
            pool.wait_ge(self.q_ready, i * 2 + 2)
            for h in range(n):
                pool.wait_ge(self.scored, i * n + (h + 1))
                nc.gpsimd.tensor_tensor(self.k_head[h % 2][:], self.k_now[:], self.mask[:, h:h + 1].to_broadcast([P, S]),
                                        ALU.mult).then_inc(self.k_ready, 1)

    def tensor(self, pe):
        nc, m, n = self.m.nc, self.m, self.units
        pe.sem_inc(self.scored, 2)
        pe.sem_inc(self.turned, 2)
        pe.sem_inc(self.mixed, 2)
        with pe.Fori(0, B * KD) as i:
            def score(h):
                pe.wait_ge(self.k_ready, i * n + (h + 1))
                pe.wait_ge(self.exp_done, i * n + (h + 1))
                out, k = self.bank(h % 2), self.k_head[h % 2]
                if h == 0:
                    pe.wait_ge(self.q_ready, i * 2 + 2)
                for qt in range(2):
                    lhs = self.q_now[:, qt * P:(qt + 1) * P]
                    if not self.causal:
                        ins = nc.tensor.matmul(out[:, qt * S:(qt + 1) * S], lhsT=lhs, rhs=k[:], start=True, stop=True)
                        continue
                    for kt in range(qt + 1):
                        cols = out[:, qt * S + kt * P:qt * S + (kt + 1) * P]
                        ins = nc.tensor.matmul(cols, lhsT=lhs, rhs=k[:, kt * P:(kt + 1) * P], start=True, stop=kt < qt)
                    ins = nc.tensor.matmul(cols, lhsT=m.ident[:], rhs=m.w["causal"][:], start=False, stop=True)
                ins.then_inc(self.scored, 1)

            def turn(h):
                pe.wait_ge(self.exp_done, i * n + (h + 3))
                pe.wait_ge(self.probT_ready, i * n + (h + 1))
                for kt in range(2):
                    for qt in range(2):
                        if self.causal and kt > qt:
                            continue
                        at = (kt * 2 + qt) * P
                        ins = nc.tensor.transpose(self.bank(2 + h % 2)[:, at:at + P],
                                                  self.prob[h % 2][:, qt, kt * P:(kt + 1) * P], m.ident[:])
                ins.then_inc(self.turned, 1)

            def mix(h):
                pe.wait_ge(self.probT_ready, i * n + (h + 3))
                if h == 0:
                    pe.wait_ge(self.out_ready, i + 1)
                for qt in range(2):
                    kts = range(qt + 1) if self.causal else range(2)
                    for kt in kts:
                        v = self.v[:, bass.ds(i, 1), kt, h * self.hd:(h + 1) * self.hd].rearrange("p o s -> p (o s)")
                        at = qt * P + h * self.hd
                        ins = nc.tensor.matmul(self.bank(4)[:, at:at + self.hd], lhsT=self.probT[h % 2][:, kt, qt, :],
                                               rhs=v, start=(kt == 0), stop=(kt == kts[-1]))
                ins.then_inc(self.mixed, 1)

            for h in range(n + 2):
                if h < n:
                    score(h)
                if 1 <= h <= n:
                    turn(h - 1)
                if h >= 2:
                    mix(h - 2)

    def scalar(self, act):
        nc, n = self.m.nc, self.units
        act.sem_inc(self.exp_done, 2)
        with act.Fori(0, B * KD) as i:
            def exp(h):
                act.wait_ge(self.max_ready, i * n + (h + 1))
                act.wait_ge(self.turned, i * n + (h + 1))
                for qt in range(2):
                    keys = (qt + 1) * P if self.causal else S
                    ins = nc.scalar.activation(self.prob[h % 2][:, qt, 0:keys], self.bank(h % 2)[:, qt * S:qt * S + keys],
                                               ACT.Exp, bias=self.neg_max[h % 2][:, qt:qt + 1],
                                               accum_out=self.sums[0][:, qt, h:h + 1])
                ins.then_inc(self.exp_done, 1)

            act.wait_ge(self.out_ready, i + 1)
            for h in range(n):
                exp(h)

    def vector(self, dve):
        nc, m, n, o = self.m.nc, self.m, self.units, self.m.dve_order
        dve.sem_inc(self.out_ready, 1)
        dve.sem_inc(self.probT_ready, 2)
        base = o.made
        with dve.Fori(0, B * KD) as i:
            o.turn, o.made = i * 2, base
            def maximum(h):
                dve.wait_ge(self.scored, i * n + (h + 3))
                dve.wait_ge(self.exp_done, i * n + (h + 1))
                bank = self.bank(h % 2)
                if self.causal:
                    for qt in range(2):
                        ins = nc.vector.tensor_reduce(self.neg_max[h % 2][:, qt:qt + 1],
                                                      bank[:, qt * S:qt * S + (qt + 1) * P], AX_X, ALU.max, negate=True)
                else:
                    ins = nc.vector.tensor_reduce(self.neg_max[h % 2][:], bank.rearrange("p (q k) -> p q k", k=S), AX_X,
                                                  ALU.max, negate=True)
                ins.then_inc(self.max_ready, 1)

            def move(h):
                dve.wait_ge(self.turned, i * n + (h + 3))
                dve.wait_ge(self.mixed, i * n + (h + 1))
                bank = self.bank(2 + h % 2)
                dst = self.probT[h % 2][:].rearrange("p k q s -> p (k q s)")
                if self.causal:
                    nc.vector.tensor_copy(dst[:, 0:2 * P], bank[:, 0:2 * P])
                    ins = nc.vector.tensor_copy(dst[:, 3 * P:4 * P], bank[:, 3 * P:4 * P])
                else:
                    ins = nc.vector.tensor_copy(dst, bank)
                ins.then_inc(self.probT_ready, 1)

            for h in range(n + 1):
                if h < n:
                    maximum(h)
                if h:
                    move(h - 1)
            dve.wait_ge(self.exp_done, i * n + (n + 2))
            o.link(dve, nc.vector.reciprocal(self.sums[1][:], self.sums[0][:]))
            dve.wait_ge(self.mixed, i * n + (n + 2))
            out = self.out[:].rearrange("p b c q f -> p (b c) (q f)")[:, bass.ds(i, 1), :].rearrange(
                "p o (x d) -> p (o x) d", d=self.hd)
            src = self.bank(4)[:, 0:2 * P].rearrange("p (x d) -> p x d", d=self.hd)
            scale = self.sums[1][:].rearrange("p q h -> p (q h)").unsqueeze(2).to_broadcast([P, 2 * self.hpc, self.hd])
            o.link(dve, nc.vector.tensor_tensor(out, src, scale, ALU.mult))
            dve.sem_inc(self.out_ready, 1)
        o.turn, o.made = None, base + 2 * B * KD


def softmax_attention(m, n, j, tag, heads, causal):
    nc = m.nc
    self_attn = causal
    w = lambda name: m.w[tag + name]
    a = Attention(m, tag, heads, causal)
    names = [] if self_attn else ["angle"]
    for c in range(KD):
        names += [f"q{c}", f"q{c}s", f"k{c}", f"k{c}s"]
    jobs = Jobs(m, tag + "in", 2, [(x, "vector") for x in names] + [("v0", "scalar"), ("v1", "scalar")])
    ends = Jobs(m, tag + "end", 2, [("out0", "vector"), ("out1", "vector")])
    tmp = [m.sb(tag + f"rot{i}", [P, B, S]) for i in range(2)]
    if self_attn:
        tables = [w(x)[:].unsqueeze(1).to_broadcast([P, B, S]) for x in ("cos", "sin")]
    else:
        turns = [m.sb(tag + f"turns{i}", [P, T]) for i in range(2)]
        whole = [m.sb(tag + f"whole{i}", [P, T]) for i in range(2)]
        tables = [t[:].rearrange("p (b s) -> p b s", s=S) for t in turns]
        turns_ready, table_ready = m.sem(tag + "turns"), m.sem(tag + "table")
    with nc.Block(name=tag + "block") as block:
        @block.gpsimd
        def _(pool):
            norm_gpsimd(m, pool, n)
            pool.wait_ge(a.inputs, 2)
            a.mask_keys(pool)

        @block.tensor
        def _(pe):
            norm_tensor(m, pe, n)
            wait_hT(m, pe, j)
            m.wait_weights(pe, tag)
            hT = feature_rhs(m.hT)
            keys = hT if self_attn else lambda k, cols: m.ctxT[:, cols]
            kc = KD if self_attn else 1
            if not self_attn:
                project(m, pe, jobs, "angle", lambda k: w("freq")[:], lambda k, cols: w("pos")[:, cols], 1)
            for c in range(KD):
                project(m, pe, jobs, f"q{c}", wcols(w("q"), c), hT, KD)
                project(m, pe, jobs, f"q{c}s", wcols(w("q"), KD + c), hT, KD)
                project(m, pe, jobs, f"k{c}", wcols(w("k"), c), keys, kc)
                project(m, pe, jobs, f"k{c}s", wcols(w("k"), KD + c), keys, kc)
            src = m.hT if self_attn else m.ctxT[:].unsqueeze(1)
            project_tokens(m, pe, jobs, ("v0", "v1"), lambda k, t: src[:, k, t * P:(t + 1) * P],
                           lambda k, t: w("v")[:, k, :], kc)
            pe.wait_ge(a.inputs, 3)
            a.tensor(pe)
            pe.wait_ge(a.out_ready, 1 + B * KD)
            for q in range(2):
                for t in range(4 * q, 4 * q + 4):
                    for c in range(KD):
                        ins = nc.tensor.transpose(m.pair(c)[:, t * P:(t + 1) * P], a.out[:, t // 2, c, t % 2, :],
                                                  m.ident[:])
                ins.then_inc(a.outT_filled, 1)
            pe.wait_ge(a.outT_ready, 4)
            project_tokens(m, pe, ends, ("out0", "out1"), lambda k, t: m.hT[:, k, t * P:(t + 1) * P],
                           lambda k, t: w("o")[:, k, :], KD)

        @block.scalar
        def _(act):
            norm_scalar(m, act, j)
            if not self_attn:
                act.wait_ge(turns_ready, 2)
                for i in range(2):
                    nc.scalar.activation(turns[i][:], turns[i][:], ACT.Sin, scale=SIN_SCALE).then_inc(table_ready, 1)
            for q in range(2):
                name = f"v{q}"
                jobs.wait_filled(act, name)
                for b in range(2):
                    for qt in range(2):
                        src = jobs.pair(name)[:, (2 * b + qt) * D:(2 * b + qt + 1) * D].rearrange("p (c f) -> p c f", c=KD)
                        at = (2 * q + b) * KD
                        ins = nc.scalar.activation(a.v[:, at:at + KD, qt, :], src, ACT.Copy)
                ins.then_inc(jobs.empty(name), 1)
            act.wait_ge(jobs.emptied["scalar"], 2)
            act.sem_inc(a.inputs, 1)
            a.scalar(act)
            for q in range(2):
                act.wait_ge(a.outT_filled, q + 1)
                for c in range(KD):
                    cols = slice(q * HALF, (q + 1) * HALF)
                    nc.scalar.activation(m.hT[:, c, cols], m.pair(c)[:, cols], ACT.Copy).then_inc(a.outT_ready, 1)

        @block.vector
        def _(dve):
            o = m.dve_order
            norm_vector(m, dve, n)
            m.wait_weights(dve, tag)
            if not self_attn:
                jobs.wait_filled(dve, "angle")
                ps = jobs.pair("angle")
                o.mark(nc.vector.tensor_scalar(turns[0][:], ps, 0.25, None, ALU.add))
                nc.vector.tensor_copy(turns[1][:], ps).then_inc(jobs.empty("angle"), 1)
                dve.wait_ge(jobs.emptied["vector"], 1)
                for i in range(2):
                    o.mark(nc.vector.tensor_scalar(whole[i][:], turns[i][:], ROUND, -ROUND, ALU.add, ALU.add))
                o.wait(dve)
                for i in range(2):
                    nc.vector.tensor_tensor(turns[i][:], turns[i][:], whole[i][:], ALU.subtract).then_inc(turns_ready, 1)
                dve.wait_ge(table_ready, 2)
            for c in range(KD):
                for x, out in (("q", a.q), ("k", a.k)):
                    rotate(m, dve, jobs, f"{x}{c}", f"{x}{c}s", tables[0], tables[1], [t[:] for t in tmp],
                           out[:, :, c, :])
            dve.sem_inc(a.inputs, 2)
            a.vector(dve)
            add_tokens(m, dve, ends, ("out0", "out1"), bias=None if self_attn else w("o_b")[:])



def feature_attention(m, n, j):
    nc = m.nc
    tag = "l2a_"
    w = lambda name: m.w[tag + name]
    HPC, HD = 8, 16
    chunks = [("q", 0), ("q", 1), ("k", 0)]
    jobs = Jobs(m, tag + "in", 2, [(f"{x}{c}{s}", "vector") for x, c in chunks for s in ("", "s")]
                + [("v", "vector"), ("norm", "scalar")] + [(f"p{x}{c}", "vector") for x, c in chunks]
                + [("t0", "scalar"), ("t1", "scalar"), ("out0", "vector"), ("out1", "vector")])
    tmp = [m.sb(tag + f"rot{i}", [P, B, S]) for i in range(2)]
    x = {f"{k}{c}": m.sb(tag + f"{k}{c}", [P, T]) for k, c in chunks}
    sq = {f"{k}{c}": m.sb(tag + f"sq_{k}{c}", [P, T]) for k, c in chunks}
    feats = sq
    v = m.sb(tag + "v", [P, TILES, P])
    norm = m.sb(tag + "norm", [P, len(chunks), TILES, HPC])
    whole = m.sb(tag + "whole", [P, T])
    pair_prod = [m.sb(tag + f"pair_prod{c}", [P, HPC, HPC, HD]) for c in range(KD)]
    value_prod = [m.sb(tag + f"value_prod{c}", [P, HPC, HD, HPC]) for c in range(KD)]
    weight = [m.sb(tag + f"weight{c}", [P, HPC, HPC]) for c in range(KD)]
    att = m.sb(tag + "att", [P, TILES, D])
    (rotated, turns_ready, feats_ready, v_ready, pair_done, weight_done, value_done, att_done) = (
        m.sem(tag + s) for s in ("rotated", "turns", "feats", "v_ready", "pair", "weight", "value", "att"))

    def head_products(eng, ops, c, t, step, done):
        if step == 0:
            q = feats[f"q{c}"][:, t * P:(t + 1) * P].rearrange("p (h f) -> p h f", f=HD)
            k = feats["k0"][:, t * P:(t + 1) * P].rearrange("p (h f) -> p h f", f=HD)
            ops.tensor_tensor(pair_prod[c][:], q.unsqueeze(1).to_broadcast([P, HPC, HPC, HD]),
                              k.unsqueeze(2).to_broadcast([P, HPC, HPC, HD]), ALU.mult).then_inc(done, 1)
        else:
            g = weight[c][:].rearrange("p k q -> p q k").unsqueeze(2).to_broadcast([P, HPC, HD, HPC])
            vt = v[:, t, :].rearrange("p (k d) -> p d k", d=HD).unsqueeze(1).to_broadcast([P, HPC, HD, HPC])
            ops.tensor_tensor(value_prod[c][:], g, vt, ALU.mult).then_inc(done, 1)

    pool_pair, pool_value = m.sem(tag + "pool_pair"), m.sem(tag + "pool_value")
    stored = [m.sem(tag + f"stored{b}") for b in range(B)]
    att_back = m.sem(tag + "att_back")
    scratch = nc.dram_tensor(tag + "scratch", (B, 2 * HPC, S, HD), F32).ap()
    with nc.Block(name=tag + "block") as block:
        @block.sync
        def _(sp):
            for t in range(TILES):
                sp.wait_ge(att_done, 2 * t + 2)
                dst = scratch[t // 2, :, t % 2 * P:(t % 2 + 1) * P, :].rearrange("h s d -> s h d")
                sp.dma_start(dst, att[:, t, :].rearrange("p (h d) -> p h d", d=HD)).then_inc(stored[t // 2], 16)
            rows = scratch.rearrange("b h (s r) d -> b (h s) (r d)", r=HD).rearrange("b (q p) f -> b p q f", p=P)
            for b in range(B):
                sp.wait_ge(stored[b], 32)
                sp.dma_start(m.h[:, 2 * b:2 * b + 2, :], rows[b]).then_inc(att_back, 16)

        @block.gpsimd
        def _(pool):
            norm_gpsimd(m, pool, n)
            pool.wait_ge(feats_ready, 3)
            pool.wait_ge(v_ready, 1)
            head_products(pool, nc.gpsimd, 1, 0, 0, pool_pair)
            for t in range(TILES):
                if t + 1 < TILES:
                    pool.wait_ge(weight_done, 2 * t + 2)
                    head_products(pool, nc.gpsimd, 1, t + 1, 0, pool_pair)
                pool.wait_ge(weight_done, 2 * t + 2)
                if t:
                    pool.wait_ge(att_done, 2 * t)
                head_products(pool, nc.gpsimd, 1, t, 1, pool_value)

        @block.tensor
        def _(pe):
            norm_tensor(m, pe, n)
            wait_hT(m, pe, j)
            m.wait_weights(pe, tag)
            hT = feature_rhs(m.hT)
            for k, c in chunks:
                half = w(k)[:].shape[2] // (2 * P)
                project(m, pe, jobs, f"{k}{c}", wcols(w(k), c), hT, KD)
                project(m, pe, jobs, f"{k}{c}s", wcols(w(k), half + c), hT, KD)
            jobs.wait_room(pe, "v")
            for t in range(TILES):
                for k in range(KD):
                    ins = nc.tensor.matmul(jobs.pair("v")[:, t * P:(t + 1) * P], lhsT=m.hT[:, k, t * P:(t + 1) * P],
                                           rhs=w("v")[:, k, :], start=(k == 0), stop=(k == KD - 1))
            ins.then_inc(jobs.filled, 1)
            jobs.wait_room(pe, "norm")
            for i, (k, c) in enumerate(chunks):
                pe.wait_ge(rotated, i + 1)
                for t in range(TILES):
                    at = (i * TILES + t) * HPC
                    ins = nc.tensor.matmul(jobs.pair("norm")[:, at:at + HPC], lhsT=sq[f"{k}{c}"][:, t * P:(t + 1) * P],
                                           rhs=w("ones")[:], start=True, stop=True)
            ins.then_inc(jobs.filled, 1)
            for k, c in chunks:
                name = f"p{k}{c}"
                jobs.wait_room(pe, name)
                for t in range(TILES):
                    ins = nc.tensor.matmul(jobs.pair(name)[:, t * P:(t + 1) * P], lhsT=x[f"{k}{c}"][:, t * P:(t + 1) * P],
                                           rhs=w("rand")[:], start=True, stop=True)
                ins.then_inc(jobs.filled, 1)
            pe.wait_ge(att_back, 16 * B)
            for c in range(KD):
                jobs.wait_room(pe, f"t{c}")
                for t in range(TILES):
                    ins = nc.tensor.transpose(jobs.pair(f"t{c}")[:, t * P:(t + 1) * P], m.h[:, t, c * P:(c + 1) * P],
                                              m.ident[:])
                ins.then_inc(jobs.filled, 1)
            pe.wait_ge(jobs.emptied["scalar"], 3)
            project_tokens(m, pe, jobs, ("out0", "out1"), lambda k, t: m.hT[:, k, t * P:(t + 1) * P],
                           lambda k, t: w("o")[:, k, :], KD)

        @block.scalar
        def _(act):
            norm_scalar(m, act, j)
            jobs.wait_filled(act, "norm")
            nc.scalar.activation(norm[:].rearrange("p a t h -> p (a t h)"),
                                 jobs.pair("norm")[:, 0:len(chunks) * TILES * HPC], ACT.Sqrt).then_inc(jobs.empty("norm"), 1)
            for i, (k, c) in enumerate(chunks):
                act.wait_ge(turns_ready, i + 1)
                f = feats[f"{k}{c}"][:]
                nc.scalar.activation(f, f, ACT.Sin, scale=SIN_SCALE).then_inc(feats_ready, 1)
            for c in range(KD):
                jobs.wait_filled(act, f"t{c}")
                nc.scalar.activation(m.hT[:, c, :], jobs.pair(f"t{c}"), ACT.Copy, scale=2.0 / HD).then_inc(jobs.empty(f"t{c}"), 1)

        @block.vector
        def _(dve):
            o = m.dve_order
            norm_vector(m, dve, n)
            m.wait_weights(dve, tag)
            tables = [w(t)[:].unsqueeze(1).to_broadcast([P, B, S]) for t in ("cos", "sin")]
            for k, c in chunks:
                b = w(k + "_b")
                half = b[:].shape[1] // 2
                rotate(m, dve, jobs, f"{k}{c}", f"{k}{c}s", tables[0], tables[1], [t[:] for t in tmp],
                       x[f"{k}{c}"][:].rearrange("p (b s) -> p b s", s=S),
                       bias=(b[:, c:c + 1], b[:, half + c:half + c + 1]))
                nc.vector.tensor_tensor(sq[f"{k}{c}"][:], x[f"{k}{c}"][:], x[f"{k}{c}"][:], ALU.mult).then_inc(rotated, 1)
            jobs.wait_filled(dve, "v")
            nc.vector.tensor_tensor(v[:], jobs.pair("v").rearrange("p (t d) -> p t d", d=P),
                                    w("v_b")[:].unsqueeze(1).to_broadcast([P, TILES, P]), ALU.add).then_inc(jobs.empty("v"), 1)
            dve.wait_ge(jobs.empty("v"), 2 * len(chunks) + 1)
            dve.sem_inc(v_ready, 1)
            dve.wait_ge(jobs.empty("norm"), 1)
            flat = norm[:].rearrange("p a t h -> p (a t h)")
            o.link(dve, nc.vector.tensor_scalar(flat, flat, 1e-6, None, ALU.max))
            o.link(dve, nc.vector.reciprocal(flat, flat))
            o.link(dve, nc.vector.tensor_scalar(flat, flat, float(1 / TWO_PI), None, ALU.mult))
            for i, (k, c) in enumerate(chunks):
                name = f"p{k}{c}"
                jobs.wait_filled(dve, name)
                f = feats[f"{k}{c}"][:]
                heads = lambda a: a.rearrange("p (x f) -> p x f", f=HD)
                r = norm[:, i, :, :].rearrange("p t h -> p (t h)").unsqueeze(2).to_broadcast([P, TILES * HPC, HD])
                nc.vector.tensor_tensor(heads(f), heads(jobs.pair(name)), r, ALU.mult).then_inc(jobs.empty(name), 1)
                dve.wait_ge(jobs.empty(name), jobs.takers[:jobs.at(name) + 1].count("vector"))
                o.link(dve, nc.vector.tensor_scalar(heads(f)[:, :, 8:16], heads(f)[:, :, 8:16], 0.25, None, ALU.add))
                o.link(dve, nc.vector.tensor_scalar(whole[:], f, ROUND, -ROUND, ALU.add, ALU.add))
                nc.vector.tensor_tensor(f, f, whole[:], ALU.subtract).then_inc(turns_ready, 1)
                dve.wait_ge(turns_ready, i + 1)
            dve.wait_ge(feats_ready, 3)
            for t in range(TILES):
                head_products(dve, nc.vector, 0, t, 0, pair_done)
                for c in range(KD):
                    dve.wait_ge((pair_done, pool_pair)[c], t + 1)
                    nc.vector.tensor_reduce(weight[c][:], pair_prod[c][:], AX_X, ALU.add).then_inc(weight_done, 1)
                dve.wait_ge(weight_done, 2 * t + 1)
                head_products(dve, nc.vector, 0, t, 1, value_done)
                for c in range(KD):
                    dve.wait_ge((value_done, pool_value)[c], t + 1)
                    out = att[:, t, c * P:(c + 1) * P].rearrange("p (h d) -> p h d", d=HD)
                    nc.vector.tensor_reduce(out, value_prod[c][:], AX_X, ALU.add).then_inc(att_done, 1)
            add_tokens(m, dve, jobs, ("out0", "out1"), bias=w("o_b")[:])



def context_mixing(m, n, j):
    nc = m.nc
    tag = "l2x_"
    w = lambda name: m.w[tag + name]
    jobs = Jobs(m, tag + "in", 2, [("q", "scalar"), ("k", "scalar"), ("e0", "scalar"), ("e1", "scalar"),
                                   ("t0", "scalar"), ("t1", "scalar"), ("out0", "vector"), ("out1", "vector")])
    q = m.sb(tag + "q", [P, T])
    k = m.sb(tag + "k", [P, T])
    att = m.sb(tag + "att", [P, TILES, S])
    attT = m.sb(tag + "attT", [P, TILES, S])
    neg_max = m.sb(tag + "neg_max", [P, TILES])
    sums = m.sb(tag + "sums", [P, TILES])
    max_ready, att_ready = m.sem(tag + "max"), m.sem(tag + "att")
    with nc.Block(name=tag + "block") as block:
        @block.gpsimd
        def _(pool):
            norm_gpsimd(m, pool, n)

        @block.tensor
        def _(pe):
            norm_tensor(m, pe, n)
            m.wait_weights(pe, tag)
            ctx = lambda k, cols: m.ctxT[:, cols]
            for x in "qk":
                project(m, pe, jobs, x, lambda k, x=x: w(x)[:], ctx, 1)
            pe.wait_ge(jobs.emptied["scalar"], 2)
            wait_hT(m, pe, j)
            for half in range(2):
                name = f"e{half}"
                jobs.wait_room(pe, name)
                for t in range(4 * half, 4 * half + 4):
                    b = t // 2
                    ins = nc.tensor.matmul(jobs.pair(name)[:, (t % 4) * S:(t % 4 + 1) * S], lhsT=q[:, t * P:(t + 1) * P],
                                           rhs=k[:, b * S:(b + 1) * S], start=True, stop=True)
                ins.then_inc(jobs.filled, 1)
            pe.wait_ge(att_ready, 1)
            for half in range(2):
                name = f"t{half}"
                jobs.wait_room(pe, name)
                for b in range(2 * half, 2 * half + 2):
                    for nt in range(2):
                        for mt in range(2):
                            at = (b % 2 * 2 + nt) * S + mt * P
                            ins = nc.tensor.transpose(jobs.pair(name)[:, at:at + P],
                                                      att[:, 2 * b + mt, nt * P:(nt + 1) * P], m.ident[:])
                ins.then_inc(jobs.filled, 1)
            pe.wait_ge(jobs.emptied["scalar"], 6)
            project_tokens(m, pe, jobs, ("out0", "out1"), lambda k, t: m.hT[:, k, t * P:(t + 1) * P],
                           lambda k, t: attT[:, t // 2 * 2 + k, :], KD)

        @block.scalar
        def _(act):
            norm_scalar(m, act, j)
            m.wait_weights(act, tag)
            for x, dst in (("q", q), ("k", k)):
                jobs.wait_filled(act, x)
                nc.scalar.activation(dst[:], jobs.pair(x), ACT.Identity, bias=w(x + "_b")[:, 0:1]).then_inc(jobs.empty(x), 1)
            for half in range(2):
                name = f"e{half}"
                act.wait_ge(max_ready, half + 1)
                for t in range(4 * half, 4 * half + 4):
                    ins = nc.scalar.activation(att[:, t, :], jobs.pair(name)[:, (t % 4) * S:(t % 4 + 1) * S], ACT.Exp,
                                               bias=neg_max[:, t:t + 1], accum_out=sums[:, t:t + 1])
                ins.then_inc(jobs.empty(name), 1)
            for half in range(2):
                name = f"t{half}"
                jobs.wait_filled(act, name)
                nc.scalar.activation(attT[:, 4 * half:4 * half + 4, :].rearrange("p t s -> p (t s)"), jobs.pair(name),
                                     ACT.Copy).then_inc(jobs.empty(name), 1)

        @block.vector
        def _(dve):
            o = m.dve_order
            norm_vector(m, dve, n)
            for half in range(2):
                name = f"e{half}"
                jobs.wait_filled(dve, name)
                nc.vector.tensor_reduce(neg_max[:, 4 * half:4 * half + 4], jobs.pair(name).rearrange("p (t s) -> p t s", s=S),
                                        AX_X, ALU.max, negate=True).then_inc(max_ready, 1)
            dve.wait_ge(jobs.emptied["scalar"], 4)
            o.link(dve, nc.vector.reciprocal(sums[:], sums[:]))
            nc.vector.tensor_tensor(att[:], att[:], sums[:].unsqueeze(2).to_broadcast([P, TILES, S]),
                                    ALU.mult).then_inc(att_ready, 1)
            add_tokens(m, dve, jobs, ("out0", "out1"))



def gated_recurrence(m, n, j):
    nc = m.nc
    tag = "l3a_"
    w = lambda name: m.w[tag + name]
    kinds = ("in", "decay", "gate")
    jobs = Jobs(m, tag + "in", 2, [(f"{x}{c}", "scalar") for x in kinds for c in range(KD)]
                + [("out0", "vector"), ("out1", "vector")])
    val = {x: m.sb(tag + x, [P, KD, T]) for x in kinds}
    part = m.sb(tag + "part", [P, T])
    att = m.sb(tag + "att", [P, KD, T])
    bias_ready, att_ready = m.sem(tag + "bias"), m.sem(tag + "att")
    with nc.Block(name=tag + "block") as block:
        @block.gpsimd
        def _(pool):
            norm_gpsimd(m, pool, n)
            m.wait_weights(pool, tag)
            nc.gpsimd.tensor_tensor(w("decay_b")[:], w("decay_b")[:], w("decay_b2")[:], ALU.add).then_inc(bias_ready, 1)

        @block.tensor
        def _(pe):
            norm_tensor(m, pe, n)
            wait_hT(m, pe, j)
            m.wait_weights(pe, tag)
            for x in kinds:
                for c in range(KD):
                    project(m, pe, jobs, f"{x}{c}", wcols(w(x), c), feature_rhs(m.hT), KD)
            pe.wait_ge(att_ready, KD)
            project_tokens(m, pe, jobs, ("out0", "out1"), lambda k, t: att[:, k, t * P:(t + 1) * P],
                           lambda k, t: w("out")[:, k, :], KD)

        @block.scalar
        def _(act):
            norm_scalar(m, act, j)
            act.wait_ge(bias_ready, 1)
            for x in kinds:
                for c in range(KD):
                    name = f"{x}{c}"
                    jobs.wait_filled(act, name)
                    nc.scalar.activation(val[x][:, c, :], jobs.pair(name), ACT.Silu if x == "in" else ACT.Sigmoid,
                                         bias=w(x + "_b")[:, c:c + 1]).then_inc(jobs.empty(name), 1)

        @block.vector
        def _(dve):
            o = m.dve_order
            norm_vector(m, dve, n)
            m.wait_weights(dve, tag)
            for c in range(KD):
                x, d, g = (val[k][:, c, :] for k in kinds)
                dve.wait_ge(jobs.emptied["scalar"], 3 + c)
                o.link(dve, nc.vector.tensor_tensor(part[:], d, x, ALU.mult))
                o.mark(nc.vector.tensor_tensor(x, x, part[:], ALU.subtract))
                o.link(dve, nc.vector.tensor_tensor(d, d, m.w["carry"][:], ALU.mult))
                o.link(dve, nc.vector.tensor_tensor_scan(part[:], d, x, 0.0, ALU.mult, ALU.add))
                dve.wait_ge(jobs.emptied["scalar"], 5 + c)
                nc.vector.tensor_tensor(att[:, c, :], g, part[:], ALU.mult).then_inc(att_ready, 1)
                dve.wait_ge(att_ready, c + 1)
            add_tokens(m, dve, jobs, ("out0", "out1"), bias=w("out_b")[:])



def mx_round(m, eng, ops, o, x, work, scale, inv, out=None):
    nc = m.nc
    blocks = lambda a: a.rearrange("p (b e) -> p b e", e=MX_BLOCK)
    n = x.shape[-1] // MX_BLOCK
    spread = lambda a: a.unsqueeze(2).to_broadcast([P, n, MX_BLOCK])
    o.link(eng, nc.vector.tensor_reduce(scale, blocks(x), AX_X, ALU.max, apply_absolute_value=True))
    o.link(eng, ops.tensor_scalar(scale, scale, 1.0 / FP8_MAX, 1e-30, ALU.mult, ALU.max))
    o.link(eng, nc.vector.reciprocal(inv, scale))
    o.link(eng, ops.tensor_tensor(blocks(x), blocks(x), spread(inv), ALU.mult))
    o.link(eng, ops.tensor_scalar(work.bitcast(I32), x.bitcast(I32), 0x7F800000, None, ALU.bitwise_and))
    o.link(eng, ops.tensor_scalar(work, work, 2.0 ** -6, 1.5 * 2.0 ** 20, ALU.max, ALU.mult))
    o.link(eng, ops.tensor_tensor(x, x, work, ALU.add))
    o.link(eng, ops.tensor_tensor(x, x, work, ALU.subtract))
    return ops.tensor_tensor(blocks(out if out is not None else x), blocks(x), spread(scale), ALU.mult)


def mx_feed_forward(m, n, j):
    nc = m.nc
    tag = "l1f_"
    w = lambda name: m.w[tag + name]
    INNER = 1024
    KI = INNER // P
    natural = {x: m.sb(tag + "nat_" + x, [P, 2 * INNER]) for x in ("gate", "up", "down")}
    gateT, upT = (m.sb(tag + x + "T", [P, KD, INNER]) for x in ("gate", "up"))
    downT = m.sb(tag + "downT", [P, KI, D])
    work = m.sb(tag + "work", [P, 2 * INNER])
    scale = m.sb(tag + "scale", [P, 2 * INNER // MX_BLOCK])
    inv = m.sb(tag + "inv", [P, 2 * INNER // MX_BLOCK])
    silu = m.sb(tag + "silu", [P, INNER])
    inner = m.sb(tag + "inner", [P, INNER])
    innerT = m.sb(tag + "innerT", [P, KI, P])
    (nat_in, w_rounded, w_turned, w_ready, h_rounded, filled, silu_done, inner_done, inner_rounded, inner_turned,
     innerT_ready, down_filled, added) = (m.sem(tag + s) for s in (
         "nat_in", "w_rounded", "w_turned", "w_ready", "h_rounded", "filled", "silu", "inner", "inner_rounded",
         "inner_turned", "innerT", "down", "added"))
    with nc.Block(name=tag + "block") as block:
        @block.sync
        def _(sp):
            for x in ("gate", "up", "down"):
                sp.dma_start(natural[x][:], m.dram[tag + x]).then_inc(nat_in, 16)

        @block.gpsimd
        def _(pool):
            norm_gpsimd(m, pool, n)

        @block.tensor
        def _(pe):
            for i, x in enumerate(("gate", "up", "down")):
                pe.wait_ge(w_rounded, i + 1)
                if i:
                    pe.wait_ge(w_ready, 2 * i)
                for k in range(2):
                    for f in range(KI):
                        if x == "down":
                            chunk, part = 4 * k + f // 2, f % 2
                            src = natural[x][:, part * INNER + chunk * P:part * INNER + (chunk + 1) * P]
                        else:
                            src = natural[x][:, f * D + k * P:f * D + (k + 1) * P]
                        ins = nc.tensor.transpose(m.pair(2 + k)[:, f * P:(f + 1) * P], src, m.ident[:])
                    ins.then_inc(w_turned, 1)
            pe.wait_ge(h_rounded, 1)
            for half in range(2):
                for t in range(4 * half, 4 * half + 4):
                    for k in range(KD):
                        ins = nc.tensor.transpose(m.pair(k)[:, t * P:(t + 1) * P], m.h[:, t, k * P:(k + 1) * P], m.ident[:])
                ins.then_inc(m.turned, 1)
            wait_hT(m, pe, j)
            pe.wait_ge(w_ready, 6)

            def up(t):
                if t:
                    pe.wait_ge(inner_done, t)
                for p, wt in enumerate((gateT, upT)):
                    for half in range(2):
                        for k in range(KD):
                            cols = slice(half * 512, (half + 1) * 512)
                            ins = nc.tensor.matmul(m.pair(p)[:, cols], lhsT=m.hT[:, k, t * P:(t + 1) * P], rhs=wt[:, k, cols],
                                                   start=(k == 0), stop=(k == KD - 1))
                ins.then_inc(filled, 1)

            def down(t):
                pe.wait_ge(inner_rounded, t + 1)
                if t:
                    pe.wait_ge(innerT_ready, t)
                for f in range(KI):
                    ins = nc.tensor.transpose(m.pair(2)[:, f * P:(f + 1) * P], inner[:, f * P:(f + 1) * P], m.ident[:])
                ins.then_inc(inner_turned, 1)
                pe.wait_ge(innerT_ready, t + 1)
                if t:
                    pe.wait_ge(added, t)
                for f in range(KI):
                    ins = nc.tensor.matmul(m.pair(3)[:, 0:D], lhsT=innerT[:, f, :], rhs=downT[:, f, :], start=(f == 0),
                                           stop=(f == KI - 1))
                ins.then_inc(down_filled, 1)

            for t in range(TILES):
                up(t)
                if t:
                    down(t - 1)
            down(TILES - 1)

        @block.scalar
        def _(act):
            for i in range(3):
                for k in range(2):
                    act.wait_ge(w_turned, 2 * i + k + 1)
                    dst = (gateT[:, k, :], upT[:, k, :],
                           downT[:, 4 * k:4 * k + 4, :].rearrange("p f d -> p (f d)"))[i]
                    nc.scalar.activation(dst, m.pair(2 + k), ACT.Copy).then_inc(w_ready, 1)
            norm_scalar(m, act, j)
            for t in range(TILES):
                act.wait_ge(filled, t + 1)
                if t:
                    act.wait_ge(inner_done, t)
                nc.scalar.activation(silu[:], m.pair(0), ACT.Silu).then_inc(silu_done, 1)
                act.wait_ge(inner_turned, t + 1)
                if t:
                    act.wait_ge(down_filled, t)
                nc.scalar.activation(innerT[:].rearrange("p f t -> p (f t)"), m.pair(2), ACT.Copy).then_inc(innerT_ready, 1)

        @block.vector
        def _(dve):
            o = m.dve_order
            norm_vector(m, dve, n)
            dve.wait_ge(m.h_ready, TILES * (n + 1))
            mx_round(m, dve, nc.vector, o, m.h[:].rearrange("p t d -> p (t d)"), work[:], scale[:],
                     inv[:]).then_inc(h_rounded, 1)
            dve.wait_ge(h_rounded, 1)
            dve.wait_ge(nat_in, 48)
            for i, x in enumerate(("gate", "up", "down")):
                mx_round(m, dve, nc.vector, o, natural[x][:], work[:], scale[:], inv[:]).then_inc(w_rounded, 1)
                dve.wait_ge(w_rounded, i + 1)

            def add(t):
                dve.wait_ge(down_filled, t + 1)
                nc.vector.tensor_tensor(m.resid[:, t, :], m.pair(3)[:, 0:D], m.resid[:, t, :], ALU.add).then_inc(added, 1)

            for t in range(TILES):
                dve.wait_ge(silu_done, t + 1)
                if t:
                    dve.wait_ge(inner_turned, t)
                nc.vector.tensor_tensor(inner[:], silu[:], m.pair(1), ALU.mult).then_inc(inner_done, 1)
                dve.wait_ge(inner_done, t + 1)
                nb = INNER // MX_BLOCK
                mx_round(m, dve, nc.vector, o, inner[:], work[:, 0:INNER], scale[:, 0:nb],
                         inv[:, 0:nb]).then_inc(inner_rounded, 1)
                dve.wait_ge(inner_rounded, t + 1)
                if t:
                    add(t - 1)
            add(TILES - 1)



def weights(m):
    m.weight("consts", "ident", [P, P])
    m.ident = m.w["ident"]
    m.weight("consts", "carry", [P, T])
    m.weight("consts", "ctxT", [P, T])
    m.ctxT = m.w["ctxT"]
    m.weight("l0_attn", "l0_qkv", [P, KD, 3 * D])
    m.weight("l0_attn", "l0_out", [P, KD, D])
    for layer in (0, 1):
        g = f"l{layer}s_"
        for name, shape in (("in", [P, D]), ("conv", [P, KD, D_CONV]), ("conv_b", [P, KD]), ("x", [P, KD, X_DBL]),
                            ("dt", [DT_RANK, D]), ("dt_b", [P, KD]), ("a", [P, KD, N_STATE]), ("d", [P, KD])):
            m.weight(g, g + name, shape)
    for group, name, shape in LATER_WEIGHTS:
        m.weight(group, name, shape)


LATER_WEIGHTS = [
    ("l0f_", "l0f_router", [P, KD, 16]), ("l2f_", "l2f_router", [P, KD, 9]), ("l3f_", "l3f_router", [P, KD, 64]),
    ("l1a_", "l1a_q", [P, KD, 2 * D]), ("l1a_", "l1a_k", [P, KD, 2 * D]), ("l1a_", "l1a_v", [P, KD, D]),
    ("l1a_", "l1a_o", [P, KD, D]), ("l1a_", "l1a_cos", [P, S]), ("l1a_", "l1a_sin", [P, S]),
    ("l1a_", "l1a_head_mask", [P, 8]), ("l1a_", "causal", [P, P]),
    ("l2a_", "l2a_q", [P, KD, 2 * D]), ("l2a_", "l2a_k", [P, KD, D]), ("l2a_", "l2a_v", [P, KD, P]),
    ("l2a_", "l2a_o", [P, KD, D]), ("l2a_", "l2a_cos", [P, S]), ("l2a_", "l2a_sin", [P, S]),
    ("l2a_", "l2a_q_b", [P, 2 * KD]), ("l2a_", "l2a_k_b", [P, 2]), ("l2a_", "l2a_v_b", [P, P]),
    ("l2a_", "l2a_o_b", [P, D]), ("l2a_", "l2a_rand", [P, P]), ("l2a_", "l2a_ones", [P, 8]),
    ("l2x_", "l2x_q", [P, P]), ("l2x_", "l2x_k", [P, P]), ("l2x_", "l2x_q_b", [P, 1]), ("l2x_", "l2x_k_b", [P, 1]),
    ("l3a_", "l3a_in", [P, KD, D]), ("l3a_", "l3a_decay", [P, KD, D]), ("l3a_", "l3a_gate", [P, KD, D]),
    ("l3a_", "l3a_out", [P, KD, D]), ("l3a_", "l3a_in_b", [P, KD]), ("l3a_", "l3a_decay_b", [P, KD]),
    ("l3a_", "l3a_decay_b2", [P, KD]), ("l3a_", "l3a_gate_b", [P, KD]), ("l3a_", "l3a_out_b", [P, D]),
    ("l3x_", "l3x_q", [P, KD, 2 * D]), ("l3x_", "l3x_k", [P, 1, 2 * D]), ("l3x_", "l3x_v", [P, 1, D]),
    ("l3x_", "l3x_o", [P, KD, D]), ("l3x_", "l3x_o_b", [P, D]), ("l3x_", "l3x_freq", [2, P]),
    ("l3x_", "l3x_pos", [2, T]), ("l3x_", "l3x_head_mask", [P, 16]),
]
START, STOP = 0, 12


def decoder(nc, dram, out):
    with ExitStack() as ctx:
        m = Machine(nc, ctx, dram)
        weights(m)
        loaded_x = m.sem("loaded_x")
        stored = m.sem("stored")
        with nc.Block(name="load_x") as block:
            @block.sync
            def _(sp):
                sp.dma_start(m.resid[:], dram["x"]).then_inc(loaded_x, 16)
                for group in m.w_loaded:
                    for name in m.w_loaded[group][2]:
                        sp.dma_start(m.w[name][:], dram[name]).then_inc(m.w_loaded[group][0], 16)
                sp.wait_ge(loaded_x, 16)
                if START:
                    m.wait_weights(sp, "consts")

            @block.gpsimd
            def _(pool):
                nc.gpsimd.memset(m.minus_half[:], -0.5)

        stages = [
            lambda n, j: linear_attention(m, n, j),
            lambda n, j: state_space(m, 0, n),
            lambda n, j: experts(m, n, j, "l0f_", routed=16, top=6, rows=88, chunks=2),
            lambda n, j: softmax_attention(m, n, j, "l1a_", heads=16, causal=True),
            lambda n, j: state_space(m, 1, n),
            lambda n, j: mx_feed_forward(m, n, j),
            lambda n, j: feature_attention(m, n, j),
            lambda n, j: context_mixing(m, n, j),
            lambda n, j: experts(m, n, j, "l2f_", routed=8, top=2, rows=88, chunks=2, shared=4, normalize=True),
            lambda n, j: gated_recurrence(m, n, j),
            lambda n, j: softmax_attention(m, n, j, "l3x_", heads=32, causal=False),
            lambda n, j: experts(m, n, j, "l3f_", routed=64, top=4, rows=96, chunks=1, normalize=True, floor=1e-12),
        ]
        first = nc.free_semaphores[0]
        m.first_stage_sem = first
        j = 0
        for n, stage in enumerate(stages[START:STOP]):
            with ExitStack() as scope:
                outer, m.ctx, m.stage_sems = m.ctx, scope, 0
                stage(n, j)
                if START + n not in (1, 4):
                    j += 1
                with nc.Block(name=f"clear{n}") as block:
                    @block.sync
                    def _(sp):
                        sp.sem_clear(range(first, first + m.stage_sems))
                m.ctx, m.stage_sems = outer, None

        with nc.Block(name="store") as block:
            @block.sync
            def _(sp):
                for group in m.w_loaded:
                    m.wait_weights(sp, group)
                sp.dma_start(out, m.resid[:]).then_inc(stored, 16)
                sp.wait_ge(stored, 16)


def rows_to_chunks(a):
    return np.ascontiguousarray(a.reshape(-1, P, a.shape[-1]).transpose(1, 0, 2))


def column(a):
    return np.ascontiguousarray(a.reshape(-1, P).T)


def constants():
    c = {}
    c["ident"] = np.eye(P, dtype=np.float32)
    carry = np.ones((P, T), np.float32)
    carry[:, ::S] = 0
    c["carry"] = carry
    f = np.arange(P)
    c["causal"] = np.where(np.arange(P)[None, :] > np.arange(P)[:, None], np.float32(-1e30), np.float32(0))
    for tag, heads, hd in (("l1a_", 8, 16), ("l3x_", 16, 8)):
        own = f[:, None] // hd == np.arange(heads)[None, :]
        c[tag + "head_mask"] = own.astype(np.float32) * np.float32(hd ** -0.5)
    step = np.arange(S, dtype=np.float32)
    inv = (np.float32(10000.0) ** (-(np.arange(0, 16, 2, dtype=np.float32) / np.float32(16)))).astype(np.float32)
    ang = inv[f % 16 // 2][:, None] * step[None, :]
    c["l1a_cos"] = np.cos(ang)
    c["l1a_sin"] = np.sin(ang) * np.where(f % 2, 1, -1).astype(np.float32)[:, None]
    ang = inv[f % 8][:, None] * step[None, :]
    c["l2a_cos"] = np.cos(ang)
    c["l2a_sin"] = np.sin(ang) * np.where(f % 16 < 8, -1, 1).astype(np.float32)[:, None]
    same = (f[:, None] // 16 == f[None, :] // 16).astype(np.float32)
    c["l2a_ones"] = np.ascontiguousarray(same[:, ::16])
    freq = 10000.0 ** -(np.arange(2) / 2)
    axis, which = f % 8 // 4, f % 4 // 2
    turns = freq[which] / TWO_PI * np.where(f % 2, 1, -1)
    c["l3x_freq"] = np.where(axis[None, :] == np.arange(2)[:, None], turns[None, :], 0).astype(np.float32)
    return c


def layouts(i):
    d = {}
    tok = lambda a: np.ascontiguousarray(a.reshape(TILES, P, -1).transpose(1, 0, 2))
    d["x"] = tok(i["x"])
    d["ctxT"] = np.ascontiguousarray(i["ctx_1024"].reshape(T, CTX).T)
    d["l0_qkv"] = rows_to_chunks(i["L0_attn_W_qkv"].T)
    d["l0_out"] = rows_to_chunks(i["L0_attn_W_out"].T)
    for layer in (0, 1):
        g, s = f"l{layer}s_", f"L{layer}_xattn_"
        d[g + "in"] = np.ascontiguousarray(i[s + "in_proj_w"].T)
        d[g + "conv"] = rows_to_chunks(i[s + "conv_w"].reshape(D, D_CONV))
        d[g + "conv_b"] = column(i[s + "conv_b"])
        d[g + "x"] = rows_to_chunks(i[s + "x_proj_w"].T)
        d[g + "dt"] = np.ascontiguousarray(i[s + "dt_proj_w"].T)
        d[g + "dt_b"] = column(i[s + "dt_proj_b"])
        d[g + "a"] = rows_to_chunks(i[s + "A_log"])
        d[g + "d"] = column(i[s + "D"])
    across = lambda a: np.ascontiguousarray(np.broadcast_to(a[None, :], (P, a.shape[0])))
    pairs = np.arange(D) ^ 1
    halves = np.arange(D) ^ 8
    both = lambda a, order: rows_to_chunks(np.concatenate([a, a[:, order]], axis=1))
    for x in "qk":
        d["l1a_" + x] = both(i["L1_attn_w" + x].T, pairs)
    d["l1a_v"] = rows_to_chunks(i["L1_attn_wv"].T)
    d["l1a_o"] = rows_to_chunks(i["L1_attn_wo"].T)
    for x in "qk":
        b = i["L2_attn_b" + x]
        d["l2a_" + x] = both(i["L2_attn_W" + x].T, halves[:len(b)])
        d[f"l2a_{x}_b"] = column(np.concatenate([b, b[halves[:len(b)]]]))
    d["l2a_v"] = rows_to_chunks(i["L2_attn_Wv"].T)
    d["l2a_v_b"] = across(i["L2_attn_bv"])
    d["l2a_o"] = rows_to_chunks(i["L2_attn_Wo"].T)
    d["l2a_o_b"] = across(i["L2_attn_bo"])
    rand = np.zeros((P, P), np.float32)
    for h in range(8):
        for part in range(2):
            rand[16 * h:16 * h + 16, 16 * h + 8 * part:16 * h + 8 * part + 8] = i["L2_attn_rand_matrix"].T
    d["l2a_rand"] = rand
    for x in "qk":
        d["l2x_" + x] = np.ascontiguousarray(i["L2_xattn_W" + x].T)
        d[f"l2x_{x}_b"] = column(i["L2_xattn_b" + x])
    for x in ("in", "decay", "gate", "out"):
        d["l3a_" + x] = rows_to_chunks(i["L3_attn_W_" + x])
    for x in ("in", "decay", "gate"):
        d[f"l3a_{x}_b"] = column(i["L3_attn_b_" + x])
    d["l3a_decay_b2"] = column(i["L3_attn_decay_bias"])
    d["l3a_out_b"] = across(i["L3_attn_b_out"])
    d["l3x_q"] = both(i["L3_xattn_Wq"], pairs)
    d["l3x_k"] = both(i["L3_xattn_Wkv"][:, :D], pairs)
    d["l3x_v"] = rows_to_chunks(i["L3_xattn_Wkv"][:, D:])
    d["l3x_o"] = rows_to_chunks(i["L3_xattn_Wout"])
    d["l3x_o_b"] = across(i["L3_xattn_bout"])
    d["l3x_pos"] = np.ascontiguousarray(i["fside_BxSx2_0"].reshape(T, 2).T)
    for x in ("gate", "up", "down"):
        d["l1f_" + x] = np.ascontiguousarray(rows_to_chunks(i[f"L1_ffn_{x}_w"]).reshape(P, -1))
    up_rows = lambda a: np.ascontiguousarray(a.reshape(a.shape[0], KD, P, -1).transpose(0, 2, 1, 3)).reshape(
        a.shape[0], P, -1)
    down_rows = lambda a, n: np.ascontiguousarray(a.reshape(a.shape[0], n, -1, D).transpose(0, 2, 1, 3)).reshape(
        a.shape[0], a.shape[1] // n, -1)
    d["l0f_router"] = rows_to_chunks(i["L0_ffn_gate_w"].T)
    d["l0f_w_in"] = up_rows(np.concatenate([i["L0_ffn_w_gate"], i["L0_ffn_w_up"]], axis=1).transpose(0, 2, 1))
    d["l0f_w_down"] = down_rows(i["L0_ffn_w_down"].transpose(0, 2, 1), 2)
    d["l2f_router"] = rows_to_chunks(np.concatenate([i["L2_ffn_gate_w"].T, i["L2_ffn_shared_gate_w"]], axis=1))
    cut = lambda a: a.reshape(D, 4, -1).transpose(1, 0, 2)
    gate = np.concatenate([i["L2_ffn_w_gate"], cut(i["L2_ffn_sw_gate"])])
    up = np.concatenate([i["L2_ffn_w_up"], cut(i["L2_ffn_sw_up"])])
    d["l2f_w_in"] = up_rows(np.concatenate([gate, up], axis=2))
    d["l2f_w_down"] = down_rows(np.concatenate([i["L2_ffn_w_down"], i["L2_ffn_sw_down"].reshape(4, -1, D)]), 2)
    d["l3f_router"] = rows_to_chunks(i["L3_ffn_gate_weight"].T)
    d["l3f_w_in"] = up_rows(i["L3_ffn_gate_up_proj"].transpose(0, 2, 1))
    d["l3f_w_down"] = down_rows(i["L3_ffn_down_proj"].transpose(0, 2, 1), 1)
    return d


def kernel(**inputs):
    import concourse.bacc as bacc
    from concourse.bass_utils import run_bass_kernel_spmd

    arrays = {**constants(), **layouts({k: np.asarray(v) for k, v in inputs.items()})}
    nc = bacc.Bacc("TRN2", target_bir_lowering=False, num_devices=1)
    dram = {n: nc.dram_tensor("in_" + n, a.shape, mybir.dt.from_np(a.dtype), kind="ExternalInput").ap()
            for n, a in arrays.items()}
    out = nc.dram_tensor("out_0", (P, TILES, D), F32, kind="ExternalOutput").ap()
    decoder(nc, dram, out)
    r = run_bass_kernel_spmd(nc, [{"in_" + n: a for n, a in arrays.items()}], core_ids=[0])
    y = r.results[0]["out_0"]
    return np.ascontiguousarray(y.transpose(1, 0, 2)).reshape(B, S, D)
```

```python
from contextlib import ExitStack

import numpy as np

import concourse.bass as bass
from concourse import mybir

F32 = mybir.dt.float32
I32 = mybir.dt.int32
U32 = mybir.dt.uint32
ALU = mybir.AluOpType
ACT = mybir.ActivationFunctionType
AX_X = mybir.AxisListType.X

P = 128
B, S, D = 4, 256, 256
CTX = 128
T = B * S
TILES = T // P
KD = D // P
HALF = T // 2
PAIR = 1024
NORMS = 12
EPS = 1e-5
TWO_PI = 2.0 * np.pi
SIN_SCALE = float(np.float32(TWO_PI * (1 - 2e-7)))
ROUND = 1.5 * 2.0 ** 23
N_STATE, D_CONV, DT_RANK = 16, 4, 8
X_DBL = DT_RANK + 2 * N_STATE
MX_BLOCK, FP8_MAX = 32, 448.0


STAGE_SEMS = 64


class Order:

    def __init__(self, sem):
        self.sem, self.made, self.turn = sem, 0, None

    def mark(self, ins):
        self.made += 1
        ins.then_inc(self.sem, 1)

    def wait(self, eng):
        eng.wait_ge(self.sem, self.made if self.turn is None else self.turn + self.made)

    def link(self, eng, ins):
        self.mark(ins)
        self.wait(eng)


class Machine:

    def __init__(self, nc, ctx, dram):
        self.nc, self.ctx, self.dram = nc, ctx, dram
        self.stage_sems = None
        self.resid = self.sb("resid", [P, TILES, D])
        self.h = self.sb("h", [P, TILES, D])
        self.hT = self.sb("hT", [P, KD, T])
        self.stats = self.sb("stats", [P, TILES, 6])
        self.moments = self.sb("moments", [P, TILES, 2])
        self.rstd = self.sb("rstd", [P, 2, TILES])
        self.minus_half = self.sb("minus_half", [P, TILES])
        self.psum = ctx.enter_context(nc.psum_tensor("psum", [P, 4 * PAIR], F32))
        self.w = {}
        self.w_loaded = {}
        self.moments_ready = self.sem("moments_ready")
        self.rstd_ready = self.sem("rstd_ready")
        self.h_ready = self.sem("h_ready")
        self.turned = self.sem("turned")
        self.hT_ready = self.sem("hT_ready")
        self.dve_order = Order(self.sem("dve_order"))
        self.act_order = Order(self.sem("act_order"))
        self.pool_order = Order(self.sem("pool_order"))
        self.norm = -1

    def sb(self, name, shape, dt=F32):
        return self.ctx.enter_context(self.nc.sbuf_tensor(name, shape, dt))

    def sem(self, name):
        if self.stage_sems is None:
            return self.ctx.enter_context(self.nc.semaphore(name))
        self.stage_sems += 1
        assert self.stage_sems <= STAGE_SEMS
        return self.ctx.enter_context(self.nc.semaphore(name, num=self.first_stage_sem + self.stage_sems - 1))

    def pair(self, i, rows=P):
        return self.psum[0:rows, i * PAIR:(i + 1) * PAIR]

    def weight(self, group, name, shape):
        self.w[name] = self.sb("w_" + name, shape)
        if group not in self.w_loaded:
            self.w_loaded[group] = [self.sem("loaded_" + group), 0, []]
        self.w_loaded[group][1] += 16
        self.w_loaded[group][2].append(name)

    def load_weights(self, eng, groups):
        for group in groups:
            for name in self.w_loaded[group][2]:
                eng.dma_start(self.w[name][:], self.dram[name]).then_inc(self.w_loaded[group][0], 16)

    def wait_weights(self, eng, group):
        eng.wait_ge(self.w_loaded[group][0], self.w_loaded[group][1])



def norm_vector(m, dve, n):
    nc, o = m.nc, m.dve_order
    for t in range(TILES):
        o.mark(nc.vector.bn_stats(m.stats[:, t, :], m.resid[:, t, :]))
    for t in range(TILES):
        dve.wait_ge(o.sem, o.made - TILES + 1 + t)
        ins = nc.vector.bn_aggr(m.moments[:, t, :], m.stats[:, t, :])
    ins.then_inc(m.moments_ready, 1)
    dve.wait_ge(m.rstd_ready, n + 1)
    for t in range(TILES):
        nc.vector.tensor_scalar(m.h[:, t, :], m.resid[:, t, :], m.moments[:, t, 0:1], m.rstd[:, 1, t:t + 1],
                                ALU.subtract, ALU.mult).then_inc(m.h_ready, 1)


def norm_gpsimd(m, pool, n):
    nc = m.nc
    pool.wait_ge(m.moments_ready, n + 1)
    m.pool_order.link(pool, nc.gpsimd.tensor_scalar(m.rstd[:, 0, :], m.moments[:, :, 1], EPS, None, ALU.add))
    nc.gpsimd.tensor_tensor(m.rstd[:, 1, :], m.rstd[:, 0, :], m.minus_half[:], ALU.pow).then_inc(m.rstd_ready, 1)


def norm_tensor(m, pe, n):
    nc = m.nc
    for t in range(TILES):
        pe.wait_ge(m.h_ready, TILES * n + t + 1)
        for k in range(KD):
            at = k * PAIR + t * P
            ins = nc.tensor.transpose(m.psum[:, at:at + P], m.h[:, t, k * P:(k + 1) * P], m.ident[:])
        if t % 4 == 3:
            ins.then_inc(m.turned, 1)


def norm_scalar(m, act, j):
    nc = m.nc
    for half in range(2):
        act.wait_ge(m.turned, 2 * j + half + 1)
        for k in range(KD):
            cols = slice(half * HALF, (half + 1) * HALF)
            nc.scalar.activation(m.hT[:, k, cols], m.pair(k)[:, cols], ACT.Copy).then_inc(m.hT_ready, 1)


def wait_hT(m, eng, j, half=1):
    eng.wait_ge(m.hT_ready, 4 * j + 2 * (half + 1))


class Jobs:

    def __init__(self, m, label, first, jobs):
        self.m, self.first = m, first
        self.names = [n for n, _ in jobs]
        self.takers = [k for _, k in jobs]
        self.filled = m.sem(label + "_filled")
        self.emptied = {k: m.sem(label + "_emptied_" + k) for k in sorted(set(self.takers))}

    def at(self, name):
        return self.names.index(name)

    def pair(self, name, rows=P):
        return self.m.pair((self.first + self.at(name)) % 4, rows)

    def wait_room(self, eng, name):
        i = self.at(name) - 4
        if i >= 0:
            k = self.takers[i]
            eng.wait_ge(self.emptied[k], self.takers[:i + 1].count(k))

    def wait_filled(self, eng, name):
        eng.wait_ge(self.filled, self.at(name) + 1)

    def empty(self, name):
        return self.emptied[self.takers[self.at(name)]]


def project(m, pe, jobs, name, w, rhs, chunks, rows=P):
    nc = m.nc
    jobs.wait_room(pe, name)
    out = jobs.pair(name, rows)
    for half in range(2):
        cols = slice(half * HALF, (half + 1) * HALF)
        for k in range(chunks):
            ins = nc.tensor.matmul(out[:, cols], lhsT=w(k), rhs=rhs(k, cols), start=(k == 0), stop=(k == chunks - 1))
    ins.then_inc(jobs.filled, 1)


def project_tokens(m, pe, jobs, names, lhs, rhs, chunks):
    nc = m.nc
    for q, name in enumerate(names):
        jobs.wait_room(pe, name)
        out = jobs.pair(name)
        for j in range(4):
            t = 4 * q + j
            for k in range(chunks):
                ins = nc.tensor.matmul(out[:, j * D:(j + 1) * D], lhsT=lhs(k, t), rhs=rhs(k, t),
                                       start=(k == 0), stop=(k == chunks - 1))
        ins.then_inc(jobs.filled, 1)


def add_tokens(m, dve, jobs, names, scale=1.0, bias=None):
    nc = m.nc
    for q, name in enumerate(names):
        jobs.wait_filled(dve, name)
        r = m.resid[:, 4 * q:4 * q + 4, :]
        ps = jobs.pair(name).rearrange("p (t d) -> p t d", d=D)
        if bias is not None:
            m.dve_order.link(dve, nc.vector.tensor_tensor(r, r, bias.unsqueeze(1).to_broadcast([P, 4, D]), ALU.add))
        nc.vector.scalar_tensor_tensor(out=r, in0=ps, scalar=scale, in1=r, op0=ALU.mult,
                                       op1=ALU.add).then_inc(jobs.empty(name), 1)


def wcols(w, c):
    return lambda k: w[:, k, c * P:(c + 1) * P]


def feature_rhs(x):
    return lambda k, cols: x[:, k, cols]



def linear_attention(m, n, j):
    nc = m.nc
    w = m.w["l0_qkv"]
    jobs = Jobs(m, "l0a", 2, [(x + str(c), "vector" if x == "v" else "scalar") for c in range(KD) for x in "qkv"]
                + [("out0", "vector"), ("out1", "vector")])
    e = [m.sb(f"l0_exp{i}", [P, T]) for i in range(2)]
    r = [m.sb(f"l0_relu{i}", [P, T]) for i in range(2)]
    sums = [m.sb(f"l0_sum{i}", [P, T]) for i in range(2)]
    att = m.sb("l0_att", [P, KD, T])
    phi_in = m.sem("l0_phi_in")
    chunk_done = m.sem("l0_chunk_done")
    with nc.Block(name="l0_attn") as block:
        @block.sync
        def _(sp):
            m.load_weights(sp, [g for g in m.w_loaded if g not in FIRST_WEIGHTS])

        @block.gpsimd
        def _(pool):
            norm_gpsimd(m, pool, n)

        @block.tensor
        def _(pe):
            m.wait_weights(pe, "consts")
            norm_tensor(m, pe, n)
            wait_hT(m, pe, j)
            m.wait_weights(pe, "l0_attn")
            for c in range(KD):
                for i, x in enumerate("qkv"):
                    project(m, pe, jobs, x + str(c), wcols(w, KD * i + c), feature_rhs(m.hT), KD)
            pe.wait_ge(chunk_done, KD)
            project_tokens(m, pe, jobs, ("out0", "out1"), lambda k, t: att[:, k, t * P:(t + 1) * P],
                           lambda k, t: m.w["l0_out"][:, k, :], KD)

        @block.scalar
        def _(act):
            norm_scalar(m, act, j)
            for c in range(KD):
                for i, x in enumerate("qk"):
                    name = x + str(c)
                    jobs.wait_filled(act, name)
                    if c:
                        act.wait_ge(chunk_done, c)
                    nc.scalar.activation(e[i][:], jobs.pair(name), ACT.Exp).then_inc(phi_in, 1)
                    nc.scalar.activation(r[i][:], jobs.pair(name), ACT.Relu).then_inc(jobs.empty(name), 1)

        @block.vector
        def _(dve):
            o = m.dve_order
            norm_vector(m, dve, n)
            m.wait_weights(dve, "consts")
            for c in range(KD):
                dve.wait_ge(jobs.emptied["scalar"], 2 * c + 2)
                for i in range(2):
                    o.mark(nc.vector.scalar_tensor_tensor(out=e[i][:], in0=e[i][:], scalar=1.0, in1=r[i][:],
                                                          op0=ALU.min, op1=ALU.add))
                o.wait(dve)
                name = "v" + str(c)
                jobs.wait_filled(dve, name)
                ins = nc.vector.tensor_tensor(r[1][:], e[1][:], jobs.pair(name), ALU.mult)
                ins.then_inc(jobs.empty(name), 1)
                dve.wait_ge(jobs.empty(name), c + 1)
                o.mark(nc.vector.tensor_tensor_scan(sums[0][:], m.w["carry"][:], r[1][:], 0.0, ALU.mult, ALU.add))
                o.mark(nc.vector.tensor_tensor_scan(sums[1][:], m.w["carry"][:], e[1][:], 0.0, ALU.mult, ALU.add))
                o.wait(dve)
                for i in range(2):
                    o.mark(nc.vector.tensor_tensor(sums[i][:], e[0][:], sums[i][:], ALU.mult))
                o.wait(dve)
                o.link(dve, nc.vector.tensor_scalar(sums[1][:], sums[1][:], 1e-9, None, ALU.add))
                o.link(dve, nc.vector.reciprocal(sums[1][:], sums[1][:]))
                nc.vector.tensor_tensor(att[:, c, :], sums[0][:], sums[1][:], ALU.mult).then_inc(chunk_done, 1)
            add_tokens(m, dve, jobs, ("out0", "out1"), scale=16 ** -0.5)



def state_space(m, layer, n):
    nc = m.nc
    g = f"l{layer}s_"
    w = {k: m.w[g + k] for k in ("in", "conv", "conv_b", "x", "dt", "dt_b", "a", "d")}
    xpad = m.sb(g + "xpad", [P, KD, B, D_CONV - 1 + S])
    conv = m.sb(g + "conv_out", [P, KD, T])
    u = m.sb(g + "u", [P, KD, T])
    xdbl = m.sb(g + "xdbl", [X_DBL, T])
    t_abs = m.sb(g + "t_abs", [P, KD, T])
    t_sq = m.sb(g + "t_sq", [P, KD, T])
    relu = m.sb(g + "relu", [P, KD, T])
    du = m.sb(g + "du", [P, KD, T])
    two = m.sb(g + "two", [P, 1])
    skip = m.hT
    gate = m.sb(g + "gate", [P, TILES, S])
    decay = [t_sq[:, i, :] for i in range(2)]
    drive = [xpad[:, i, :, :].rearrange("p b s -> p (b s)")[:, 0:T] for i in range(2)]
    state = [relu[:, i, :] for i in range(2)]
    read = [conv[:, i, :] for i in range(2)]
    SLOTS = 4
    bc = [m.sb(g + f"bc{i}", [P, 2, T]) for i in range(SLOTS)]
    scratch = nc.dram_tensor(g + "scratch", (X_DBL, T), F32).ap()
    delta = t_abs
    (x_filled, pads, x_out, conv_done, u_ready, xdbl_filled, xdbl_ready, stored, dt_filled, act_dt, delta_ready,
     du_ready, gate_ready, decay_ready, drive_ready, scanned, read_ready, summed, product, turned,
     skip_ready, ratio_ready) = (m.sem(g + s) for s in (
         "x_filled", "pads", "x_out", "conv_done", "u_ready", "xdbl_filled", "xdbl_ready", "stored", "dt_filled",
         "act_dt", "delta_ready", "du_ready", "gate_ready", "decay_ready", "drive_ready", "scanned", "read_ready",
         "summed", "product", "turned", "skip_ready", "ratio_ready"))
    bc_in = [m.sem(g + f"bc_in{i}") for i in range(SLOTS)]
    GROUPS = N_STATE // SLOTS

    with nc.Block(name=g + "block") as block:
        @block.sync
        def _(sp):
            sp.wait_ge(xdbl_ready, 1)
            sp.dma_start(scratch, xdbl[:]).then_inc(stored, 16)
            sp.wait_ge(stored, 16)
            rows = scratch[DT_RANK:X_DBL, :].rearrange("(a n) t -> n a t", n=N_STATE)
            for s in range(SLOTS):
                sp.dma_start(bc[s][:], rows[s].partition_broadcast(P)).then_inc(bc_in[s], 16)
            with sp.Fori(1, GROUPS) as i:
                for s in range(SLOTS):
                    sp.wait_ge(read_ready, (i * SLOTS + s - SLOTS + 1) * KD)
                    src = rows[bass.ds(i * SLOTS + s, 1)].rearrange("o a t -> (o a) t")
                    sp.dma_start(bc[s][:], src.partition_broadcast(P)).then_inc(bc_in[s], 16)

        @block.gpsimd
        def _(pool):
            o = m.pool_order
            nc.gpsimd.memset(two[:], 2.0)
            nc.gpsimd.memset(xpad[:], 0.0).then_inc(pads, 1)
            norm_gpsimd(m, pool, n)
            pool.wait_ge(u_ready, KD)
            for c in range(KD):
                pool.wait_ge(delta_ready, c + 1)
                o.mark(nc.gpsimd.tensor_tensor(du[:, c, :], delta[:, c, :], u[:, c, :], ALU.mult))
            o.wait(pool)
            for c in range(KD):
                first = delta[:, c, :].rearrange("p (b s) -> p b s", s=S)[:, :, 0:1]
                ins = nc.gpsimd.memset(first, 1e25)
            ins.then_inc(du_ready, 1)

            def group(i, q0):
                for s in range(SLOTS):
                    pool.wait_ge(bc_in[s], (i + 1) * 16)
                    for c in range(KD):
                        pool.wait_ge(scanned, q0 + s * KD + c + 1)
                        nc.gpsimd.tensor_tensor(drive[c], du[:, c, :], bc[s][:, 0, :],
                                                ALU.mult).then_inc(drive_ready, 1)
            with pool.Fori(0, GROUPS) as i:
                group(i, i * (SLOTS * KD))

        @block.tensor
        def _(pe):
            m.wait_weights(pe, g)
            for c in range(KD):
                for half in range(2):
                    cols = slice(half * HALF, (half + 1) * HALF)
                    ins = nc.tensor.matmul(m.pair(c)[:, cols], lhsT=w["in"][:, c * P:(c + 1) * P], rhs=m.ctxT[:, cols],
                                           start=True, stop=True)
                ins.then_inc(x_filled, 1)
            pe.wait_ge(u_ready, KD)
            for half in range(2):
                cols = slice(half * HALF, (half + 1) * HALF)
                for k in range(KD):
                    ins = nc.tensor.matmul(m.pair(2, X_DBL)[:, cols], lhsT=w["x"][:, k, :], rhs=u[:, k, cols],
                                           start=(k == 0), stop=(k == KD - 1))
            ins.then_inc(xdbl_filled, 1)
            pe.wait_ge(xdbl_ready, 1)
            for c in range(KD):
                for half in range(2):
                    cols = slice(half * HALF, (half + 1) * HALF)
                    ins = nc.tensor.matmul(m.pair(c)[:, cols], lhsT=w["dt"][:, c * P:(c + 1) * P],
                                           rhs=xdbl[0:DT_RANK, cols], start=True, stop=True)
                ins.then_inc(dt_filled, 1)
            pe.wait_ge(skip_ready, KD)

            def add(c, rhs, start, stop):
                for half in range(2):
                    cols = slice(half * HALF, (half + 1) * HALF)
                    ins = nc.tensor.matmul(m.pair(2 + c)[:, cols], lhsT=m.ident[:], rhs=rhs[:, cols], start=start,
                                           stop=stop, skip_group_check=True)
                return ins

            for c in range(KD):
                add(c, skip[:, c, :], True, False)

            def group(q0, last):
                for s in range(SLOTS):
                    for c in range(KD):
                        pe.wait_ge(read_ready, q0 + s * KD + c + 1)
                        add(c, read[c], False, last and s == SLOTS - 1).then_inc(summed, 1)
            with pe.Fori(0, GROUPS - 1) as i:
                group(i * (SLOTS * KD), False)
            group((GROUPS - 1) * SLOTS * KD, True)
            pe.wait_ge(product, KD)
            for q in range(2):
                for b in range(2 * q, 2 * q + 2):
                    for lh in range(2):
                        for c in range(KD):
                            at = q * PAIR + (2 * (b % 2) + lh) * D + c * P
                            src = conv[:, c, b * S + lh * P:b * S + (lh + 1) * P]
                            ins = nc.tensor.transpose(m.psum[:, at:at + P], src, m.ident[:])
                ins.then_inc(turned, 1)

        @block.scalar
        def _(act):
            act.wait_ge(pads, 1)
            for c in range(KD):
                act.wait_ge(x_filled, c + 1)
                nc.scalar.activation(xpad[:, c, :, D_CONV - 1:], m.pair(c).rearrange("p (b s) -> p b s", s=S),
                                     ACT.Copy).then_inc(x_out, 1)
            for c in range(KD):
                act.wait_ge(conv_done, c + 1)
                nc.scalar.activation(u[:, c, :], conv[:, c, :], ACT.Silu, bias=w["conv_b"][:, c:c + 1]).then_inc(u_ready, 1)
            act.wait_ge(u_ready, KD)
            for c in range(KD):
                nc.scalar.activation(skip[:, c, :], u[:, c, :], ACT.Copy, scale=w["d"][:, c:c + 1]).then_inc(skip_ready, 1)
            act.wait_ge(xdbl_filled, 1)
            nc.scalar.activation(xdbl[:], m.pair(2, X_DBL), ACT.Copy).then_inc(xdbl_ready, 1)
            for c in range(KD):
                act.wait_ge(dt_filled, c + 1)
                m.act_order.link(act, nc.scalar.activation(t_abs[:, c, :], m.pair(c), ACT.Abs, bias=w["dt_b"][:, c:c + 1]))
                nc.scalar.activation(relu[:, c, :], m.pair(c), ACT.Relu, bias=w["dt_b"][:, c:c + 1])
                m.act_order.link(act, nc.scalar.activation(t_abs[:, c, :], t_abs[:, c, :], ACT.Exp, scale=-1.0))
            for c in range(KD):
                m.act_order.mark(nc.scalar.activation(t_sq[:, c, :], t_abs[:, c, :], ACT.Ln, bias=two[:]))
            m.act_order.wait(act)
            for c in range(KD):
                nc.scalar.activation(t_sq[:, c, :], t_sq[:, c, :], ACT.Exp, scale=-1.0).then_inc(act_dt, 1)
            act.wait_ge(m.h_ready, TILES * (n + 1))
            nc.scalar.activation(gate[:], m.h[:], ACT.Silu).then_inc(gate_ready, 1)
            m.act_order.link(act, nc.scalar.activation(w["a"][:], w["a"][:], ACT.Exp))
            m.act_order.link(act, nc.scalar.mul(w["a"][:], w["a"][:], -1.0))
            act.wait_ge(du_ready, 1)
            with act.Fori(0, GROUPS) as i:
                for s in range(SLOTS):
                    for c in range(KD):
                        act.wait_ge(scanned, i * (SLOTS * KD) + s * KD + c + 1)
                        at = i * SLOTS + s
                        nc.scalar.activation(decay[c], delta[:, c, :], ACT.Exp,
                                             scale=w["a"][:, c, bass.ds(at, 1)]).then_inc(decay_ready, 1)

        @block.vector
        def _(dve):
            o = m.dve_order
            dve.sem_inc(scanned, KD)
            m.wait_weights(dve, g)
            for c in range(KD):
                dve.wait_ge(x_out, c + 1)
                out = conv[:, c, :].rearrange("p (b s) -> p b s", s=S)
                o.link(dve, nc.vector.tensor_scalar(out, xpad[:, c, :, 0:S], w["conv"][:, c, 0:1], None, ALU.mult))
                for k in range(1, D_CONV):
                    ins = nc.vector.scalar_tensor_tensor(out=out, in0=xpad[:, c, :, k:k + S], scalar=w["conv"][:, c, k:k + 1],
                                                         in1=out, op0=ALU.mult, op1=ALU.add)
                    if k < D_CONV - 1:
                        o.link(dve, ins)
                ins.then_inc(conv_done, 1)
            norm_vector(m, dve, n)
            for c in range(KD):
                dve.wait_ge(act_dt, c + 1)
                softplus_ratio(m, dve, c, t_abs[:, c, :], t_sq[:, c, :], ratio_ready)
                softplus_tail(dve, nc.vector, o, t_abs[:, c, :], t_sq[:, c, :], conv[:, c, :], relu[:, c, :],
                              delta[:, c, :], delta_ready)

            def unit(q, c, s, i):
                dve.wait_ge(decay_ready, q + 1)
                dve.wait_ge(drive_ready, q + 1)
                nc.vector.tensor_tensor_scan(state[c], decay[c], drive[c], 0.0, ALU.mult,
                                             ALU.add).then_inc(scanned, 1)
                dve.wait_ge(scanned, q + 1 + KD)
                dve.wait_ge(summed, q + 1)
                nc.vector.tensor_tensor(read[c], state[c], bc[s][:, 1, :], ALU.mult).then_inc(read_ready, 1)

            dve.sem_inc(summed, KD)
            with dve.Fori(0, GROUPS) as i:
                for s in range(SLOTS):
                    for c in range(KD):
                        unit(i * (SLOTS * KD) + s * KD + c, c, s, i)
            dve.wait_ge(summed, KD + N_STATE * KD)
            dve.wait_ge(gate_ready, 1)
            for c in range(KD):
                y = m.pair(2 + c).rearrange("p (b s) -> p b s", s=S)
                z = gate[:].rearrange("p (b c) s -> p b c s", c=KD)[:, :, c, :]
                nc.vector.tensor_tensor(conv[:, c, :].rearrange("p (b s) -> p b s", s=S), y, z,
                                        ALU.mult).then_inc(product, 1)
            for q in range(2):
                dve.wait_ge(turned, q + 1)
                r = m.resid[:, 4 * q:4 * q + 4, :]
                o.link(dve, nc.vector.tensor_tensor(r, m.pair(q).rearrange("p (t d) -> p t d", d=D), r, ALU.add))


def softplus_ratio(m, dve, c, e, q, ratio_ready):
    nc, o = m.nc, m.dve_order
    nc.vector.tensor_tensor(e, e, q, ALU.mult).then_inc(ratio_ready, 1)
    dve.wait_ge(ratio_ready, c + 1)


def softplus_tail(dve, ops, o, s, sq, p, relu, delta, delta_ready):
    def times(p, scalar, by, op0, op1, out=None):
        return ops.scalar_tensor_tensor(out=p if out is None else out, in0=p, scalar=scalar, in1=by, op0=op0, op1=op1)

    o.link(dve, ops.tensor_tensor(sq, s, s, ALU.mult))
    o.link(dve, ops.tensor_scalar(p, sq, 1 / 11, None, ALU.mult))
    for odd in (9, 7, 5, 3):
        o.link(dve, times(p, 1 / odd, sq, ALU.add, ALU.mult))
    o.link(dve, times(p, 1.0, s, ALU.add, ALU.mult))
    times(p, 2.0, relu, ALU.mult, ALU.add, out=delta).then_inc(delta_ready, 1)



GROUP = 4


def by_steps(eng, groups, step, lag):
    for s in range(GROUP):
        step(0, s, True, False)
    with eng.Fori(1, groups) as i:
        for s in range(GROUP):
            step(i * GROUP, s, False, False)
    for s in range(lag):
        step(groups * GROUP, s, False, True)


def experts(m, n, j, tag, routed, top, rows, chunks, shared=0, normalize=False, floor=None):
    nc = m.nc
    E = routed + shared
    R = routed + (1 if shared else 0)
    K = top + shared
    F = rows * chunks
    PAD = 8 - top
    BLOCKS = -(-((K * T + E * (P - 1)) // P) // GROUP) * GROUP
    GROUPS = BLOCKS // GROUP
    FEWEST = K * T // P // GROUP
    GONE = -2.0
    sb, sem = m.sb, lambda s: m.sem(tag + s)
    router, iota, token = m.w[tag + "router"], m.w["iota"], m.w["token"]
    ring = lambda name, shape, count: [sb(tag + f"{name}{i}", shape) for i in range(count)]
    combine = sb(tag + "combine", [P, TILES, E])
    probs = sb(tag + "probs", [P, TILES, routed + PAD])
    rest = sb(tag + "rest", [P, TILES, routed + PAD])
    best = sb(tag + "best", [P, TILES, 8])
    row = sb(tag + "row", [P, TILES])
    goes = sb(tag + "goes", [P, TILES, E])
    before = sb(tag + "before", [P, TILES + 1, E])
    number = sb(tag + "number", [P, TILES, E])
    slots = sb(tag + "slots", [P, TILES, E])
    picked = sb(tag + "picked", [P, TILES, E])
    over = sb(tag + "over", [P, E, TILES])
    blocks, ends, starts = (sb(tag + s, [P, E]) for s in ("blocks", "ends", "starts"))
    limits = sb(tag + "limits", [P, TILES])
    earlier = sb(tag + "earlier", [P, TILES])
    turns = sb(tag + "turns", [P, GROUPS])
    slot, weight, block_of, lane_of = (sb(tag + s, [P, K, TILES]) for s in ("slot", "weight", "block_of", "lane_of"))
    slot_index = sb(tag + "slot_index", [P, K, TILES], U32)
    owner, groups_f = sb(tag + "owner", [P, 1]), sb(tag + "groups_f", [P, 1])
    owners_diag = sb(tag + "owners_diag", [P, P])
    owners = sb(tag + "owners", [1, P], I32)
    more_turns = sb(tag + "more_turns", [1, 2], I32)
    lane_hot = ring("lane_hot", [P, TILES, P], 2)
    block_hot = ring("block_hot", [P, TILES, BLOCKS], 2)
    token_of = sb(tag + "token_of", [P, BLOCKS], U32)
    token_now = sb(tag + "token_now", [P, GROUP], U32)
    x = ring("x", [P, D], GROUP)
    xT = ring("xT", [P, KD, P], 2)
    w_in = ring("w_in", [P, KD, 2 * F], GROUP)
    w_down = ring("w_down", [rows, chunks, D], GROUP)
    silu = ring("silu", [P, F], 2)
    gated = ring("gated", [P, F], 2)
    gatedT = ring("gatedT", [rows, chunks, P], 2)
    y = ring("y", [P, D], GROUP)
    back = ring("back", [P, D], TILES)
    h_rows = nc.dram_tensor(tag + "h_rows", (T, D), F32).ap()
    y_rows = nc.dram_tensor(tag + "y_rows", ((BLOCKS + GROUP) * P, D), F32).ap()
    y_groups = y_rows.rearrange("(g b p) d -> g b p d", b=GROUP, p=P)

    bank = lambda i: m.psum[:, i * 512:(i + 1) * 512]
    logits = bank(4)[:, 0:TILES * R].rearrange("p (t e) -> p t e", e=R)
    rank = bank(5)[:, 0:TILES * E]
    counts = bank(6)[:, 0:E]
    owner_row = bank(7)[:, 0:P]
    table = bank(4)[:, 0:BLOCKS]
    xT_ps = [bank(i)[:, 0:D].rearrange("p (k t) -> p k t", t=P) for i in (0, 1)]
    in_ps = [bank(i)[:, 0:2 * F] for i in (2, 3)]
    gT_ps = [bank(i)[0:rows, 0:chunks * P].rearrange("p (c t) -> p c t", t=P) for i in (4, 5)]
    y_ps = [bank(i)[:, 0:D] for i in (6, 7)]

    (routed_ready, less_max, exps, shared_ready, goes_ready, counted, owner_ready, owners_filled, lists_ready,
     lanes_ready, blocks_ready, tokens_ready, tabled, table_ready, h_stored, token_ready, x_turned, xT_ready,
     in_done, silu_done, gate_done, g_turned, gT_ready, down_done, y_ready, filled, all_filled, may_gather,
     accumulated) = (
        sem(s) for s in ("logits", "less_max", "exps", "shared", "goes", "counted", "owner", "owners_filled",
                         "lists", "lanes", "blocks_of", "tokens", "tabled", "table", "h_stored", "token", "x_turned",
                         "xT", "in_done", "silu", "gate", "g_turned", "gT", "down_done", "y", "filled",
                         "all_filled", "may_gather", "accumulated"))
    in_loaded, down_loaded, y_stored = (
        [sem(f"{s}{i}") for i in range(GROUP)] for s in ("in_loaded", "down_loaded", "y_stored"))
    x_loaded, back_loaded = m.gather_sems[tag]

    def group_count(eng):
        eng.wait_ge(lists_ready, 2)
        return eng.value_load(more_turns[0:1, 0:1], min_val=0, max_val=GROUPS - FEWEST) + FEWEST

    with nc.Block(name=tag + "block") as block:
        @block.sync
        def _(sp):
            sp.wait_ge(m.h_ready, TILES * (n + 1))
            sp.dma_start(h_rows.rearrange("(t p) d -> p t d", p=P), m.h[:]).then_inc(h_stored, 16)
            groups = group_count(sp)

            def step(base, s, first, last):
                e = sp.value_load(owners[0:1, bass.ds(base + s, 1)], min_val=0, max_val=E - 1)
                for w, name, used, loaded in ((w_in, "w_in", in_done, in_loaded), (w_down, "w_down", down_done, down_loaded)):
                    if not first:
                        sp.wait_ge(used, base + (s - GROUP + 1))
                    src = m.dram[tag + name][bass.ds(e, 1)].rearrange("o p x -> (o p) x")
                    sp.dma_start(w[s][:].rearrange("p c x -> p (c x)"), src).then_inc(loaded[s], 16)
            by_steps(sp, groups, step, 0)

        @block.gpsimd
        def _(pool):
            norm_gpsimd(m, pool, n)
            m.wait_weights(pool, "routing")
            for c in range(K):
                pool.wait_ge(blocks_ready, c + 1)
                nc.gpsimd.tensor_tensor(block_hot[c % 2][:], block_hot[c % 2][:],
                                        token[:].unsqueeze(2).to_broadcast([P, TILES, BLOCKS]),
                                        ALU.mult).then_inc(tokens_ready, 1)
            groups = group_count(pool)
            pool.wait_ge(table_ready, 1)
            pool.wait_ge(h_stored, 16)

            def step(base, s, first, last):
                if s == 0:
                    if not first:
                        for k in range(GROUP):
                            pool.wait_ge(x_loaded[k], base * (16 // GROUP))
                    nc.gpsimd.tensor_copy(token_now[:], token_of[:, bass.ds(base, GROUP)]).then_inc(token_ready, GROUP)
                    pool.wait_ge(token_ready, base + GROUP)
                if not first:
                    pool.wait_ge(x_turned, base + (s - GROUP + 1))
                    pool.sem_inc(may_gather, 1)
                nc.gpsimd.indirect_dma_start(
                    x[s][:], None, h_rows, bass.IndirectOffsetOnAxis(ap=token_now[:, s:s + 1], axis=0)).then_inc(
                        x_loaded[s], 16)
            by_steps(pool, groups, step, 0)
            for s in range(GROUP):
                pool.wait_ge(y_stored[s], groups * 16 + 16)
            pool.sem_inc(may_gather, 1)
            pool.wait_ge(all_filled, 1)
            for q in range(K * TILES):
                c, t = divmod(q, TILES)
                if c:
                    pool.wait_ge(accumulated, q - TILES + 1)
                nc.gpsimd.indirect_dma_start(
                    back[t][:], None, y_rows, bass.IndirectOffsetOnAxis(ap=slot_index[:, c, t:t + 1], axis=0)).then_inc(
                        back_loaded[t], 16)

        @block.tensor
        def _(pe):
            norm_tensor(m, pe, n)
            wait_hT(m, pe, j)
            m.wait_weights(pe, tag)
            for t in range(TILES):
                for k in range(KD):
                    ins = nc.tensor.matmul(logits[:, t, :], lhsT=m.hT[:, k, t * P:(t + 1) * P], rhs=router[:, k, :],
                                           start=(k == 0), stop=(k == KD - 1))
            ins.then_inc(routed_ready, 1)
            m.wait_weights(pe, "routing")
            pe.wait_ge(goes_ready, 1)
            nc.tensor.matmul(rank, lhsT=m.w["earlier"][:], rhs=goes[:].rearrange("p t e -> p (t e)"),
                             start=True, stop=False)
            nc.tensor.matmul(rank, lhsT=m.w["ones"][:], rhs=before[:, 0:TILES, :].rearrange("p t e -> p (t e)"),
                             start=False, stop=True)
            nc.tensor.matmul(counts, lhsT=m.w["ones"][:], rhs=before[:, TILES, :], start=True,
                             stop=True).then_inc(counted, 1)
            pe.wait_ge(owner_ready, 1)
            nc.tensor.matmul(owner_row, lhsT=m.w["ones"][:], rhs=owners_diag[:], start=True,
                             stop=True).then_inc(owners_filled, 1)
            for c in range(K):
                pe.wait_ge(lanes_ready, c + 1)
                pe.wait_ge(tokens_ready, c + 1)
                for t in range(TILES):
                    ins = nc.tensor.matmul(table, lhsT=lane_hot[c % 2][:, t, :], rhs=block_hot[c % 2][:, t, :],
                                           start=(c + t == 0), stop=(c == K - 1 and t == TILES - 1))
                ins.then_inc(tabled, 1)
            groups = group_count(pe)
            pe.wait_ge(table_ready, 1)

            def step(base, s, first, last):
                turn = lambda d: base * (16 // GROUP) + ((s - d) // GROUP + 1) * 16
                if not last:
                    pe.wait_ge(x_loaded[s % GROUP], turn(0))
                    if not first or s >= 2:
                        pe.wait_ge(xT_ready, base + (s - 1))
                    for k in range(KD):
                        ins = nc.tensor.transpose(xT_ps[s % 2][:, k, :], x[s % GROUP][:, k * P:(k + 1) * P], m.ident[:])
                    ins.then_inc(x_turned, 1)
                if (not first or s >= 1) and (not last or s < 1):
                    d = s - 1
                    pe.wait_ge(xT_ready, base + (d + 1))
                    pe.wait_ge(in_loaded[d % GROUP], turn(1))
                    if not first or d >= 2:
                        pe.wait_ge(gate_done, base + (d - 1))
                    for k in range(KD):
                        ins = nc.tensor.matmul(in_ps[d % 2], lhsT=xT[d % 2][:, k, :], rhs=w_in[d % GROUP][:, k, :],
                                               start=(k == 0), stop=(k == KD - 1))
                    ins.then_inc(in_done, 1)
                if (not first or s >= 2) and (not last or s < 2):
                    d = s - 2
                    pe.wait_ge(gate_done, base + (d + 1))
                    if not first or d >= 2:
                        pe.wait_ge(gT_ready, base + (d - 1))
                    for c in range(chunks):
                        ins = nc.tensor.transpose(gT_ps[d % 2][:, c, :], gated[d % 2][:, c * rows:(c + 1) * rows],
                                                  m.ident[:])
                    ins.then_inc(g_turned, 1)
                if not first or s >= 3:
                    d = s - 3
                    pe.wait_ge(gT_ready, base + (d + 1))
                    pe.wait_ge(down_loaded[d % GROUP], turn(3))
                    if not first or d >= 2:
                        pe.wait_ge(y_ready, base + d)
                    for c in range(chunks):
                        ins = nc.tensor.matmul(y_ps[d % 2], lhsT=gatedT[d % 2][:, c, :], rhs=w_down[d % GROUP][:, c, :],
                                               start=(c == 0), stop=(c == chunks - 1))
                    ins.then_inc(down_done, 1)
            by_steps(pe, groups, step, 3)

        @block.scalar
        def _(act):
            norm_scalar(m, act, j)
            act.wait_ge(less_max, 1)
            nc.scalar.activation(probs[:, :, 0:routed], probs[:, :, 0:routed], ACT.Exp).then_inc(exps, 1)
            if shared:
                gate = logits[:, :, routed:R].to_broadcast([P, TILES, shared])
                nc.scalar.activation(combine[:, :, routed:E], gate, ACT.Sigmoid).then_inc(shared_ready, 1)
            groups = group_count(act)
            for s in range(GROUP):
                act.sem_inc(y_stored[s], 16)
            unused = act.value_load(more_turns[0:1, 1:2], min_val=0, max_val=GROUPS - FEWEST)
            act.wait_ge(m.h_ready, TILES * (n + 1))
            with act.Fori(0, unused + 1) as i:
                act.dma_start(y_groups[bass.ds(GROUPS - i, 1)].rearrange("o b p d -> p (o b) d"),
                              m.h[:, 0:GROUP, :]).then_inc(filled, 16)

            def step(base, s, first, last):
                if not last:
                    act.wait_ge(x_turned, base + (s + 1))
                    if not first or s >= 2:
                        act.wait_ge(in_done, base + (s - 1))
                    nc.scalar.activation(xT[s % 2][:], xT_ps[s % 2], ACT.Copy).then_inc(xT_ready, 1)
                if (not first or s >= 1) and (not last or s < 1):
                    d = s - 1
                    act.wait_ge(in_done, base + (d + 1))
                    if not first or d >= 2:
                        act.wait_ge(gate_done, base + (d - 1))
                    nc.scalar.activation(silu[d % 2][:], in_ps[d % 2][:, 0:F], ACT.Silu).then_inc(silu_done, 1)
                if not first:
                    d = s - 4
                    act.wait_ge(y_ready, base + (d + 2))
                    dst = y_rows.rearrange("(b p) d -> b p d", p=P)[bass.ds(base + d, 1)].rearrange("o p d -> (o p) d")
                    act.dma_start(dst, y[d % GROUP][:]).then_inc(y_stored[d % GROUP], 16)
            by_steps(act, groups, step, 4)
            act.wait_ge(filled, unused * 16 + 16)
            act.sem_inc(all_filled, 1)

        @block.vector
        def _(dve):
            o = m.dve_order
            norm_vector(m, dve, n)
            m.wait_weights(dve, "routing")
            m.wait_weights(dve, "consts")
            o.mark(nc.vector.memset(probs[:, :, routed:], -1.0))
            if shared:
                o.mark(nc.vector.memset(goes[:, :, routed:], 1.0))
            o.mark(nc.vector.memset(before[:, 0, :], 0.0))
            o.mark(nc.vector.tensor_scalar(limits[:], iota[:, 0:TILES], float(P), None, ALU.mult))
            o.mark(nc.vector.tensor_scalar(earlier[:], iota[:, 0:TILES], float(K), None, ALU.mult))
            o.mark(nc.vector.tensor_scalar(turns[:], iota[:, 0:GROUPS], float(GROUP), None, ALU.mult))
            dve.wait_ge(routed_ready, 1)
            o.link(dve, nc.vector.tensor_reduce(row[:], logits[:, :, 0:routed], AX_X, ALU.max))
            nc.vector.tensor_tensor(probs[:, :, 0:routed], logits[:, :, 0:routed],
                                    row[:].unsqueeze(2).to_broadcast([P, TILES, routed]), ALU.subtract).then_inc(less_max, 1)
            dve.wait_ge(exps, 1)
            o.link(dve, nc.vector.tensor_reduce(row[:], probs[:, :, 0:routed], AX_X, ALU.add))
            o.link(dve, nc.vector.reciprocal(row[:], row[:]))
            o.link(dve, nc.vector.tensor_tensor(probs[:, :, 0:routed], probs[:, :, 0:routed],
                                                row[:].unsqueeze(2).to_broadcast([P, TILES, routed]), ALU.mult))
            for t in range(TILES):
                o.mark(nc.vector.max(best[:, t, :], probs[:, t, :]))
            o.wait(dve)
            o.link(dve, nc.vector.memset(best[:, :, top:], -1.0))
            for t in range(TILES):
                o.mark(nc.vector.match_replace(out=rest[:, t, :], in_to_replace=best[:, t, :], in_values=probs[:, t, :],
                                               imm_value=GONE))
            o.wait(dve)
            o.link(dve, nc.vector.tensor_scalar(goes[:, :, 0:routed], rest[:, :, 0:routed], GONE, None, ALU.is_equal))
            for t in range(TILES):
                o.link(dve, nc.vector.tensor_tensor(before[:, t + 1, :], before[:, t, :], goes[:, t, :], ALU.add))
            dve.sem_inc(goes_ready, 1)
            o.link(dve, nc.vector.tensor_tensor(combine[:, :, 0:routed], probs[:, :, 0:routed], goes[:, :, 0:routed],
                                                ALU.mult))
            flat = lambda a: a[:].rearrange("p t e -> p (t e)")
            o.link(dve, nc.vector.tensor_tensor_scan(flat(number), flat(goes), flat(goes), 0.0, ALU.add, ALU.max))
            o.link(dve, nc.vector.tensor_tensor(number[:], number[:], earlier[:].unsqueeze(2).to_broadcast([P, TILES, E]),
                                                ALU.subtract))
            o.link(dve, nc.vector.tensor_tensor(number[:], number[:], goes[:], ALU.mult))
            dve.wait_ge(counted, 1)
            o.link(dve, nc.vector.tensor_tensor(over[:], counts.unsqueeze(2).to_broadcast([P, E, TILES]),
                                                limits[:].unsqueeze(1).to_broadcast([P, E, TILES]), ALU.is_gt))
            o.link(dve, nc.vector.tensor_reduce(blocks[:], over[:], AX_X, ALU.add))
            o.link(dve, nc.vector.tensor_tensor_scan(ends[:], blocks[:], blocks[:], 0.0, ALU.add, ALU.max))
            o.link(dve, nc.vector.tensor_scalar(starts[:], ends[:], token[:, 0:1], None, ALU.is_le))
            o.link(dve, nc.vector.tensor_reduce(owner[:], starts[:], AX_X, ALU.add))
            o.link(dve, nc.vector.tensor_scalar(owner[:], owner[:], float(E - 1), None, ALU.min))
            nc.vector.tensor_scalar(owners_diag[:], m.ident[:], owner[:, 0:1], None, ALU.mult).then_inc(owner_ready, 1)
            o.link(dve, nc.vector.tensor_scalar(turns[:], turns[:], ends[:, E - 1:E], None, ALU.is_lt))
            o.link(dve, nc.vector.tensor_reduce(groups_f[:], turns[:], AX_X, ALU.add))
            o.link(dve, nc.vector.tensor_scalar(more_turns[:, 0:1], groups_f[0:1, :], float(FEWEST), None, ALU.subtract))
            o.link(dve, nc.vector.tensor_scalar(more_turns[:, 1:2], groups_f[0:1, :], -1.0, float(GROUPS), ALU.mult, ALU.add))
            dve.sem_inc(lists_ready, 1)
            dve.wait_ge(owners_filled, 1)
            nc.vector.tensor_copy(owners[:], owner_row[0:1, :]).then_inc(lists_ready, 1)
            o.link(dve, nc.vector.tensor_tensor(starts[:], ends[:], blocks[:], ALU.subtract))
            o.link(dve, nc.vector.tensor_scalar(starts[:], starts[:], float(P), None, ALU.mult))
            o.link(dve, nc.vector.tensor_tensor(slots[:], rank.rearrange("p (t e) -> p t e", e=E),
                                                starts[:].unsqueeze(1).to_broadcast([P, TILES, E]), ALU.add))
            if normalize:
                o.link(dve, nc.vector.tensor_reduce(row[:], combine[:, :, 0:routed], AX_X, ALU.add))
                if floor is not None:
                    o.link(dve, nc.vector.tensor_scalar(row[:], row[:], floor, None, ALU.max))
                o.link(dve, nc.vector.reciprocal(row[:], row[:]))
                o.link(dve, nc.vector.tensor_tensor(combine[:, :, 0:routed], combine[:, :, 0:routed],
                                                    row[:].unsqueeze(2).to_broadcast([P, TILES, routed]), ALU.mult))
            if shared:
                dve.wait_ge(shared_ready, 1)
            for c in range(K):
                for src, dst in ((slots, slot), (combine, weight)):
                    o.link(dve, nc.vector.scalar_tensor_tensor(out=picked[:], in0=number[:], scalar=float(c + 1),
                                                               in1=src[:], op0=ALU.is_equal, op1=ALU.mult))
                    o.link(dve, nc.vector.tensor_reduce(dst[:, c, :], picked[:], AX_X, ALU.add))
            o.link(dve, nc.vector.tensor_scalar(block_of[:], slot[:], 1.0 / P, -(P - 1) / (2.0 * P), ALU.mult, ALU.add))
            o.link(dve, nc.vector.tensor_scalar(block_of[:], block_of[:], ROUND, None, ALU.add))
            o.link(dve, nc.vector.tensor_scalar(block_of[:], block_of[:], ROUND, None, ALU.subtract))
            o.link(dve, nc.vector.scalar_tensor_tensor(out=lane_of[:], in0=block_of[:], scalar=-float(P), in1=slot[:],
                                                       op0=ALU.mult, op1=ALU.add))
            for c in range(K):
                if c >= 2:
                    dve.wait_ge(tabled, c - 1)
                nc.vector.tensor_tensor(block_hot[c % 2][:], iota[:, 0:BLOCKS].unsqueeze(1).to_broadcast([P, TILES, BLOCKS]),
                                        block_of[:, c, :].unsqueeze(2).to_broadcast([P, TILES, BLOCKS]),
                                        ALU.is_equal).then_inc(blocks_ready, 1)
                nc.vector.tensor_tensor(lane_hot[c % 2][:], iota[:].unsqueeze(1).to_broadcast([P, TILES, P]),
                                        lane_of[:, c, :].unsqueeze(2).to_broadcast([P, TILES, P]),
                                        ALU.is_equal).then_inc(lanes_ready, 1)
            o.link(dve, nc.vector.tensor_copy(slot_index[:], slot[:]))
            dve.wait_ge(tabled, K)
            nc.vector.tensor_copy(token_of[:], table).then_inc(table_ready, 1)
            groups = group_count(dve)
            dve.sem_inc(y_ready, 1)

            def step(base, s, first, last):
                if (not first or s >= 2) and (not last or s < 2):
                    d = s - 2
                    dve.wait_ge(g_turned, base + (d + 1))
                    if not first or d >= 2:
                        dve.wait_ge(down_done, base + (d - 1))
                    nc.vector.tensor_copy(gatedT[d % 2][:], gT_ps[d % 2]).then_inc(gT_ready, 1)
                if (not first or s >= 1) and (not last or s < 1):
                    d = s - 1
                    dve.wait_ge(silu_done, base + (d + 1))
                    if not first or d >= 2:
                        dve.wait_ge(g_turned, base + (d - 1))
                    nc.vector.tensor_tensor(gated[d % 2][:], silu[d % 2][:], in_ps[d % 2][:, F:2 * F],
                                            ALU.mult).then_inc(gate_done, 1)
                if not first or s >= 3:
                    d = s - 3
                    dve.wait_ge(down_done, base + (d + 1))
                    if not first:
                        dve.wait_ge(y_stored[d % GROUP], base * (16 // GROUP) + (d // GROUP + 1) * 16)
                    nc.vector.tensor_copy(y[d % GROUP][:], y_ps[d % 2]).then_inc(y_ready, 1)
            by_steps(dve, groups, step, 3)
            with dve.Fori(0, K) as c:
                for t in range(TILES):
                    dve.wait_ge(back_loaded[t], c * 16 + 16)
                    dve.wait_ge(accumulated, c * TILES)
                    nc.vector.scalar_tensor_tensor(
                        out=m.resid[:, t, :], in0=back[t][:], scalar=weight[:, bass.ds(c, 1), t], in1=m.resid[:, t, :],
                        op0=ALU.mult, op1=ALU.add).then_inc(accumulated, 1)



def rotate(m, dve, jobs, name, swapped, cos, sin, tmp, out, bias=(None, None)):
    nc, o = m.nc, m.dve_order
    for x, table, t, b in ((name, cos, tmp[0], bias[0]), (swapped, sin, tmp[1], bias[1])):
        jobs.wait_filled(dve, x)
        src = jobs.pair(x).rearrange("p (b s) -> p b s", s=S)
        if b is None:
            ins = nc.vector.tensor_tensor(t, src, table, ALU.mult)
        else:
            ins = nc.vector.scalar_tensor_tensor(out=t, in0=src, scalar=b, in1=table, op0=ALU.add, op1=ALU.mult)
        ins.then_inc(jobs.empty(x), 1)
        dve.wait_ge(jobs.empty(x), jobs.takers[:jobs.at(x) + 1].count("vector"))
    o.link(dve, nc.vector.tensor_tensor(out, tmp[0], tmp[1], ALU.add))



class Attention:

    SCORES = 4

    def __init__(self, m, tag, heads, causal):
        self.m, self.causal = m, causal
        self.hpc = heads // KD
        self.hd = D // heads
        self.units = heads
        sb, sem = m.sb, lambda s: m.sem(tag + s)
        self.q = sb(tag + "q", [P, B, KD, S])
        self.k = sb(tag + "k", [P, B, KD, S])
        self.v = sb(tag + "v", [P, B, KD, 2, P])
        self.q_head = [sb(tag + f"q_head{i}", [P, S]) for i in range(self.SCORES)]
        self.prob = [sb(tag + f"prob{i}", [P, 2, S]) for i in range(self.SCORES)]
        self.probT = [sb(tag + f"probT{i}", [P, 2, 2, P]) for i in range(2)]
        self.neg_max = [sb(tag + f"neg_max{i}", [P, 2]) for i in range(self.SCORES)]
        self.sums = [sb(tag + f"sums{i}", [P, 2, self.hpc]) for i in range(KD)]
        self.inv = [sb(tag + f"inv{i}", [P, 2, self.hpc]) for i in range(KD)]
        self.out = sb(tag + "out", [P, B, KD, 2 * P])
        self.mask = m.w[tag + "head_mask"]
        (self.inputs, self.may_mask, self.q_ready, self.scored, self.max_ready, self.exp_done, self.turned,
         self.probT_ready, self.mixed, self.inv_ready, self.out_ready, self.outT_filled, self.outT_ready) = (
            sem(s) for s in ("inputs", "may_mask", "q_ready", "scored", "max_ready", "exp_done", "turned", "probT_ready",
                             "mixed", "inv_ready", "out_ready", "outT_filled", "outT_ready"))

    def bank(self, i):
        return self.m.psum[:, i * 512:(i + 1) * 512]

    def mask_queries(self, pool):
        nc, n = self.m.nc, self.units
        with pool.Fori(0, B) as i:
            for h in range(n):
                pool.wait_ge(self.scored, i * n + (h + 1))
                pool.sem_inc(self.may_mask, 1)
                at = h % self.hpc
                q = self.q[:].rearrange("p b c s -> p b (c s)")[:, bass.ds(i, 1), h // self.hpc * S:(h // self.hpc + 1) * S]
                nc.gpsimd.tensor_tensor(self.q_head[h % self.SCORES][:], q.rearrange("p o s -> p (o s)"),
                                        self.mask[:, at:at + 1].to_broadcast([P, S]), ALU.mult).then_inc(self.q_ready, 1)

    def tensor(self, pe):
        nc, m, n, hpc = self.m.nc, self.m, self.units, self.hpc
        pe.sem_inc(self.scored, self.SCORES)
        pe.sem_inc(self.turned, self.SCORES)
        pe.sem_inc(self.mixed, 2)
        with pe.Fori(0, B) as i:
            def score(h):
                pe.wait_ge(self.q_ready, i * n + (h + 1))
                pe.wait_ge(self.exp_done, i * n + (h + 1))
                out = self.bank(h % self.SCORES)
                k = self.k[:, bass.ds(i, 1), h // hpc, :].rearrange("p o s -> p (o s)")
                for qt in range(2):
                    lhs = self.q_head[h % self.SCORES][:, qt * P:(qt + 1) * P]
                    if not self.causal:
                        ins = nc.tensor.matmul(out[:, qt * S:(qt + 1) * S], lhsT=lhs, rhs=k, start=True, stop=True)
                        continue
                    for kt in range(qt + 1):
                        cols = out[:, qt * S + kt * P:qt * S + (kt + 1) * P]
                        ins = nc.tensor.matmul(cols, lhsT=lhs, rhs=k[:, kt * P:(kt + 1) * P], start=True, stop=kt < qt)
                    ins = nc.tensor.matmul(cols, lhsT=m.ident[:], rhs=m.w["causal"][:], start=False, stop=True)
                ins.then_inc(self.scored, 1)

            def turn(h):
                pe.wait_ge(self.exp_done, i * n + (h + 1 + self.SCORES))
                pe.wait_ge(self.probT_ready, i * n + (h + 1))
                for kt in range(2):
                    for qt in range(2):
                        if self.causal and kt > qt:
                            continue
                        at = (kt * 2 + qt) * P
                        ins = nc.tensor.transpose(self.bank(4 + h % 2)[:, at:at + P],
                                                  self.prob[h % self.SCORES][:, qt, kt * P:(kt + 1) * P], m.ident[:])
                ins.then_inc(self.turned, 1)

            def mix(h):
                c, hh = h // hpc, h % hpc
                pe.wait_ge(self.probT_ready, i * n + (h + 3))
                if hh == 0:
                    pe.wait_ge(self.out_ready, i * KD + (c + 1))
                for qt in range(2):
                    kts = range(qt + 1) if self.causal else range(2)
                    for kt in kts:
                        v = self.v[:, bass.ds(i, 1), c, kt, hh * self.hd:(hh + 1) * self.hd].rearrange("p o s -> p (o s)")
                        at = qt * P + hh * self.hd
                        ins = nc.tensor.matmul(self.bank(6 + c)[:, at:at + self.hd], lhsT=self.probT[h % 2][:, kt, qt, :],
                                               rhs=v, start=(kt == 0), stop=(kt == kts[-1]))
                ins.then_inc(self.mixed, 1)

            for h in range(n + 3):
                if h < n:
                    score(h)
                if 2 <= h <= n + 1:
                    turn(h - 2)
                if h >= 3:
                    mix(h - 3)

    def scalar(self, act):
        nc, n, hpc = self.m.nc, self.units, self.hpc
        act.sem_inc(self.exp_done, self.SCORES)
        with act.Fori(0, B) as i:
            for h in range(n):
                c, hh = h // hpc, h % hpc
                if hh == 0:
                    act.wait_ge(self.inv_ready, i * KD + (c + 1))
                act.wait_ge(self.max_ready, i * n + (h + 1))
                act.wait_ge(self.turned, i * n + (h + 1))
                for qt in range(2):
                    keys = (qt + 1) * P if self.causal else S
                    ins = nc.scalar.activation(self.prob[h % self.SCORES][:, qt, 0:keys],
                                               self.bank(h % self.SCORES)[:, qt * S:qt * S + keys], ACT.Exp,
                                               bias=self.neg_max[h % self.SCORES][:, qt:qt + 1],
                                               accum_out=self.sums[c][:, qt, hh:hh + 1])
                ins.then_inc(self.exp_done, 1)

    def vector(self, dve):
        nc, n, hpc = self.m.nc, self.units, self.hpc
        dve.sem_inc(self.out_ready, KD)
        dve.sem_inc(self.inv_ready, KD)
        dve.sem_inc(self.probT_ready, 2)
        with dve.Fori(0, B) as i:
            def maximum(h):
                dve.wait_ge(self.scored, i * n + (h + 1 + self.SCORES))
                dve.wait_ge(self.exp_done, i * n + (h + 1))
                bank, neg_max = self.bank(h % self.SCORES), self.neg_max[h % self.SCORES]
                if self.causal:
                    for qt in range(2):
                        ins = nc.vector.tensor_reduce(neg_max[:, qt:qt + 1], bank[:, qt * S:qt * S + (qt + 1) * P], AX_X,
                                                      ALU.max, negate=True)
                else:
                    ins = nc.vector.tensor_reduce(neg_max[:], bank.rearrange("p (q k) -> p q k", k=S), AX_X, ALU.max,
                                                  negate=True)
                ins.then_inc(self.max_ready, 1)

            def move(h):
                dve.wait_ge(self.turned, i * n + (h + 1 + self.SCORES))
                dve.wait_ge(self.mixed, i * n + (h + 1))
                bank = self.bank(4 + h % 2)
                dst = self.probT[h % 2][:].rearrange("p k q s -> p (k q s)")
                if self.causal:
                    nc.vector.tensor_copy(dst[:, 0:2 * P], bank[:, 0:2 * P])
                    ins = nc.vector.tensor_copy(dst[:, 3 * P:4 * P], bank[:, 3 * P:4 * P])
                else:
                    ins = nc.vector.tensor_copy(dst, bank)
                ins.then_inc(self.probT_ready, 1)

            def normalize(c):
                dve.wait_ge(self.exp_done, i * n + ((c + 1) * hpc + self.SCORES))
                nc.vector.reciprocal(self.inv[c][:], self.sums[c][:]).then_inc(self.inv_ready, 1)
                dve.wait_ge(self.inv_ready, i * KD + (c + 1 + KD))
                dve.wait_ge(self.mixed, i * n + ((c + 1) * hpc + 2))
                out = self.out[:, bass.ds(i, 1), c, :].rearrange("p o (x d) -> p (o x) d", d=self.hd)
                src = self.bank(6 + c)[:, 0:2 * P].rearrange("p (x d) -> p x d", d=self.hd)
                scale = self.inv[c][:].rearrange("p q h -> p (q h)").unsqueeze(2).to_broadcast([P, 2 * hpc, self.hd])
                nc.vector.tensor_tensor(out, src, scale, ALU.mult).then_inc(self.out_ready, 1)

            for h in range(n + 2):
                if h < n:
                    maximum(h)
                if h >= 2:
                    move(h - 2)
                if h == hpc + 4:
                    normalize(0)
            normalize(1)


def softmax_attention(m, n, j, tag, heads, causal):
    nc = m.nc
    self_attn = causal
    w = lambda name: m.w[tag + name]
    a = Attention(m, tag, heads, causal)
    names = [] if self_attn else ["angle"]
    for c in range(KD):
        names += [f"q{c}", f"q{c}s", f"k{c}", f"k{c}s"]
    jobs = Jobs(m, tag + "in", 2, [(x, "vector") for x in names] + [("v0", "scalar"), ("v1", "scalar")])
    ends = Jobs(m, tag + "end", 2, [("out0", "vector"), ("out1", "vector")])
    tmp = [m.sb(tag + f"rot{i}", [P, B, S]) for i in range(2)]
    if self_attn:
        tables = [w(x)[:].unsqueeze(1).to_broadcast([P, B, S]) for x in ("cos", "sin")]
    else:
        turns = [m.sb(tag + f"turns{i}", [P, T]) for i in range(2)]
        whole = [m.sb(tag + f"whole{i}", [P, T]) for i in range(2)]
        tables = [t[:].rearrange("p (b s) -> p b s", s=S) for t in turns]
        turns_ready, table_ready = m.sem(tag + "turns"), m.sem(tag + "table")
    with nc.Block(name=tag + "block") as block:
        @block.gpsimd
        def _(pool):
            norm_gpsimd(m, pool, n)
            pool.wait_ge(a.inputs, 2)
            a.mask_queries(pool)

        @block.tensor
        def _(pe):
            norm_tensor(m, pe, n)
            wait_hT(m, pe, j)
            m.wait_weights(pe, tag)
            hT = feature_rhs(m.hT)
            keys = hT if self_attn else lambda k, cols: m.ctxT[:, cols]
            kc = KD if self_attn else 1
            if not self_attn:
                project(m, pe, jobs, "angle", lambda k: w("freq")[:], lambda k, cols: w("pos")[:, cols], 1)
            for c in range(KD):
                project(m, pe, jobs, f"q{c}", wcols(w("q"), c), hT, KD)
                project(m, pe, jobs, f"q{c}s", wcols(w("q"), KD + c), hT, KD)
                project(m, pe, jobs, f"k{c}", wcols(w("k"), c), keys, kc)
                project(m, pe, jobs, f"k{c}s", wcols(w("k"), KD + c), keys, kc)
            src = m.hT if self_attn else m.ctxT[:].unsqueeze(1)
            project_tokens(m, pe, jobs, ("v0", "v1"), lambda k, t: src[:, k, t * P:(t + 1) * P],
                           lambda k, t: w("v")[:, k, :], kc)
            pe.wait_ge(a.inputs, 3)
            a.tensor(pe)
            pe.wait_ge(a.out_ready, KD + B * KD)
            for q in range(2):
                for t in range(4 * q, 4 * q + 4):
                    for c in range(KD):
                        ins = nc.tensor.transpose(m.pair(c)[:, t * P:(t + 1) * P], a.out[:, t // 2, c, t % 2 * P:(t % 2 + 1) * P],
                                                  m.ident[:])
                ins.then_inc(a.outT_filled, 1)
            pe.wait_ge(a.outT_ready, 4)
            project_tokens(m, pe, ends, ("out0", "out1"), lambda k, t: m.hT[:, k, t * P:(t + 1) * P],
                           lambda k, t: w("o")[:, k, :], KD)

        @block.scalar
        def _(act):
            norm_scalar(m, act, j)
            if not self_attn:
                act.wait_ge(turns_ready, 2)
                for i in range(2):
                    nc.scalar.activation(turns[i][:], turns[i][:], ACT.Sin, scale=SIN_SCALE).then_inc(table_ready, 1)
            for q in range(2):
                name = f"v{q}"
                jobs.wait_filled(act, name)
                for b in range(2):
                    for qt in range(2):
                        src = jobs.pair(name)[:, (2 * b + qt) * D:(2 * b + qt + 1) * D].rearrange("p (c f) -> p c f", c=KD)
                        ins = nc.scalar.activation(a.v[:, 2 * q + b, :, qt, :], src, ACT.Copy)
                ins.then_inc(jobs.empty(name), 1)
            act.wait_ge(jobs.emptied["scalar"], 2)
            act.sem_inc(a.inputs, 1)
            a.scalar(act)
            for q in range(2):
                act.wait_ge(a.outT_filled, q + 1)
                for c in range(KD):
                    cols = slice(q * HALF, (q + 1) * HALF)
                    nc.scalar.activation(m.hT[:, c, cols], m.pair(c)[:, cols], ACT.Copy).then_inc(a.outT_ready, 1)

        @block.vector
        def _(dve):
            o = m.dve_order
            norm_vector(m, dve, n)
            m.wait_weights(dve, tag)
            if not self_attn:
                jobs.wait_filled(dve, "angle")
                ps = jobs.pair("angle")
                o.mark(nc.vector.tensor_scalar(turns[0][:], ps, 0.25, None, ALU.add))
                nc.vector.tensor_copy(turns[1][:], ps).then_inc(jobs.empty("angle"), 1)
                dve.wait_ge(jobs.emptied["vector"], 1)
                for i in range(2):
                    o.mark(nc.vector.tensor_scalar(whole[i][:], turns[i][:], ROUND, -ROUND, ALU.add, ALU.add))
                o.wait(dve)
                for i in range(2):
                    nc.vector.tensor_tensor(turns[i][:], turns[i][:], whole[i][:], ALU.subtract).then_inc(turns_ready, 1)
                dve.wait_ge(table_ready, 2)
            for c in range(KD):
                for x, out in (("q", a.q), ("k", a.k)):
                    rotate(m, dve, jobs, f"{x}{c}", f"{x}{c}s", tables[0], tables[1], [t[:] for t in tmp],
                           out[:, :, c, :])
            dve.sem_inc(a.inputs, 2)
            a.vector(dve)
            add_tokens(m, dve, ends, ("out0", "out1"), bias=None if self_attn else w("o_b")[:])



def feature_attention(m, n, j):
    nc = m.nc
    tag = "l2a_"
    w = lambda name: m.w[tag + name]
    HPC, HD = 8, 16
    chunks = [("q", 0), ("q", 1), ("k", 0)]
    jobs = Jobs(m, tag + "in", 2, [(f"{x}{c}{s}", "vector") for x, c in chunks for s in ("", "s")]
                + [("v", "vector"), ("norm", "scalar")] + [(f"p{x}{c}", "vector") for x, c in chunks]
                + [("t0", "scalar"), ("t1", "scalar"), ("out0", "vector"), ("out1", "vector")])
    tmp = [m.sb(tag + f"rot{i}", [P, B, S]) for i in range(2)]
    x = {f"{k}{c}": m.sb(tag + f"{k}{c}", [P, T]) for k, c in chunks}
    sq = {f"{k}{c}": m.sb(tag + f"sq_{k}{c}", [P, T]) for k, c in chunks}
    feats = sq
    v = m.sb(tag + "v", [P, TILES, P])
    norm = m.sb(tag + "norm", [P, len(chunks), TILES, HPC])
    whole = m.sb(tag + "whole", [P, T])
    pair_prod = [m.sb(tag + f"pair_prod{c}", [P, HPC, HPC, HD]) for c in range(KD)]
    value_prod = [m.sb(tag + f"value_prod{c}", [P, HPC, HD, HPC]) for c in range(KD)]
    weight = [m.sb(tag + f"weight{c}", [P, HPC, HPC]) for c in range(KD)]
    att = m.sb(tag + "att", [P, TILES, D])
    (rotated, turns_ready, feats_ready, v_ready, pair_done, weight_done, value_done, att_done) = (
        m.sem(tag + s) for s in ("rotated", "turns", "feats", "v_ready", "pair", "weight", "value", "att"))

    def head_products(eng, ops, c, t, step, done):
        if step == 0:
            q = feats[f"q{c}"][:, t * P:(t + 1) * P].rearrange("p (h f) -> p h f", f=HD)
            k = feats["k0"][:, t * P:(t + 1) * P].rearrange("p (h f) -> p h f", f=HD)
            ops.tensor_tensor(pair_prod[c][:], q.unsqueeze(1).to_broadcast([P, HPC, HPC, HD]),
                              k.unsqueeze(2).to_broadcast([P, HPC, HPC, HD]), ALU.mult).then_inc(done, 1)
        else:
            g = weight[c][:].rearrange("p k q -> p q k").unsqueeze(2).to_broadcast([P, HPC, HD, HPC])
            vt = v[:, t, :].rearrange("p (k d) -> p d k", d=HD).unsqueeze(1).to_broadcast([P, HPC, HD, HPC])
            ops.tensor_tensor(value_prod[c][:], g, vt, ALU.mult).then_inc(done, 1)

    pool_pair, pool_value = m.sem(tag + "pool_pair"), m.sem(tag + "pool_value")
    stored = [m.sem(tag + f"stored{b}") for b in range(B)]
    att_back = m.sem(tag + "att_back")
    scratch = nc.dram_tensor(tag + "scratch", (B, 2 * HPC, S, HD), F32).ap()
    with nc.Block(name=tag + "block") as block:
        @block.sync
        def _(sp):
            for t in range(TILES):
                sp.wait_ge(att_done, 2 * t + 2)
                dst = scratch[t // 2, :, t % 2 * P:(t % 2 + 1) * P, :].rearrange("h s d -> s h d")
                sp.dma_start(dst, att[:, t, :].rearrange("p (h d) -> p h d", d=HD)).then_inc(stored[t // 2], 16)
            rows = scratch.rearrange("b h (s r) d -> b (h s) (r d)", r=HD).rearrange("b (q p) f -> b p q f", p=P)
            for b in range(B):
                sp.wait_ge(stored[b], 32)
                sp.dma_start(m.h[:, 2 * b:2 * b + 2, :], rows[b]).then_inc(att_back, 16)

        @block.gpsimd
        def _(pool):
            norm_gpsimd(m, pool, n)
            pool.wait_ge(feats_ready, 3)
            pool.wait_ge(v_ready, 1)
            head_products(pool, nc.gpsimd, 1, 0, 0, pool_pair)
            for t in range(TILES):
                if t + 1 < TILES:
                    pool.wait_ge(weight_done, 2 * t + 2)
                    head_products(pool, nc.gpsimd, 1, t + 1, 0, pool_pair)
                pool.wait_ge(weight_done, 2 * t + 2)
                if t:
                    pool.wait_ge(att_done, 2 * t)
                head_products(pool, nc.gpsimd, 1, t, 1, pool_value)

        @block.tensor
        def _(pe):
            norm_tensor(m, pe, n)
            wait_hT(m, pe, j)
            m.wait_weights(pe, tag)
            hT = feature_rhs(m.hT)
            for k, c in chunks:
                half = w(k)[:].shape[2] // (2 * P)
                project(m, pe, jobs, f"{k}{c}", wcols(w(k), c), hT, KD)
                project(m, pe, jobs, f"{k}{c}s", wcols(w(k), half + c), hT, KD)
            jobs.wait_room(pe, "v")
            for t in range(TILES):
                for k in range(KD):
                    ins = nc.tensor.matmul(jobs.pair("v")[:, t * P:(t + 1) * P], lhsT=m.hT[:, k, t * P:(t + 1) * P],
                                           rhs=w("v")[:, k, :], start=(k == 0), stop=(k == KD - 1))
            ins.then_inc(jobs.filled, 1)
            jobs.wait_room(pe, "norm")
            for i, (k, c) in enumerate(chunks):
                pe.wait_ge(rotated, i + 1)
                for t in range(TILES):
                    at = (i * TILES + t) * HPC
                    ins = nc.tensor.matmul(jobs.pair("norm")[:, at:at + HPC], lhsT=sq[f"{k}{c}"][:, t * P:(t + 1) * P],
                                           rhs=w("ones")[:], start=True, stop=True)
            ins.then_inc(jobs.filled, 1)
            for k, c in chunks:
                name = f"p{k}{c}"
                jobs.wait_room(pe, name)
                for t in range(TILES):
                    ins = nc.tensor.matmul(jobs.pair(name)[:, t * P:(t + 1) * P], lhsT=x[f"{k}{c}"][:, t * P:(t + 1) * P],
                                           rhs=w("rand")[:], start=True, stop=True)
                ins.then_inc(jobs.filled, 1)
            pe.wait_ge(att_back, 16 * B)
            for c in range(KD):
                jobs.wait_room(pe, f"t{c}")
                for t in range(TILES):
                    ins = nc.tensor.transpose(jobs.pair(f"t{c}")[:, t * P:(t + 1) * P], m.h[:, t, c * P:(c + 1) * P],
                                              m.ident[:])
                ins.then_inc(jobs.filled, 1)
            pe.wait_ge(jobs.emptied["scalar"], 3)
            project_tokens(m, pe, jobs, ("out0", "out1"), lambda k, t: m.hT[:, k, t * P:(t + 1) * P],
                           lambda k, t: w("o")[:, k, :], KD)

        @block.scalar
        def _(act):
            norm_scalar(m, act, j)
            jobs.wait_filled(act, "norm")
            nc.scalar.activation(norm[:].rearrange("p a t h -> p (a t h)"),
                                 jobs.pair("norm")[:, 0:len(chunks) * TILES * HPC], ACT.Sqrt).then_inc(jobs.empty("norm"), 1)
            for i, (k, c) in enumerate(chunks):
                act.wait_ge(turns_ready, i + 1)
                f = feats[f"{k}{c}"][:]
                nc.scalar.activation(f, f, ACT.Sin, scale=SIN_SCALE).then_inc(feats_ready, 1)
            for c in range(KD):
                jobs.wait_filled(act, f"t{c}")
                nc.scalar.activation(m.hT[:, c, :], jobs.pair(f"t{c}"), ACT.Copy, scale=2.0 / HD).then_inc(jobs.empty(f"t{c}"), 1)

        @block.vector
        def _(dve):
            o = m.dve_order
            norm_vector(m, dve, n)
            m.wait_weights(dve, tag)
            tables = [w(t)[:].unsqueeze(1).to_broadcast([P, B, S]) for t in ("cos", "sin")]
            for k, c in chunks:
                b = w(k + "_b")
                half = b[:].shape[1] // 2
                rotate(m, dve, jobs, f"{k}{c}", f"{k}{c}s", tables[0], tables[1], [t[:] for t in tmp],
                       x[f"{k}{c}"][:].rearrange("p (b s) -> p b s", s=S),
                       bias=(b[:, c:c + 1], b[:, half + c:half + c + 1]))
                nc.vector.tensor_tensor(sq[f"{k}{c}"][:], x[f"{k}{c}"][:], x[f"{k}{c}"][:], ALU.mult).then_inc(rotated, 1)
            jobs.wait_filled(dve, "v")
            nc.vector.tensor_tensor(v[:], jobs.pair("v").rearrange("p (t d) -> p t d", d=P),
                                    w("v_b")[:].unsqueeze(1).to_broadcast([P, TILES, P]), ALU.add).then_inc(jobs.empty("v"), 1)
            dve.wait_ge(jobs.empty("v"), 2 * len(chunks) + 1)
            dve.sem_inc(v_ready, 1)
            dve.wait_ge(jobs.empty("norm"), 1)
            flat = norm[:].rearrange("p a t h -> p (a t h)")
            o.link(dve, nc.vector.tensor_scalar(flat, flat, 1e-6, None, ALU.max))
            o.link(dve, nc.vector.reciprocal(flat, flat))
            o.link(dve, nc.vector.tensor_scalar(flat, flat, float(1 / TWO_PI), None, ALU.mult))
            for i, (k, c) in enumerate(chunks):
                name = f"p{k}{c}"
                jobs.wait_filled(dve, name)
                f = feats[f"{k}{c}"][:]
                heads = lambda a: a.rearrange("p (x f) -> p x f", f=HD)
                r = norm[:, i, :, :].rearrange("p t h -> p (t h)").unsqueeze(2).to_broadcast([P, TILES * HPC, HD])
                nc.vector.tensor_tensor(heads(f), heads(jobs.pair(name)), r, ALU.mult).then_inc(jobs.empty(name), 1)
                dve.wait_ge(jobs.empty(name), jobs.takers[:jobs.at(name) + 1].count("vector"))
                o.link(dve, nc.vector.tensor_scalar(heads(f)[:, :, 8:16], heads(f)[:, :, 8:16], 0.25, None, ALU.add))
                o.link(dve, nc.vector.tensor_scalar(whole[:], f, ROUND, -ROUND, ALU.add, ALU.add))
                nc.vector.tensor_tensor(f, f, whole[:], ALU.subtract).then_inc(turns_ready, 1)
                dve.wait_ge(turns_ready, i + 1)
            dve.wait_ge(feats_ready, 3)
            for t in range(TILES):
                head_products(dve, nc.vector, 0, t, 0, pair_done)
                for c in range(KD):
                    dve.wait_ge((pair_done, pool_pair)[c], t + 1)
                    nc.vector.tensor_reduce(weight[c][:], pair_prod[c][:], AX_X, ALU.add).then_inc(weight_done, 1)
                dve.wait_ge(weight_done, 2 * t + 1)
                head_products(dve, nc.vector, 0, t, 1, value_done)
                for c in range(KD):
                    dve.wait_ge((value_done, pool_value)[c], t + 1)
                    out = att[:, t, c * P:(c + 1) * P].rearrange("p (h d) -> p h d", d=HD)
                    nc.vector.tensor_reduce(out, value_prod[c][:], AX_X, ALU.add).then_inc(att_done, 1)
            add_tokens(m, dve, jobs, ("out0", "out1"), bias=w("o_b")[:])



def context_mixing(m, n, j):
    nc = m.nc
    tag = "l2x_"
    w = lambda name: m.w[tag + name]
    jobs = Jobs(m, tag + "in", 2, [("q", "scalar"), ("k", "scalar"), ("e0", "scalar"), ("e1", "scalar"),
                                   ("t0", "scalar"), ("t1", "scalar"), ("out0", "vector"), ("out1", "vector")])
    q = m.sb(tag + "q", [P, T])
    k = m.sb(tag + "k", [P, T])
    att = m.sb(tag + "att", [P, TILES, S])
    attT = m.sb(tag + "attT", [P, TILES, S])
    neg_max = m.sb(tag + "neg_max", [P, TILES])
    sums = m.sb(tag + "sums", [P, TILES])
    max_ready, att_ready = m.sem(tag + "max"), m.sem(tag + "att")
    with nc.Block(name=tag + "block") as block:
        @block.gpsimd
        def _(pool):
            norm_gpsimd(m, pool, n)

        @block.tensor
        def _(pe):
            norm_tensor(m, pe, n)
            m.wait_weights(pe, tag)
            ctx = lambda k, cols: m.ctxT[:, cols]
            for x in "qk":
                project(m, pe, jobs, x, lambda k, x=x: w(x)[:], ctx, 1)
            pe.wait_ge(jobs.emptied["scalar"], 2)
            wait_hT(m, pe, j)
            for half in range(2):
                name = f"e{half}"
                jobs.wait_room(pe, name)
                for t in range(4 * half, 4 * half + 4):
                    b = t // 2
                    ins = nc.tensor.matmul(jobs.pair(name)[:, (t % 4) * S:(t % 4 + 1) * S], lhsT=q[:, t * P:(t + 1) * P],
                                           rhs=k[:, b * S:(b + 1) * S], start=True, stop=True)
                ins.then_inc(jobs.filled, 1)
            pe.wait_ge(att_ready, 1)
            for half in range(2):
                name = f"t{half}"
                jobs.wait_room(pe, name)
                for b in range(2 * half, 2 * half + 2):
                    for nt in range(2):
                        for mt in range(2):
                            at = (b % 2 * 2 + nt) * S + mt * P
                            ins = nc.tensor.transpose(jobs.pair(name)[:, at:at + P],
                                                      att[:, 2 * b + mt, nt * P:(nt + 1) * P], m.ident[:])
                ins.then_inc(jobs.filled, 1)
            pe.wait_ge(jobs.emptied["scalar"], 6)
            project_tokens(m, pe, jobs, ("out0", "out1"), lambda k, t: m.hT[:, k, t * P:(t + 1) * P],
                           lambda k, t: attT[:, t // 2 * 2 + k, :], KD)

        @block.scalar
        def _(act):
            norm_scalar(m, act, j)
            m.wait_weights(act, tag)
            for x, dst in (("q", q), ("k", k)):
                jobs.wait_filled(act, x)
                nc.scalar.activation(dst[:], jobs.pair(x), ACT.Identity, bias=w(x + "_b")[:, 0:1]).then_inc(jobs.empty(x), 1)
            for half in range(2):
                name = f"e{half}"
                act.wait_ge(max_ready, half + 1)
                for t in range(4 * half, 4 * half + 4):
                    ins = nc.scalar.activation(att[:, t, :], jobs.pair(name)[:, (t % 4) * S:(t % 4 + 1) * S], ACT.Exp,
                                               bias=neg_max[:, t:t + 1], accum_out=sums[:, t:t + 1])
                ins.then_inc(jobs.empty(name), 1)
            for half in range(2):
                name = f"t{half}"
                jobs.wait_filled(act, name)
                nc.scalar.activation(attT[:, 4 * half:4 * half + 4, :].rearrange("p t s -> p (t s)"), jobs.pair(name),
                                     ACT.Copy).then_inc(jobs.empty(name), 1)

        @block.vector
        def _(dve):
            o = m.dve_order
            norm_vector(m, dve, n)
            for half in range(2):
                name = f"e{half}"
                jobs.wait_filled(dve, name)
                nc.vector.tensor_reduce(neg_max[:, 4 * half:4 * half + 4], jobs.pair(name).rearrange("p (t s) -> p t s", s=S),
                                        AX_X, ALU.max, negate=True).then_inc(max_ready, 1)
            dve.wait_ge(jobs.emptied["scalar"], 4)
            o.link(dve, nc.vector.reciprocal(sums[:], sums[:]))
            nc.vector.tensor_tensor(att[:], att[:], sums[:].unsqueeze(2).to_broadcast([P, TILES, S]),
                                    ALU.mult).then_inc(att_ready, 1)
            add_tokens(m, dve, jobs, ("out0", "out1"))



def gated_recurrence(m, n, j):
    nc = m.nc
    tag = "l3a_"
    w = lambda name: m.w[tag + name]
    kinds = ("in", "decay", "gate")
    jobs = Jobs(m, tag + "in", 2, [(f"{x}{c}", "scalar") for x in kinds for c in range(KD)]
                + [("out0", "vector"), ("out1", "vector")])
    val = {x: m.sb(tag + x, [P, KD, T]) for x in kinds}
    part = m.sb(tag + "part", [P, T])
    att = m.sb(tag + "att", [P, KD, T])
    bias_ready, att_ready = m.sem(tag + "bias"), m.sem(tag + "att")
    with nc.Block(name=tag + "block") as block:
        @block.gpsimd
        def _(pool):
            norm_gpsimd(m, pool, n)
            m.wait_weights(pool, tag)
            nc.gpsimd.tensor_tensor(w("decay_b")[:], w("decay_b")[:], w("decay_b2")[:], ALU.add).then_inc(bias_ready, 1)

        @block.tensor
        def _(pe):
            norm_tensor(m, pe, n)
            wait_hT(m, pe, j)
            m.wait_weights(pe, tag)
            for x in kinds:
                for c in range(KD):
                    project(m, pe, jobs, f"{x}{c}", wcols(w(x), c), feature_rhs(m.hT), KD)
            pe.wait_ge(att_ready, KD)
            project_tokens(m, pe, jobs, ("out0", "out1"), lambda k, t: att[:, k, t * P:(t + 1) * P],
                           lambda k, t: w("out")[:, k, :], KD)

        @block.scalar
        def _(act):
            norm_scalar(m, act, j)
            act.wait_ge(bias_ready, 1)
            for x in kinds:
                for c in range(KD):
                    name = f"{x}{c}"
                    jobs.wait_filled(act, name)
                    nc.scalar.activation(val[x][:, c, :], jobs.pair(name), ACT.Silu if x == "in" else ACT.Sigmoid,
                                         bias=w(x + "_b")[:, c:c + 1]).then_inc(jobs.empty(name), 1)

        @block.vector
        def _(dve):
            o = m.dve_order
            norm_vector(m, dve, n)
            m.wait_weights(dve, tag)
            for c in range(KD):
                x, d, g = (val[k][:, c, :] for k in kinds)
                dve.wait_ge(jobs.emptied["scalar"], 3 + c)
                o.link(dve, nc.vector.tensor_tensor(part[:], d, x, ALU.mult))
                o.mark(nc.vector.tensor_tensor(x, x, part[:], ALU.subtract))
                o.link(dve, nc.vector.tensor_tensor(d, d, m.w["carry"][:], ALU.mult))
                o.link(dve, nc.vector.tensor_tensor_scan(part[:], d, x, 0.0, ALU.mult, ALU.add))
                dve.wait_ge(jobs.emptied["scalar"], 5 + c)
                nc.vector.tensor_tensor(att[:, c, :], g, part[:], ALU.mult).then_inc(att_ready, 1)
                dve.wait_ge(att_ready, c + 1)
            add_tokens(m, dve, jobs, ("out0", "out1"), bias=w("out_b")[:])



def mx_round(m, eng, ops, o, x, work, scale, inv, out=None):
    nc = m.nc
    blocks = lambda a: a.rearrange("p (b e) -> p b e", e=MX_BLOCK)
    n = x.shape[-1] // MX_BLOCK
    spread = lambda a: a.unsqueeze(2).to_broadcast([P, n, MX_BLOCK])
    o.link(eng, nc.vector.tensor_reduce(scale, blocks(x), AX_X, ALU.max, apply_absolute_value=True))
    o.link(eng, ops.tensor_scalar(scale, scale, 1.0 / FP8_MAX, 1e-30, ALU.mult, ALU.max))
    o.link(eng, nc.vector.reciprocal(inv, scale))
    o.link(eng, ops.tensor_tensor(blocks(x), blocks(x), spread(inv), ALU.mult))
    o.link(eng, ops.tensor_scalar(work.bitcast(I32), x.bitcast(I32), 0x7F800000, None, ALU.bitwise_and))
    o.link(eng, ops.tensor_scalar(work, work, 2.0 ** -6, 1.5 * 2.0 ** 20, ALU.max, ALU.mult))
    o.link(eng, ops.tensor_tensor(x, x, work, ALU.add))
    o.link(eng, ops.tensor_tensor(x, x, work, ALU.subtract))
    return ops.tensor_tensor(blocks(out if out is not None else x), blocks(x), spread(scale), ALU.mult)


def mx_feed_forward(m, n, j):
    nc = m.nc
    tag = "l1f_"
    w = lambda name: m.w[tag + name]
    INNER = 1024
    KI = INNER // P
    natural = {x: m.sb(tag + "nat_" + x, [P, 2 * INNER]) for x in ("gate", "up", "down")}
    gateT, upT = (m.sb(tag + x + "T", [P, KD, INNER]) for x in ("gate", "up"))
    downT = m.sb(tag + "downT", [P, KI, D])
    work = m.sb(tag + "work", [P, 2 * INNER])
    scale = m.sb(tag + "scale", [P, 2 * INNER // MX_BLOCK])
    inv = m.sb(tag + "inv", [P, 2 * INNER // MX_BLOCK])
    silu = m.sb(tag + "silu", [P, INNER])
    inner = m.sb(tag + "inner", [P, INNER])
    innerT = m.sb(tag + "innerT", [P, KI, P])
    (nat_in, w_rounded, w_turned, w_ready, h_rounded, filled, silu_done, inner_done, inner_rounded, inner_turned,
     innerT_ready, down_filled, added) = (m.sem(tag + s) for s in (
         "nat_in", "w_rounded", "w_turned", "w_ready", "h_rounded", "filled", "silu", "inner", "inner_rounded",
         "inner_turned", "innerT", "down", "added"))
    with nc.Block(name=tag + "block") as block:
        @block.sync
        def _(sp):
            for x in ("gate", "up", "down"):
                sp.dma_start(natural[x][:], m.dram[tag + x]).then_inc(nat_in, 16)

        @block.gpsimd
        def _(pool):
            norm_gpsimd(m, pool, n)

        @block.tensor
        def _(pe):
            for i, x in enumerate(("gate", "up", "down")):
                pe.wait_ge(w_rounded, i + 1)
                if i:
                    pe.wait_ge(w_ready, 2 * i)
                for k in range(2):
                    for f in range(KI):
                        if x == "down":
                            chunk, part = 4 * k + f // 2, f % 2
                            src = natural[x][:, part * INNER + chunk * P:part * INNER + (chunk + 1) * P]
                        else:
                            src = natural[x][:, f * D + k * P:f * D + (k + 1) * P]
                        ins = nc.tensor.transpose(m.pair(2 + k)[:, f * P:(f + 1) * P], src, m.ident[:])
                    ins.then_inc(w_turned, 1)
            pe.wait_ge(h_rounded, 1)
            for half in range(2):
                for t in range(4 * half, 4 * half + 4):
                    for k in range(KD):
                        ins = nc.tensor.transpose(m.pair(k)[:, t * P:(t + 1) * P], m.h[:, t, k * P:(k + 1) * P], m.ident[:])
                ins.then_inc(m.turned, 1)
            wait_hT(m, pe, j)
            pe.wait_ge(w_ready, 6)

            def up(t):
                if t:
                    pe.wait_ge(inner_done, t)
                for p, wt in enumerate((gateT, upT)):
                    for half in range(2):
                        for k in range(KD):
                            cols = slice(half * 512, (half + 1) * 512)
                            ins = nc.tensor.matmul(m.pair(p)[:, cols], lhsT=m.hT[:, k, t * P:(t + 1) * P], rhs=wt[:, k, cols],
                                                   start=(k == 0), stop=(k == KD - 1))
                ins.then_inc(filled, 1)

            def down(t):
                pe.wait_ge(inner_rounded, t + 1)
                if t:
                    pe.wait_ge(innerT_ready, t)
                for f in range(KI):
                    ins = nc.tensor.transpose(m.pair(2)[:, f * P:(f + 1) * P], inner[:, f * P:(f + 1) * P], m.ident[:])
                ins.then_inc(inner_turned, 1)
                pe.wait_ge(innerT_ready, t + 1)
                if t:
                    pe.wait_ge(added, t)
                for f in range(KI):
                    ins = nc.tensor.matmul(m.pair(3)[:, 0:D], lhsT=innerT[:, f, :], rhs=downT[:, f, :], start=(f == 0),
                                           stop=(f == KI - 1))
                ins.then_inc(down_filled, 1)

            for t in range(TILES):
                up(t)
                if t:
                    down(t - 1)
            down(TILES - 1)

        @block.scalar
        def _(act):
            for i in range(3):
                for k in range(2):
                    act.wait_ge(w_turned, 2 * i + k + 1)
                    dst = (gateT[:, k, :], upT[:, k, :],
                           downT[:, 4 * k:4 * k + 4, :].rearrange("p f d -> p (f d)"))[i]
                    nc.scalar.activation(dst, m.pair(2 + k), ACT.Copy).then_inc(w_ready, 1)
            norm_scalar(m, act, j)
            for t in range(TILES):
                act.wait_ge(filled, t + 1)
                if t:
                    act.wait_ge(inner_done, t)
                nc.scalar.activation(silu[:], m.pair(0), ACT.Silu).then_inc(silu_done, 1)
                act.wait_ge(inner_turned, t + 1)
                if t:
                    act.wait_ge(down_filled, t)
                nc.scalar.activation(innerT[:].rearrange("p f t -> p (f t)"), m.pair(2), ACT.Copy).then_inc(innerT_ready, 1)

        @block.vector
        def _(dve):
            o = m.dve_order
            norm_vector(m, dve, n)
            dve.wait_ge(m.h_ready, TILES * (n + 1))
            mx_round(m, dve, nc.vector, o, m.h[:].rearrange("p t d -> p (t d)"), work[:], scale[:],
                     inv[:]).then_inc(h_rounded, 1)
            dve.wait_ge(h_rounded, 1)
            dve.wait_ge(nat_in, 48)
            for i, x in enumerate(("gate", "up", "down")):
                mx_round(m, dve, nc.vector, o, natural[x][:], work[:], scale[:], inv[:]).then_inc(w_rounded, 1)
                dve.wait_ge(w_rounded, i + 1)

            def add(t):
                dve.wait_ge(down_filled, t + 1)
                nc.vector.tensor_tensor(m.resid[:, t, :], m.pair(3)[:, 0:D], m.resid[:, t, :], ALU.add).then_inc(added, 1)

            for t in range(TILES):
                dve.wait_ge(silu_done, t + 1)
                if t:
                    dve.wait_ge(inner_turned, t)
                nc.vector.tensor_tensor(inner[:], silu[:], m.pair(1), ALU.mult).then_inc(inner_done, 1)
                dve.wait_ge(inner_done, t + 1)
                nb = INNER // MX_BLOCK
                mx_round(m, dve, nc.vector, o, inner[:], work[:, 0:INNER], scale[:, 0:nb],
                         inv[:, 0:nb]).then_inc(inner_rounded, 1)
                dve.wait_ge(inner_rounded, t + 1)
                if t:
                    add(t - 1)
            add(TILES - 1)



def weights(m):
    m.weight("consts", "ident", [P, P])
    m.ident = m.w["ident"]
    m.weight("consts", "carry", [P, T])
    m.weight("consts", "ctxT", [P, T])
    m.ctxT = m.w["ctxT"]
    for name, shape in (("iota", [P, P]), ("token", [P, TILES]), ("earlier", [P, P]), ("ones", [P, P])):
        m.weight("routing", name, shape)
    m.weight("l0_attn", "l0_qkv", [P, KD, 3 * D])
    m.weight("l0_attn", "l0_out", [P, KD, D])
    for layer in (0, 1):
        g = f"l{layer}s_"
        for name, shape in (("in", [P, D]), ("conv", [P, KD, D_CONV]), ("conv_b", [P, KD]), ("x", [P, KD, X_DBL]),
                            ("dt", [DT_RANK, D]), ("dt_b", [P, KD]), ("a", [P, KD, N_STATE]), ("d", [P, KD])):
            m.weight(g, g + name, shape)
    for group, name, shape in LATER_WEIGHTS:
        m.weight(group, name, shape)


LATER_WEIGHTS = [
    ("l0f_", "l0f_router", [P, KD, 16]), ("l2f_", "l2f_router", [P, KD, 9]), ("l3f_", "l3f_router", [P, KD, 64]),
    ("l1a_", "l1a_q", [P, KD, 2 * D]), ("l1a_", "l1a_k", [P, KD, 2 * D]), ("l1a_", "l1a_v", [P, KD, D]),
    ("l1a_", "l1a_o", [P, KD, D]), ("l1a_", "l1a_cos", [P, S]), ("l1a_", "l1a_sin", [P, S]),
    ("l1a_", "l1a_head_mask", [P, 8]), ("l1a_", "causal", [P, P]),
    ("l2a_", "l2a_q", [P, KD, 2 * D]), ("l2a_", "l2a_k", [P, KD, D]), ("l2a_", "l2a_v", [P, KD, P]),
    ("l2a_", "l2a_o", [P, KD, D]), ("l2a_", "l2a_cos", [P, S]), ("l2a_", "l2a_sin", [P, S]),
    ("l2a_", "l2a_q_b", [P, 2 * KD]), ("l2a_", "l2a_k_b", [P, 2]), ("l2a_", "l2a_v_b", [P, P]),
    ("l2a_", "l2a_o_b", [P, D]), ("l2a_", "l2a_rand", [P, P]), ("l2a_", "l2a_ones", [P, 8]),
    ("l2x_", "l2x_q", [P, P]), ("l2x_", "l2x_k", [P, P]), ("l2x_", "l2x_q_b", [P, 1]), ("l2x_", "l2x_k_b", [P, 1]),
    ("l3a_", "l3a_in", [P, KD, D]), ("l3a_", "l3a_decay", [P, KD, D]), ("l3a_", "l3a_gate", [P, KD, D]),
    ("l3a_", "l3a_out", [P, KD, D]), ("l3a_", "l3a_in_b", [P, KD]), ("l3a_", "l3a_decay_b", [P, KD]),
    ("l3a_", "l3a_decay_b2", [P, KD]), ("l3a_", "l3a_gate_b", [P, KD]), ("l3a_", "l3a_out_b", [P, D]),
    ("l3x_", "l3x_q", [P, KD, 2 * D]), ("l3x_", "l3x_k", [P, 1, 2 * D]), ("l3x_", "l3x_v", [P, 1, D]),
    ("l3x_", "l3x_o", [P, KD, D]), ("l3x_", "l3x_o_b", [P, D]), ("l3x_", "l3x_freq", [2, P]),
    ("l3x_", "l3x_pos", [2, T]), ("l3x_", "l3x_head_mask", [P, 16]),
]
FIRST_WEIGHTS = ("consts", "l0_attn")
START, STOP = 0, 12


def decoder(nc, dram, out):
    with ExitStack() as ctx:
        m = Machine(nc, ctx, dram)
        weights(m)
        loaded_x = m.sem("loaded_x")
        m.gather_sems = {tag: ([m.sem(tag + f"x_loaded{i}") for i in range(GROUP)],
                               [m.sem(tag + f"back_loaded{i}") for i in range(TILES)])
                         for tag in ("l0f_", "l2f_", "l3f_")}
        stored = m.sem("stored")
        with nc.Block(name="load_x") as block:
            @block.sync
            def _(sp):
                sp.dma_start(m.resid[:], dram["x"]).then_inc(loaded_x, 16)
                m.load_weights(sp, m.w_loaded if START else FIRST_WEIGHTS)
                sp.wait_ge(loaded_x, 16)
                if START:
                    m.wait_weights(sp, "consts")

            @block.gpsimd
            def _(pool):
                nc.gpsimd.memset(m.minus_half[:], -0.5)

        stages = [
            lambda n, j: linear_attention(m, n, j),
            lambda n, j: state_space(m, 0, n),
            lambda n, j: experts(m, n, j, "l0f_", routed=16, top=6, rows=88, chunks=2),
            lambda n, j: softmax_attention(m, n, j, "l1a_", heads=16, causal=True),
            lambda n, j: state_space(m, 1, n),
            lambda n, j: mx_feed_forward(m, n, j),
            lambda n, j: feature_attention(m, n, j),
            lambda n, j: context_mixing(m, n, j),
            lambda n, j: experts(m, n, j, "l2f_", routed=8, top=2, rows=88, chunks=2, shared=4, normalize=True),
            lambda n, j: gated_recurrence(m, n, j),
            lambda n, j: softmax_attention(m, n, j, "l3x_", heads=32, causal=False),
            lambda n, j: experts(m, n, j, "l3f_", routed=64, top=4, rows=96, chunks=1, normalize=True, floor=1e-12),
        ]
        first = nc.free_semaphores[0]
        m.first_stage_sem = first
        j = 0
        for n, stage in enumerate(stages[START:STOP]):
            with ExitStack() as scope:
                outer, m.ctx, m.stage_sems = m.ctx, scope, 0
                stage(n, j)
                if START + n not in (1, 4):
                    j += 1
                with nc.Block(name=f"clear{n}") as block:
                    @block.sync
                    def _(sp):
                        sp.sem_clear(range(first, first + m.stage_sems))
                m.ctx, m.stage_sems = outer, None

        with nc.Block(name="store") as block:
            @block.sync
            def _(sp):
                for group in m.w_loaded:
                    m.wait_weights(sp, group)
                sp.dma_start(out, m.resid[:]).then_inc(stored, 16)
                sp.wait_ge(stored, 16)


def rows_to_chunks(a):
    return np.ascontiguousarray(a.reshape(-1, P, a.shape[-1]).transpose(1, 0, 2))


def column(a):
    return np.ascontiguousarray(a.reshape(-1, P).T)


def constants():
    c = {}
    c["ident"] = np.eye(P, dtype=np.float32)
    carry = np.ones((P, T), np.float32)
    carry[:, ::S] = 0
    c["carry"] = carry
    c["iota"] = np.broadcast_to(np.arange(P, dtype=np.float32), (P, P)).copy()
    c["token"] = (np.arange(P)[:, None] + P * np.arange(TILES)[None, :]).astype(np.float32)
    c["earlier"] = np.triu(np.ones((P, P), np.float32), 1)
    c["ones"] = np.ones((P, P), np.float32)
    f = np.arange(P)
    c["causal"] = np.where(np.arange(P)[None, :] > np.arange(P)[:, None], np.float32(-1e30), np.float32(0))
    for tag, heads, hd in (("l1a_", 8, 16), ("l3x_", 16, 8)):
        own = f[:, None] // hd == np.arange(heads)[None, :]
        c[tag + "head_mask"] = own.astype(np.float32) * np.float32(hd ** -0.5)
    step = np.arange(S, dtype=np.float32)
    inv = (np.float32(10000.0) ** (-(np.arange(0, 16, 2, dtype=np.float32) / np.float32(16)))).astype(np.float32)
    ang = inv[f % 16 // 2][:, None] * step[None, :]
    c["l1a_cos"] = np.cos(ang)
    c["l1a_sin"] = np.sin(ang) * np.where(f % 2, 1, -1).astype(np.float32)[:, None]
    ang = inv[f % 8][:, None] * step[None, :]
    c["l2a_cos"] = np.cos(ang)
    c["l2a_sin"] = np.sin(ang) * np.where(f % 16 < 8, -1, 1).astype(np.float32)[:, None]
    same = (f[:, None] // 16 == f[None, :] // 16).astype(np.float32)
    c["l2a_ones"] = np.ascontiguousarray(same[:, ::16])
    freq = 10000.0 ** -(np.arange(2) / 2)
    axis, which = f % 8 // 4, f % 4 // 2
    turns = freq[which] / TWO_PI * np.where(f % 2, 1, -1)
    c["l3x_freq"] = np.where(axis[None, :] == np.arange(2)[:, None], turns[None, :], 0).astype(np.float32)
    return c


def layouts(i):
    d = {}
    tok = lambda a: np.ascontiguousarray(a.reshape(TILES, P, -1).transpose(1, 0, 2))
    d["x"] = tok(i["x"])
    d["ctxT"] = np.ascontiguousarray(i["ctx_1024"].reshape(T, CTX).T)
    d["l0_qkv"] = rows_to_chunks(i["L0_attn_W_qkv"].T)
    d["l0_out"] = rows_to_chunks(i["L0_attn_W_out"].T)
    for layer in (0, 1):
        g, s = f"l{layer}s_", f"L{layer}_xattn_"
        d[g + "in"] = np.ascontiguousarray(i[s + "in_proj_w"].T)
        d[g + "conv"] = rows_to_chunks(i[s + "conv_w"].reshape(D, D_CONV))
        d[g + "conv_b"] = column(i[s + "conv_b"])
        d[g + "x"] = rows_to_chunks(i[s + "x_proj_w"].T)
        d[g + "dt"] = np.ascontiguousarray(i[s + "dt_proj_w"].T)
        d[g + "dt_b"] = column(i[s + "dt_proj_b"])
        d[g + "a"] = rows_to_chunks(i[s + "A_log"])
        d[g + "d"] = column(i[s + "D"])
    across = lambda a: np.ascontiguousarray(np.broadcast_to(a[None, :], (P, a.shape[0])))
    pairs = np.arange(D) ^ 1
    halves = np.arange(D) ^ 8
    both = lambda a, order: rows_to_chunks(np.concatenate([a, a[:, order]], axis=1))
    for x in "qk":
        d["l1a_" + x] = both(i["L1_attn_w" + x].T, pairs)
    d["l1a_v"] = rows_to_chunks(i["L1_attn_wv"].T)
    d["l1a_o"] = rows_to_chunks(i["L1_attn_wo"].T)
    for x in "qk":
        b = i["L2_attn_b" + x]
        d["l2a_" + x] = both(i["L2_attn_W" + x].T, halves[:len(b)])
        d[f"l2a_{x}_b"] = column(np.concatenate([b, b[halves[:len(b)]]]))
    d["l2a_v"] = rows_to_chunks(i["L2_attn_Wv"].T)
    d["l2a_v_b"] = across(i["L2_attn_bv"])
    d["l2a_o"] = rows_to_chunks(i["L2_attn_Wo"].T)
    d["l2a_o_b"] = across(i["L2_attn_bo"])
    rand = np.zeros((P, P), np.float32)
    for h in range(8):
        for part in range(2):
            rand[16 * h:16 * h + 16, 16 * h + 8 * part:16 * h + 8 * part + 8] = i["L2_attn_rand_matrix"].T
    d["l2a_rand"] = rand
    for x in "qk":
        d["l2x_" + x] = np.ascontiguousarray(i["L2_xattn_W" + x].T)
        d[f"l2x_{x}_b"] = column(i["L2_xattn_b" + x])
    for x in ("in", "decay", "gate", "out"):
        d["l3a_" + x] = rows_to_chunks(i["L3_attn_W_" + x])
    for x in ("in", "decay", "gate"):
        d[f"l3a_{x}_b"] = column(i["L3_attn_b_" + x])
    d["l3a_decay_b2"] = column(i["L3_attn_decay_bias"])
    d["l3a_out_b"] = across(i["L3_attn_b_out"])
    d["l3x_q"] = both(i["L3_xattn_Wq"], pairs)
    d["l3x_k"] = both(i["L3_xattn_Wkv"][:, :D], pairs)
    d["l3x_v"] = rows_to_chunks(i["L3_xattn_Wkv"][:, D:])
    d["l3x_o"] = rows_to_chunks(i["L3_xattn_Wout"])
    d["l3x_o_b"] = across(i["L3_xattn_bout"])
    d["l3x_pos"] = np.ascontiguousarray(i["fside_BxSx2_0"].reshape(T, 2).T)
    for x in ("gate", "up", "down"):
        d["l1f_" + x] = np.ascontiguousarray(rows_to_chunks(i[f"L1_ffn_{x}_w"]).reshape(P, -1))
    up_rows = lambda a: np.ascontiguousarray(a.reshape(a.shape[0], KD, P, -1).transpose(0, 2, 1, 3)).reshape(
        a.shape[0], P, -1)
    down_rows = lambda a, n: np.ascontiguousarray(a.reshape(a.shape[0], n, -1, D).transpose(0, 2, 1, 3)).reshape(
        a.shape[0], a.shape[1] // n, -1)
    d["l0f_router"] = rows_to_chunks(i["L0_ffn_gate_w"].T)
    d["l0f_w_in"] = up_rows(np.concatenate([i["L0_ffn_w_gate"], i["L0_ffn_w_up"]], axis=1).transpose(0, 2, 1))
    d["l0f_w_down"] = down_rows(i["L0_ffn_w_down"].transpose(0, 2, 1), 2)
    d["l2f_router"] = rows_to_chunks(np.concatenate([i["L2_ffn_gate_w"].T, i["L2_ffn_shared_gate_w"]], axis=1))
    cut = lambda a: a.reshape(D, 4, -1).transpose(1, 0, 2)
    gate = np.concatenate([i["L2_ffn_w_gate"], cut(i["L2_ffn_sw_gate"])])
    up = np.concatenate([i["L2_ffn_w_up"], cut(i["L2_ffn_sw_up"])])
    d["l2f_w_in"] = up_rows(np.concatenate([gate, up], axis=2))
    d["l2f_w_down"] = down_rows(np.concatenate([i["L2_ffn_w_down"], i["L2_ffn_sw_down"].reshape(4, -1, D)]), 2)
    d["l3f_router"] = rows_to_chunks(i["L3_ffn_gate_weight"].T)
    d["l3f_w_in"] = up_rows(i["L3_ffn_gate_up_proj"].transpose(0, 2, 1))
    d["l3f_w_down"] = down_rows(i["L3_ffn_down_proj"].transpose(0, 2, 1), 1)
    return d


def kernel(**inputs):
    import concourse.bacc as bacc
    from concourse.bass_utils import run_bass_kernel_spmd

    arrays = {**constants(), **layouts({k: np.asarray(v) for k, v in inputs.items()})}
    nc = bacc.Bacc("TRN2", target_bir_lowering=False, num_devices=1)
    dram = {n: nc.dram_tensor("in_" + n, a.shape, mybir.dt.from_np(a.dtype), kind="ExternalInput").ap()
            for n, a in arrays.items()}
    out = nc.dram_tensor("out_0", (P, TILES, D), F32, kind="ExternalOutput").ap()
    decoder(nc, dram, out)
    r = run_bass_kernel_spmd(nc, [{"in_" + n: a for n, a in arrays.items()}], core_ids=[0])
    y = r.results[0]["out_0"]
    return np.ascontiguousarray(y.transpose(1, 0, 2)).reshape(B, S, D)
```

```python
from contextlib import ExitStack

import numpy as np

import concourse.bass as bass
from concourse import mybir

F32 = mybir.dt.float32
I32 = mybir.dt.int32
U32 = mybir.dt.uint32
BF16 = mybir.dt.bfloat16
F16 = mybir.dt.float16
ALU = mybir.AluOpType
ACT = mybir.ActivationFunctionType
AX_X = mybir.AxisListType.X

P = 128
B, S, D = 4, 256, 256
CTX = 128
T = B * S
TILES = T // P
KD = D // P
HALF = T // 2
PAIR = 1024
NORMS = 12
EPS = 1e-5
TWO_PI = 2.0 * np.pi
SIN_SCALE = float(np.float32(TWO_PI * (1 - 2e-7)))
ROUND = 1.5 * 2.0 ** 23
N_STATE, D_CONV, DT_RANK = 16, 4, 8
X_DBL = DT_RANK + 2 * N_STATE
MX_BLOCK, FP8_MAX = 32, 448.0


STAGE_SEMS = 64


class Order:

    def __init__(self, sem):
        self.sem, self.made, self.turn = sem, 0, None

    def mark(self, ins):
        self.made += 1
        ins.then_inc(self.sem, 1)

    def wait(self, eng):
        eng.wait_ge(self.sem, self.made if self.turn is None else self.turn + self.made)

    def link(self, eng, ins):
        self.mark(ins)
        self.wait(eng)


class Machine:

    def __init__(self, nc, ctx, dram):
        self.nc, self.ctx, self.dram = nc, ctx, dram
        self.stage_sems = None
        self.resid = self.sb("resid", [P, TILES, D])
        self.h = self.sb("h", [P, TILES, D])
        self.hT = self.sb("hT", [P, KD, T])
        self.stats = self.sb("stats", [P, TILES, 6])
        self.moments = self.sb("moments", [P, TILES, 2])
        self.rstd = self.sb("rstd", [P, 2, TILES])
        self.minus_half = self.sb("minus_half", [P, TILES])
        self.psum = ctx.enter_context(nc.psum_tensor("psum", [P, 4 * PAIR], F32))
        self.w = {}
        self.w_loaded = {}
        self.moments_ready = self.sem("moments_ready")
        self.rstd_ready = self.sem("rstd_ready")
        self.h_ready = self.sem("h_ready")
        self.turned = self.sem("turned")
        self.hT_ready = self.sem("hT_ready")
        self.dve_order = Order(self.sem("dve_order"))
        self.act_order = Order(self.sem("act_order"))
        self.pool_order = Order(self.sem("pool_order"))
        self.norm = -1

    def sb(self, name, shape, dt=F32):
        return self.ctx.enter_context(self.nc.sbuf_tensor(name, shape, dt))

    def sem(self, name):
        if self.stage_sems is None:
            return self.ctx.enter_context(self.nc.semaphore(name))
        self.stage_sems += 1
        assert self.stage_sems <= STAGE_SEMS
        return self.ctx.enter_context(self.nc.semaphore(name, num=self.first_stage_sem + self.stage_sems - 1))

    def pair(self, i, rows=P):
        return self.psum[0:rows, i * PAIR:(i + 1) * PAIR]

    def weight(self, group, name, shape):
        self.w[name] = self.sb("w_" + name, shape)
        if group not in self.w_loaded:
            self.w_loaded[group] = [self.sem("loaded_" + group), 0, []]
        self.w_loaded[group][1] += 16
        self.w_loaded[group][2].append(name)

    def load_weights(self, eng, groups):
        for group in groups:
            for name in self.w_loaded[group][2]:
                eng.dma_start(self.w[name][:], self.dram[name]).then_inc(self.w_loaded[group][0], 16)

    def wait_weights(self, eng, group):
        eng.wait_ge(self.w_loaded[group][0], self.w_loaded[group][1])



def norm_vector(m, dve, n):
    nc, o = m.nc, m.dve_order
    for t in range(TILES):
        o.mark(nc.vector.bn_stats(m.stats[:, t, :], m.resid[:, t, :]))
    for t in range(TILES):
        dve.wait_ge(o.sem, o.made - TILES + 1 + t)
        ins = nc.vector.bn_aggr(m.moments[:, t, :], m.stats[:, t, :])
    ins.then_inc(m.moments_ready, 1)
    dve.wait_ge(m.rstd_ready, n + 1)
    for t in range(TILES):
        nc.vector.tensor_scalar(m.h[:, t, :], m.resid[:, t, :], m.moments[:, t, 0:1], m.rstd[:, 1, t:t + 1],
                                ALU.subtract, ALU.mult).then_inc(m.h_ready, 1)


def norm_gpsimd(m, pool, n):
    nc = m.nc
    pool.wait_ge(m.moments_ready, n + 1)
    m.pool_order.link(pool, nc.gpsimd.tensor_scalar(m.rstd[:, 0, :], m.moments[:, :, 1], EPS, None, ALU.add))
    nc.gpsimd.tensor_tensor(m.rstd[:, 1, :], m.rstd[:, 0, :], m.minus_half[:], ALU.pow).then_inc(m.rstd_ready, 1)


def norm_tensor(m, pe, n):
    nc = m.nc
    for t in range(TILES):
        pe.wait_ge(m.h_ready, TILES * n + t + 1)
        for k in range(KD):
            at = k * PAIR + t * P
            ins = nc.tensor.transpose(m.psum[:, at:at + P], m.h[:, t, k * P:(k + 1) * P], m.ident[:])
        if t % 4 == 3:
            ins.then_inc(m.turned, 1)


def norm_scalar(m, act, j):
    nc = m.nc
    for half in range(2):
        act.wait_ge(m.turned, 2 * j + half + 1)
        for k in range(KD):
            cols = slice(half * HALF, (half + 1) * HALF)
            nc.scalar.activation(m.hT[:, k, cols], m.pair(k)[:, cols], ACT.Copy).then_inc(m.hT_ready, 1)


def wait_hT(m, eng, j, half=1):
    eng.wait_ge(m.hT_ready, 4 * j + 2 * (half + 1))


class Jobs:

    def __init__(self, m, label, first, jobs):
        self.m, self.first = m, first
        self.names = [n for n, _ in jobs]
        self.takers = [k for _, k in jobs]
        self.filled = m.sem(label + "_filled")
        self.emptied = {k: m.sem(label + "_emptied_" + k) for k in sorted(set(self.takers))}

    def at(self, name):
        return self.names.index(name)

    def pair(self, name, rows=P):
        return self.m.pair((self.first + self.at(name)) % 4, rows)

    def wait_room(self, eng, name):
        i = self.at(name) - 4
        if i >= 0:
            k = self.takers[i]
            eng.wait_ge(self.emptied[k], self.takers[:i + 1].count(k))

    def wait_filled(self, eng, name):
        eng.wait_ge(self.filled, self.at(name) + 1)

    def empty(self, name):
        return self.emptied[self.takers[self.at(name)]]


def project(m, pe, jobs, name, w, rhs, chunks, rows=P, turn=None):
    nc = m.nc
    jobs.wait_room(pe, name)
    out = jobs.pair(name, rows)
    for half in range(2):
        cols = slice(half * HALF, (half + 1) * HALF)
        if turn is not None:
            wait_hT(m, pe, turn, half)
        for k in range(chunks):
            ins = nc.tensor.matmul(out[:, cols], lhsT=w(k), rhs=rhs(k, cols), start=(k == 0), stop=(k == chunks - 1))
    ins.then_inc(jobs.filled, 1)


def project_tokens(m, pe, jobs, names, lhs, rhs, chunks):
    nc = m.nc
    for q, name in enumerate(names):
        jobs.wait_room(pe, name)
        out = jobs.pair(name)
        for j in range(4):
            t = 4 * q + j
            for k in range(chunks):
                ins = nc.tensor.matmul(out[:, j * D:(j + 1) * D], lhsT=lhs(k, t), rhs=rhs(k, t),
                                       start=(k == 0), stop=(k == chunks - 1))
        ins.then_inc(jobs.filled, 1)


def add_tokens(m, dve, jobs, names, scale=1.0, bias=None):
    nc = m.nc
    if bias is not None:
        m.dve_order.link(dve, nc.vector.tensor_tensor(m.resid[:], m.resid[:],
                                                      bias.unsqueeze(1).to_broadcast([P, TILES, D]), ALU.add))
    for q, name in enumerate(names):
        jobs.wait_filled(dve, name)
        r = m.resid[:, 4 * q:4 * q + 4, :]
        ps = jobs.pair(name).rearrange("p (t d) -> p t d", d=D)
        nc.vector.scalar_tensor_tensor(out=r, in0=ps, scalar=scale, in1=r, op0=ALU.mult,
                                       op1=ALU.add).then_inc(jobs.empty(name), 1)


def wcols(w, c):
    return lambda k: w[:, k, c * P:(c + 1) * P]


def feature_rhs(x):
    return lambda k, cols: x[:, k, cols]



def linear_attention(m, n, j):
    nc = m.nc
    w = m.w["l0_qkv"]
    jobs = Jobs(m, "l0a", 2, [(x + str(c), "vector" if x == "v" else "scalar") for c in range(KD) for x in "qkv"]
                + [("out0", "vector"), ("out1", "vector")])
    e = [m.sb(f"l0_exp{i}", [P, T]) for i in range(2)]
    r = [m.sb(f"l0_relu{i}", [P, T]) for i in range(2)]
    sums = [m.sb(f"l0_sum{i}", [P, T]) for i in range(2)]
    att = m.sb("l0_att", [P, KD, T])
    phi_in = m.sem("l0_phi_in")
    chunk_done = m.sem("l0_chunk_done")
    with nc.Block(name="l0_attn") as block:
        @block.sync
        def _(sp):
            m.load_weights(sp, [g for g in m.w_loaded if g not in FIRST_WEIGHTS])

        @block.gpsimd
        def _(pool):
            norm_gpsimd(m, pool, n)

        @block.tensor
        def _(pe):
            m.wait_weights(pe, "consts")
            norm_tensor(m, pe, n)
            m.wait_weights(pe, "l0_attn")
            for c in range(KD):
                for i, x in enumerate("qkv"):
                    project(m, pe, jobs, x + str(c), wcols(w, KD * i + c), feature_rhs(m.hT), KD,
                            turn=j if c + i == 0 else None)
            pe.wait_ge(chunk_done, KD)
            project_tokens(m, pe, jobs, ("out0", "out1"), lambda k, t: att[:, k, t * P:(t + 1) * P],
                           lambda k, t: m.w["l0_out"][:, k, :], KD)

        @block.scalar
        def _(act):
            norm_scalar(m, act, j)
            for c in range(KD):
                for i, x in enumerate("qk"):
                    name = x + str(c)
                    jobs.wait_filled(act, name)
                    if c:
                        act.wait_ge(chunk_done, c)
                    nc.scalar.activation(e[i][:], jobs.pair(name), ACT.Exp).then_inc(phi_in, 1)
                    nc.scalar.activation(r[i][:], jobs.pair(name), ACT.Relu).then_inc(jobs.empty(name), 1)

        @block.vector
        def _(dve):
            o = m.dve_order
            norm_vector(m, dve, n)
            m.wait_weights(dve, "consts")
            for c in range(KD):
                dve.wait_ge(jobs.emptied["scalar"], 2 * c + 2)
                for i in range(2):
                    o.mark(nc.vector.scalar_tensor_tensor(out=e[i][:], in0=e[i][:], scalar=1.0, in1=r[i][:],
                                                          op0=ALU.min, op1=ALU.add))
                o.wait(dve)
                name = "v" + str(c)
                jobs.wait_filled(dve, name)
                ins = nc.vector.tensor_tensor(r[1][:], e[1][:], jobs.pair(name), ALU.mult)
                ins.then_inc(jobs.empty(name), 1)
                dve.wait_ge(jobs.empty(name), c + 1)
                o.mark(nc.vector.tensor_tensor_scan(sums[0][:], m.w["carry"][:], r[1][:], 0.0, ALU.mult, ALU.add))
                o.mark(nc.vector.tensor_tensor_scan(sums[1][:], m.w["carry"][:], e[1][:], 0.0, ALU.mult, ALU.add))
                o.wait(dve)
                for i in range(2):
                    o.mark(nc.vector.tensor_tensor(sums[i][:], e[0][:], sums[i][:], ALU.mult))
                o.wait(dve)
                o.link(dve, nc.vector.tensor_scalar(sums[1][:], sums[1][:], 1e-9, None, ALU.add))
                o.link(dve, nc.vector.reciprocal(sums[1][:], sums[1][:]))
                nc.vector.tensor_tensor(att[:, c, :], sums[0][:], sums[1][:], ALU.mult).then_inc(chunk_done, 1)
            add_tokens(m, dve, jobs, ("out0", "out1"), scale=16 ** -0.5)



def state_space(m, layer, n):
    nc = m.nc
    g = f"l{layer}s_"
    w = {k: m.w[g + k] for k in ("in", "conv", "conv_b", "x", "dt", "dt_b", "a", "d")}
    xpad = m.sb(g + "xpad", [P, KD, B, D_CONV - 1 + S])
    conv = m.sb(g + "conv_out", [P, KD, T])
    u = m.sb(g + "u", [P, KD, T])
    xdbl = m.sb(g + "xdbl", [X_DBL, T])
    t_abs = m.sb(g + "t_abs", [P, KD, T])
    t_sq = m.sb(g + "t_sq", [P, KD, T])
    relu = m.sb(g + "relu", [P, KD, T])
    du = m.sb(g + "du", [P, KD, T])
    two = m.sb(g + "two", [P, 1])
    skip = m.hT
    gate = m.sb(g + "gate", [P, TILES, S])
    decay = [t_sq[:, i, :] for i in range(2)]
    drive = [xpad[:, i, :, :].rearrange("p b s -> p (b s)")[:, 0:T] for i in range(2)]
    state = [relu[:, i, :] for i in range(2)]
    read = [conv[:, i, :] for i in range(2)]
    SLOTS = 4
    bc = [m.sb(g + f"bc{i}", [P, 2, T]) for i in range(SLOTS)]
    scratch = nc.dram_tensor(g + "scratch", (X_DBL, T), F32).ap()
    delta = t_abs
    (x_filled, pads, x_out, conv_done, u_ready, xdbl_filled, xdbl_ready, stored, dt_filled, act_dt, delta_ready,
     du_ready, gate_ready, decay_ready, drive_ready, scanned, read_ready, summed, product, turned,
     skip_ready, ratio_ready) = (m.sem(g + s) for s in (
         "x_filled", "pads", "x_out", "conv_done", "u_ready", "xdbl_filled", "xdbl_ready", "stored", "dt_filled",
         "act_dt", "delta_ready", "du_ready", "gate_ready", "decay_ready", "drive_ready", "scanned", "read_ready",
         "summed", "product", "turned", "skip_ready", "ratio_ready"))
    bc_in = [m.sem(g + f"bc_in{i}") for i in range(SLOTS)]
    GROUPS = N_STATE // SLOTS

    with nc.Block(name=g + "block") as block:
        @block.sync
        def _(sp):
            sp.wait_ge(xdbl_ready, 1)
            sp.dma_start(scratch, xdbl[:]).then_inc(stored, 16)
            sp.wait_ge(stored, 16)
            rows = scratch[DT_RANK:X_DBL, :].rearrange("(a n) t -> n a t", n=N_STATE)
            for s in range(SLOTS):
                sp.dma_start(bc[s][:], rows[s].partition_broadcast(P)).then_inc(bc_in[s], 16)
            with sp.Fori(1, GROUPS) as i:
                for s in range(SLOTS):
                    sp.wait_ge(read_ready, (i * SLOTS + s - SLOTS + 1) * KD)
                    src = rows[bass.ds(i * SLOTS + s, 1)].rearrange("o a t -> (o a) t")
                    sp.dma_start(bc[s][:], src.partition_broadcast(P)).then_inc(bc_in[s], 16)

        @block.gpsimd
        def _(pool):
            o = m.pool_order
            nc.gpsimd.memset(two[:], 2.0)
            nc.gpsimd.memset(xpad[:], 0.0).then_inc(pads, 1)
            norm_gpsimd(m, pool, n)
            pool.wait_ge(u_ready, KD)
            for c in range(KD):
                pool.wait_ge(delta_ready, c + 1)
                o.mark(nc.gpsimd.tensor_tensor(du[:, c, :], delta[:, c, :], u[:, c, :], ALU.mult))
            o.wait(pool)
            for c in range(KD):
                first = delta[:, c, :].rearrange("p (b s) -> p b s", s=S)[:, :, 0:1]
                ins = nc.gpsimd.memset(first, 1e25)
            ins.then_inc(du_ready, 1)

            def group(i, q0):
                for s in range(SLOTS):
                    pool.wait_ge(bc_in[s], (i + 1) * 16)
                    for c in range(KD):
                        pool.wait_ge(scanned, q0 + s * KD + c + 1)
                        nc.gpsimd.tensor_tensor(drive[c], du[:, c, :], bc[s][:, 0, :],
                                                ALU.mult).then_inc(drive_ready, 1)
            with pool.Fori(0, GROUPS) as i:
                group(i, i * (SLOTS * KD))

        @block.tensor
        def _(pe):
            m.wait_weights(pe, g)
            for c in range(KD):
                for half in range(2):
                    cols = slice(half * HALF, (half + 1) * HALF)
                    ins = nc.tensor.matmul(m.pair(c)[:, cols], lhsT=w["in"][:, c * P:(c + 1) * P], rhs=m.ctxT[:, cols],
                                           start=True, stop=True)
                ins.then_inc(x_filled, 1)
            pe.wait_ge(u_ready, KD)
            for half in range(2):
                cols = slice(half * HALF, (half + 1) * HALF)
                for k in range(KD):
                    ins = nc.tensor.matmul(m.pair(2, X_DBL)[:, cols], lhsT=w["x"][:, k, :], rhs=u[:, k, cols],
                                           start=(k == 0), stop=(k == KD - 1))
            ins.then_inc(xdbl_filled, 1)
            pe.wait_ge(xdbl_ready, 1)
            for c in range(KD):
                for half in range(2):
                    cols = slice(half * HALF, (half + 1) * HALF)
                    ins = nc.tensor.matmul(m.pair(c)[:, cols], lhsT=w["dt"][:, c * P:(c + 1) * P],
                                           rhs=xdbl[0:DT_RANK, cols], start=True, stop=True)
                ins.then_inc(dt_filled, 1)
            pe.wait_ge(skip_ready, KD)

            def add(c, rhs, start, stop):
                for half in range(2):
                    cols = slice(half * HALF, (half + 1) * HALF)
                    ins = nc.tensor.matmul(m.pair(2 + c)[:, cols], lhsT=m.ident[:], rhs=rhs[:, cols], start=start,
                                           stop=stop, skip_group_check=True)
                return ins

            for c in range(KD):
                add(c, skip[:, c, :], True, False)

            def group(q0, last):
                for s in range(SLOTS):
                    for c in range(KD):
                        pe.wait_ge(read_ready, q0 + s * KD + c + 1)
                        add(c, read[c], False, last and s == SLOTS - 1).then_inc(summed, 1)
            with pe.Fori(0, GROUPS - 1) as i:
                group(i * (SLOTS * KD), False)
            group((GROUPS - 1) * SLOTS * KD, True)
            pe.wait_ge(product, KD)
            for q in range(2):
                for b in range(2 * q, 2 * q + 2):
                    for lh in range(2):
                        for c in range(KD):
                            at = q * PAIR + (2 * (b % 2) + lh) * D + c * P
                            src = conv[:, c, b * S + lh * P:b * S + (lh + 1) * P]
                            ins = nc.tensor.transpose(m.psum[:, at:at + P], src, m.ident[:])
                ins.then_inc(turned, 1)

        @block.scalar
        def _(act):
            act.wait_ge(pads, 1)
            for c in range(KD):
                act.wait_ge(x_filled, c + 1)
                nc.scalar.activation(xpad[:, c, :, D_CONV - 1:], m.pair(c).rearrange("p (b s) -> p b s", s=S),
                                     ACT.Copy).then_inc(x_out, 1)
            for c in range(KD):
                act.wait_ge(conv_done, c + 1)
                nc.scalar.activation(u[:, c, :], conv[:, c, :], ACT.Silu, bias=w["conv_b"][:, c:c + 1]).then_inc(u_ready, 1)
            act.wait_ge(u_ready, KD)
            for c in range(KD):
                nc.scalar.activation(skip[:, c, :], u[:, c, :], ACT.Copy, scale=w["d"][:, c:c + 1]).then_inc(skip_ready, 1)
            act.wait_ge(xdbl_filled, 1)
            nc.scalar.activation(xdbl[:], m.pair(2, X_DBL), ACT.Copy).then_inc(xdbl_ready, 1)
            for c in range(KD):
                act.wait_ge(dt_filled, c + 1)
                m.act_order.link(act, nc.scalar.activation(t_abs[:, c, :], m.pair(c), ACT.Abs, bias=w["dt_b"][:, c:c + 1]))
                nc.scalar.activation(relu[:, c, :], m.pair(c), ACT.Relu, bias=w["dt_b"][:, c:c + 1])
                m.act_order.link(act, nc.scalar.activation(t_abs[:, c, :], t_abs[:, c, :], ACT.Exp, scale=-1.0))
            for c in range(KD):
                m.act_order.mark(nc.scalar.activation(t_sq[:, c, :], t_abs[:, c, :], ACT.Ln, bias=two[:]))
            m.act_order.wait(act)
            for c in range(KD):
                nc.scalar.activation(t_sq[:, c, :], t_sq[:, c, :], ACT.Exp, scale=-1.0).then_inc(act_dt, 1)
            act.wait_ge(m.h_ready, TILES * (n + 1))
            nc.scalar.activation(gate[:], m.h[:], ACT.Silu).then_inc(gate_ready, 1)
            m.act_order.link(act, nc.scalar.activation(w["a"][:], w["a"][:], ACT.Exp))
            m.act_order.link(act, nc.scalar.mul(w["a"][:], w["a"][:], -1.0))
            act.wait_ge(du_ready, 1)
            with act.Fori(0, GROUPS) as i:
                for s in range(SLOTS):
                    for c in range(KD):
                        act.wait_ge(scanned, i * (SLOTS * KD) + s * KD + c + 1)
                        at = i * SLOTS + s
                        nc.scalar.activation(decay[c], delta[:, c, :], ACT.Exp,
                                             scale=w["a"][:, c, bass.ds(at, 1)]).then_inc(decay_ready, 1)

        @block.vector
        def _(dve):
            o = m.dve_order
            dve.sem_inc(scanned, KD)
            m.wait_weights(dve, g)
            for c in range(KD):
                dve.wait_ge(x_out, c + 1)
                out = conv[:, c, :].rearrange("p (b s) -> p b s", s=S)
                o.link(dve, nc.vector.tensor_scalar(out, xpad[:, c, :, 0:S], w["conv"][:, c, 0:1], None, ALU.mult))
                for k in range(1, D_CONV):
                    ins = nc.vector.scalar_tensor_tensor(out=out, in0=xpad[:, c, :, k:k + S], scalar=w["conv"][:, c, k:k + 1],
                                                         in1=out, op0=ALU.mult, op1=ALU.add)
                    if k < D_CONV - 1:
                        o.link(dve, ins)
                ins.then_inc(conv_done, 1)
            norm_vector(m, dve, n)
            for c in range(KD):
                dve.wait_ge(act_dt, c + 1)
                softplus_ratio(m, dve, c, t_abs[:, c, :], t_sq[:, c, :], ratio_ready)
                softplus_tail(dve, nc.vector, o, t_abs[:, c, :], t_sq[:, c, :], conv[:, c, :], relu[:, c, :],
                              delta[:, c, :], delta_ready)

            def unit(q, c, s, i):
                dve.wait_ge(decay_ready, q + 1)
                dve.wait_ge(drive_ready, q + 1)
                nc.vector.tensor_tensor_scan(state[c], decay[c], drive[c], 0.0, ALU.mult,
                                             ALU.add).then_inc(scanned, 1)
                dve.wait_ge(scanned, q + 1 + KD)
                dve.wait_ge(summed, q + 1)
                nc.vector.tensor_tensor(read[c], state[c], bc[s][:, 1, :], ALU.mult).then_inc(read_ready, 1)

            dve.sem_inc(summed, KD)
            with dve.Fori(0, GROUPS) as i:
                for s in range(SLOTS):
                    for c in range(KD):
                        unit(i * (SLOTS * KD) + s * KD + c, c, s, i)
            dve.wait_ge(summed, KD + N_STATE * KD)
            dve.wait_ge(gate_ready, 1)
            for c in range(KD):
                y = m.pair(2 + c).rearrange("p (b s) -> p b s", s=S)
                z = gate[:].rearrange("p (b c) s -> p b c s", c=KD)[:, :, c, :]
                nc.vector.tensor_tensor(conv[:, c, :].rearrange("p (b s) -> p b s", s=S), y, z,
                                        ALU.mult).then_inc(product, 1)
            for q in range(2):
                dve.wait_ge(turned, q + 1)
                r = m.resid[:, 4 * q:4 * q + 4, :]
                o.link(dve, nc.vector.tensor_tensor(r, m.pair(q).rearrange("p (t d) -> p t d", d=D), r, ALU.add))


def softplus_ratio(m, dve, c, e, q, ratio_ready):
    nc, o = m.nc, m.dve_order
    nc.vector.tensor_tensor(e, e, q, ALU.mult).then_inc(ratio_ready, 1)
    dve.wait_ge(ratio_ready, c + 1)


def softplus_tail(dve, ops, o, s, sq, p, relu, delta, delta_ready):
    def times(p, scalar, by, op0, op1, out=None):
        return ops.scalar_tensor_tensor(out=p if out is None else out, in0=p, scalar=scalar, in1=by, op0=op0, op1=op1)

    o.link(dve, ops.tensor_tensor(sq, s, s, ALU.mult))
    o.link(dve, ops.tensor_scalar(p, sq, 1 / 11, None, ALU.mult))
    for odd in (9, 7, 5, 3):
        o.link(dve, times(p, 1 / odd, sq, ALU.add, ALU.mult))
    o.link(dve, times(p, 1.0, s, ALU.add, ALU.mult))
    times(p, 2.0, relu, ALU.mult, ALU.add, out=delta).then_inc(delta_ready, 1)



ROUTED_BY = 9
GROUP = 4


def by_steps(eng, groups, step, lag):
    for s in range(GROUP):
        step(0, s, True, False)
    with eng.Fori(1, groups) as i:
        for s in range(GROUP):
            step(i * GROUP, s, False, False)
    for s in range(lag):
        step(groups * GROUP, s, False, True)


def experts(m, n, j, tag, routed, top, rows, chunks, shared=0, normalize=False, floor=None):
    nc = m.nc
    E = routed
    R = routed + (1 if shared else 0)
    K = top
    F = rows * chunks
    PAD = 8 - top
    BLOCKS = -(-((K * T + E * (P - 1)) // P) // GROUP) * GROUP
    GROUPS = BLOCKS // GROUP
    FEWEST = K * T // P // GROUP
    GONE = -2.0
    sb, sem = m.sb, lambda s: m.sem(tag + s)
    router, iota, token = m.w[tag + "router"], m.w["iota"], m.w["token"]
    ring = lambda name, shape, count, dt=F32: [sb(tag + f"{name}{i}", shape, dt) for i in range(count)]
    combine = sb(tag + "combine", [P, TILES, E])
    probs = sb(tag + "probs", [P, TILES, routed + PAD])
    rest = sb(tag + "rest", [P, TILES, routed + PAD])
    best = sb(tag + "best", [P, TILES, 8])
    row = sb(tag + "row", [P, TILES])
    goes = sb(tag + "goes", [P, TILES, E])
    before = sb(tag + "before", [P, TILES + 1, E])
    number = sb(tag + "number", [P, TILES, E])
    slots = sb(tag + "slots", [P, TILES, E])
    picked = [sb(tag + f"picked{i}", [P, TILES, E]) for i in range(2)]
    over = sb(tag + "over", [P, E, TILES])
    blocks, ends, starts = (sb(tag + s, [P, E]) for s in ("blocks", "ends", "starts"))
    limits = sb(tag + "limits", [P, TILES])
    earlier = sb(tag + "earlier", [P, TILES])
    turns = sb(tag + "turns", [P, GROUPS])
    slot, weight, block_of, lane_of = (sb(tag + s, [P, K, TILES]) for s in ("slot", "weight", "block_of", "lane_of"))
    slot_index = sb(tag + "slot_index", [P, K, TILES], U32)
    owner, groups_f = sb(tag + "owner", [P, 1]), sb(tag + "groups_f", [P, 1])
    owners_diag = sb(tag + "owners_diag", [P, P])
    owners = sb(tag + "owners", [1, P], I32)
    more_turns = sb(tag + "more_turns", [1, 1], I32)
    lane_hot = ring("lane_hot", [P, TILES, P], 2, F16)
    block_hot = ring("block_hot", [P, TILES, BLOCKS], 2, F16)
    token_of = sb(tag + "token_of", [P, BLOCKS], U32)
    token_now = sb(tag + "token_now", [P, GROUP], U32)
    open_gate = sb(tag + "open_gate", [P, TILES]) if shared else None
    shared_y = ring("shared_y", [P, D], 2) if shared else None
    up = ring("up", [P, F], 2) if shared else None
    x = ring("x", [P, D], GROUP)
    xT = ring("xT", [P, KD, P], 2)
    w_in = ring("w_in", [P, KD, 2 * F], GROUP)
    w_down = ring("w_down", [rows, chunks, D], GROUP)
    silu = ring("silu", [P, F], 2)
    gated = ring("gated", [P, F], 2)
    gatedT = ring("gatedT", [rows, chunks, P], 2)
    y = ring("y", [P, D], GROUP)
    back = ring("back", [P, D], TILES)
    h_rows = nc.dram_tensor(tag + "h_rows", (T, D), F32).ap()
    y_rows = nc.dram_tensor(tag + "y_rows", (BLOCKS * P, D), F32).ap()
    y_groups = y_rows.rearrange("(g b p) d -> g b p d", b=GROUP, p=P)

    bank = lambda i: m.psum[:, i * 512:(i + 1) * 512]
    logits = bank(4)[:, 0:TILES * R].rearrange("p (t e) -> p t e", e=R)
    rank = bank(5)[:, 0:TILES * E]
    counts = bank(6)[:, 0:E]
    owner_row = bank(6)[:, 0:P]
    table = bank(4)[:, 0:BLOCKS]
    xT_ps = [bank(i)[:, 0:D].rearrange("p (k t) -> p k t", t=P) for i in (0, 1)]
    in_ps = [bank(i)[:, 0:2 * F] for i in (2, 3)]
    gT_ps = [bank(i)[0:rows, 0:chunks * P].rearrange("p (c t) -> p c t", t=P) for i in (4, 5)]
    y_ps = [bank(i)[:, 0:D] for i in (6, 7)]

    (routed_ready, less_max, exps, shared_ready, goes_ready, counted, owner_ready, owners_filled, lists_ready,
     lanes_ready, blocks_ready, tokens_ready, tabled, table_ready, h_stored, token_ready, x_turned, xT_ready,
     in_done, silu_done, gate_done, g_turned, gT_ready, down_done, y_ready, filled, may_gather,
     accumulated) = (
        sem(s) for s in ("logits", "less_max", "exps", "shared", "goes", "counted", "owner", "owners_filled",
                         "lists", "lanes", "blocks_of", "tokens", "tabled", "table", "h_stored", "token", "x_turned",
                         "xT", "in_done", "silu", "gate", "g_turned", "gT", "down_done", "y", "filled",
                         "may_gather", "accumulated"))
    in_loaded, down_loaded, y_stored = (
        [sem(f"{s}{i}") for i in range(GROUP)] for s in ("in_loaded", "down_loaded", "y_stored"))
    x_loaded, back_loaded = m.gather_sems[tag]
    UNITS = shared * TILES
    if shared:
        assert shared == GROUP
        s_in_ps = [bank(i)[:, 0:2 * F] for i in (0, 1)]
        s_gT_ps = bank(2)[0:rows, 0:chunks * P].rearrange("p (c t) -> p c t", t=P)
        s_y_ps = [bank(i)[:, 0:D] for i in (3, 7)]
        s_in, s_silu, s_gate, s_turned, s_gT, s_down, s_weighed, s_added = (
            sem(s) for s in ("s_in", "s_silu", "s_gate", "s_turned", "s_gT", "s_down", "s_weighed", "s_added"))
    EARLIER = 16 if shared else 0

    def source(name, e):
        return m.dram[tag + name][bass.ds(e, 1)].rearrange("o p x -> (o p) x")

    def shared_tensor(pe, u):
        if u < UNITS:
            t, e = divmod(u, shared)
            if t == 0:
                pe.wait_ge(in_loaded[e], 16)
            if u >= 2:
                pe.wait_ge(s_silu, u - 1)
            for k in range(KD):
                ins = nc.tensor.matmul(s_in_ps[u % 2], lhsT=m.hT[:, k, t * P:(t + 1) * P], rhs=w_in[e][:, k, :],
                                       start=(k == 0), stop=(k == KD - 1))
            ins.then_inc(s_in, 1)
        if 1 <= u <= UNITS:
            v = u - 1
            pe.wait_ge(s_gate, v + 1)
            if v:
                pe.wait_ge(s_gT, v)
            for c in range(chunks):
                ins = nc.tensor.transpose(s_gT_ps[:, c, :], gated[v % 2][:, c * rows:(c + 1) * rows], m.ident[:])
            ins.then_inc(s_turned, 1)
        if u >= 2:
            t, e = divmod(u - 2, shared)
            pe.wait_ge(s_gT, u - 1)
            if t == 0:
                pe.wait_ge(down_loaded[e], 16)
            if e == 0 and t >= 2:
                pe.wait_ge(s_weighed, t - 1)
            for c in range(chunks):
                ins = nc.tensor.matmul(s_y_ps[t % 2], lhsT=gatedT[u % 2][:, c, :], rhs=w_down[e][:, c, :],
                                       start=(e == 0 and c == 0), stop=(e == shared - 1 and c == chunks - 1))
            ins.then_inc(s_down, 1)

    def shared_scalar(act):
        act.wait_ge(shared_ready, 1)
        for u in range(UNITS + 3):
            if u < UNITS:
                act.wait_ge(s_in, u + 1)
                if u >= 2:
                    act.wait_ge(s_gate, u - 1)
                nc.scalar.activation(silu[u % 2][:], s_in_ps[u % 2][:, 0:F], ACT.Silu)
                nc.scalar.activation(up[u % 2][:], s_in_ps[u % 2][:, F:2 * F], ACT.Copy).then_inc(s_silu, 1)
            if 1 <= u <= UNITS:
                act.wait_ge(s_turned, u)
                if u >= 3:
                    act.wait_ge(s_down, u - 2)
                nc.scalar.activation(gatedT[(u - 1) % 2][:], s_gT_ps, ACT.Copy).then_inc(s_gT, 1)
            if u >= shared and u % shared == 2:
                t = u // shared - 1
                act.wait_ge(s_down, (t + 1) * shared)
                if t >= 2:
                    act.wait_ge(s_added, t - 1)
                nc.scalar.activation(shared_y[t % 2][:], s_y_ps[t % 2], ACT.Copy,
                                     scale=open_gate[:, t:t + 1]).then_inc(s_weighed, 1)

    def shared_gpsimd(pool):
        def add(t):
            pool.wait_ge(s_weighed, t + 1)
            nc.gpsimd.tensor_tensor(m.resid[:, t, :], shared_y[t % 2][:], m.resid[:, t, :], ALU.add).then_inc(s_added, 1)

        for u in range(UNITS):
            pool.wait_ge(s_silu, u + 1)
            if u >= 2:
                pool.wait_ge(s_turned, u - 1)
            nc.gpsimd.tensor_tensor(gated[u % 2][:], silu[u % 2][:], up[u % 2][:], ALU.mult).then_inc(s_gate, 1)
            if u >= shared and u % shared == 3:
                add(u // shared - 1)
        add(TILES - 1)

    def number_tokens(eng, ops, c):
        eng.wait_ge(blocks_ready, c + 1)
        ops.tensor_tensor(block_hot[c % 2][:], block_hot[c % 2][:],
                          token[:].unsqueeze(2).to_broadcast([P, TILES, BLOCKS]), ALU.mult).then_inc(tokens_ready, 1)

    def group_count(eng):
        eng.wait_ge(lists_ready, 2)
        return eng.value_load(more_turns[0:1, 0:1], min_val=0, max_val=GROUPS - FEWEST) + FEWEST

    with nc.Block(name=tag + "block") as block:
        @block.sync
        def _(sp):
            for e in range(shared):
                sp.dma_start(w_in[e][:].rearrange("p c x -> p (c x)"), source("w_in", routed + e)).then_inc(in_loaded[e], 16)
                sp.dma_start(w_down[e][:].rearrange("p c x -> p (c x)"), source("w_down", routed + e)).then_inc(
                    down_loaded[e], 16)
            sp.wait_ge(m.h_ready, TILES * (n + 1))
            sp.dma_start(h_rows.rearrange("(t p) d -> p t d", p=P), m.h[:]).then_inc(h_stored, 16)
            with sp.Fori(FEWEST, GROUPS) as i:
                sp.dma_start(y_groups[bass.ds(i, 1)].rearrange("o b p d -> p (o b) d"),
                             m.h[:, 0:GROUP, :]).then_inc(filled, 16)
            groups = group_count(sp)

            def step(base, s, first, last):
                e = sp.value_load(owners[0:1, bass.ds(base + s, 1)], min_val=0, max_val=E - 1)
                for w, name, used, loaded in ((w_in, "w_in", in_done, in_loaded), (w_down, "w_down", down_done, down_loaded)):
                    if first and shared:
                        sp.wait_ge(s_in if w is w_in else s_down, UNITS - shared + s + 1)
                    if not first:
                        sp.wait_ge(used, base + (s - GROUP + 1))
                    sp.dma_start(w[s][:].rearrange("p c x -> p (c x)"), source(name, e)).then_inc(loaded[s], 16)
            by_steps(sp, groups, step, 0)

        @block.gpsimd
        def _(pool):
            norm_gpsimd(m, pool, n)
            m.wait_weights(pool, "routing")
            if shared:
                shared_gpsimd(pool)
            else:
                for c in range(K):
                    number_tokens(pool, nc.gpsimd, c)
            groups = group_count(pool)
            pool.wait_ge(table_ready, 1)
            pool.wait_ge(h_stored, 16)

            def step(base, s, first, last):
                if s == 0:
                    if not first:
                        for k in range(GROUP):
                            pool.wait_ge(x_loaded[k], base * (16 // GROUP))
                    nc.gpsimd.tensor_copy(token_now[:], token_of[:, bass.ds(base, GROUP)]).then_inc(token_ready, GROUP)
                    pool.wait_ge(token_ready, base + GROUP)
                if not first:
                    pool.wait_ge(x_turned, base + (s - GROUP + 1))
                    pool.sem_inc(may_gather, 1)
                nc.gpsimd.indirect_dma_start(
                    x[s][:], None, h_rows, bass.IndirectOffsetOnAxis(ap=token_now[:, s:s + 1], axis=0)).then_inc(
                        x_loaded[s], 16)
            by_steps(pool, groups, step, 0)
            for s in range(GROUP):
                pool.wait_ge(y_stored[s], groups * 16 + 16)
            pool.sem_inc(may_gather, 1)
            for q in range(K * TILES):
                c, t = divmod(q, TILES)
                if c:
                    pool.wait_ge(accumulated, q - TILES + 1)
                nc.gpsimd.indirect_dma_start(
                    back[t][:], None, y_rows, bass.IndirectOffsetOnAxis(ap=slot_index[:, c, t:t + 1], axis=0)).then_inc(
                        back_loaded[t], 16)

        @block.tensor
        def _(pe):
            norm_tensor(m, pe, n)
            m.wait_weights(pe, tag)
            for t in range(TILES):
                if t % 4 == 0:
                    wait_hT(m, pe, j, half=t // 4)
                for k in range(KD):
                    ins = nc.tensor.matmul(logits[:, t, :], lhsT=m.hT[:, k, t * P:(t + 1) * P], rhs=router[:, k, :],
                                           start=(k == 0), stop=(k == KD - 1))
            ins.then_inc(routed_ready, 1)
            m.wait_weights(pe, "routing")

            def count():
                pe.wait_ge(goes_ready, 1)
                nc.tensor.matmul(rank, lhsT=m.w["earlier"][:], rhs=goes[:].rearrange("p t e -> p (t e)"),
                                 start=True, stop=False)
                nc.tensor.matmul(rank, lhsT=m.w["ones"][:], rhs=before[:, 0:TILES, :].rearrange("p t e -> p (t e)"),
                                 start=False, stop=True)
                nc.tensor.matmul(counts, lhsT=m.w["ones"][:], rhs=before[:, TILES, :], start=True,
                                 stop=True).then_inc(counted, 1)

            def list_owners():
                pe.wait_ge(owner_ready, 1)
                nc.tensor.matmul(owner_row, lhsT=m.w["ones"][:], rhs=owners_diag[:], start=True,
                                 stop=True).then_inc(owners_filled, 1)

            def list_tokens(c):
                pe.wait_ge(lanes_ready, c + 1)
                pe.wait_ge(tokens_ready, c + 1)
                for t in range(TILES):
                    ins = nc.tensor.matmul(table, lhsT=lane_hot[c % 2][:, t, :], rhs=block_hot[c % 2][:, t, :],
                                           start=(c + t == 0), stop=(c == K - 1 and t == TILES - 1))
                ins.then_inc(tabled, 1)

            for u in range(UNITS + 2 if shared else 0):
                if u == ROUTED_BY:
                    count()
                if u == ROUTED_BY + 4:
                    list_owners()
                shared_tensor(pe, u)
                if ROUTED_BY + 14 <= u < ROUTED_BY + 14 + K:
                    list_tokens(u - ROUTED_BY - 14)
            if shared:
                pe.wait_ge(s_weighed, TILES)
            else:
                count()
                list_owners()
                for c in range(K):
                    list_tokens(c)
            groups = group_count(pe)
            pe.wait_ge(table_ready, 1)

            def step(base, s, first, last):
                turn = lambda d: base * (16 // GROUP) + ((s - d) // GROUP + 1) * 16 + (EARLIER if d else 0)
                if not last:
                    pe.wait_ge(x_loaded[s % GROUP], turn(0))
                    if not first or s >= 2:
                        pe.wait_ge(xT_ready, base + (s - 1))
                    for k in range(KD):
                        ins = nc.tensor.transpose(xT_ps[s % 2][:, k, :], x[s % GROUP][:, k * P:(k + 1) * P], m.ident[:])
                    ins.then_inc(x_turned, 1)
                if (not first or s >= 1) and (not last or s < 1):
                    d = s - 1
                    pe.wait_ge(xT_ready, base + (d + 1))
                    pe.wait_ge(in_loaded[d % GROUP], turn(1))
                    if not first or d >= 2:
                        pe.wait_ge(gate_done, base + (d - 1))
                    for k in range(KD):
                        ins = nc.tensor.matmul(in_ps[d % 2], lhsT=xT[d % 2][:, k, :], rhs=w_in[d % GROUP][:, k, :],
                                               start=(k == 0), stop=(k == KD - 1))
                    ins.then_inc(in_done, 1)
                if (not first or s >= 2) and (not last or s < 2):
                    d = s - 2
                    pe.wait_ge(gate_done, base + (d + 1))
                    if not first or d >= 2:
                        pe.wait_ge(gT_ready, base + (d - 1))
                    for c in range(chunks):
                        ins = nc.tensor.transpose(gT_ps[d % 2][:, c, :], gated[d % 2][:, c * rows:(c + 1) * rows],
                                                  m.ident[:])
                    ins.then_inc(g_turned, 1)
                if not first or s >= 3:
                    d = s - 3
                    pe.wait_ge(gT_ready, base + (d + 1))
                    pe.wait_ge(down_loaded[d % GROUP], turn(3))
                    if not first or d >= 2:
                        pe.wait_ge(y_ready, base + d)
                    for c in range(chunks):
                        ins = nc.tensor.matmul(y_ps[d % 2], lhsT=gatedT[d % 2][:, c, :], rhs=w_down[d % GROUP][:, c, :],
                                               start=(c == 0), stop=(c == chunks - 1))
                    ins.then_inc(down_done, 1)
            by_steps(pe, groups, step, 3)

        @block.scalar
        def _(act):
            norm_scalar(m, act, j)
            act.wait_ge(less_max, 1)
            nc.scalar.activation(probs[:, :, 0:routed], probs[:, :, 0:routed], ACT.Exp).then_inc(exps, 1)
            if shared:
                gate = logits[:, :, routed:R].rearrange("p t o -> p (t o)")
                nc.scalar.activation(open_gate[:], gate, ACT.Sigmoid).then_inc(shared_ready, 1)
                shared_scalar(act)
            for s in range(GROUP):
                act.sem_inc(y_stored[s], 16)
            groups = group_count(act)
            act.wait_ge(filled, (GROUPS - FEWEST) * 16)

            def step(base, s, first, last):
                if not last:
                    act.wait_ge(x_turned, base + (s + 1))
                    if not first or s >= 2:
                        act.wait_ge(in_done, base + (s - 1))
                    nc.scalar.activation(xT[s % 2][:], xT_ps[s % 2], ACT.Copy).then_inc(xT_ready, 1)
                if (not first or s >= 1) and (not last or s < 1):
                    d = s - 1
                    act.wait_ge(in_done, base + (d + 1))
                    if not first or d >= 2:
                        act.wait_ge(gate_done, base + (d - 1))
                    nc.scalar.activation(silu[d % 2][:], in_ps[d % 2][:, 0:F], ACT.Silu).then_inc(silu_done, 1)
                if not first:
                    d = s - 4
                    act.wait_ge(y_ready, base + (d + 2))
                    dst = y_rows.rearrange("(b p) d -> b p d", p=P)[bass.ds(base + d, 1)].rearrange("o p d -> (o p) d")
                    act.dma_start(dst, y[d % GROUP][:]).then_inc(y_stored[d % GROUP], 16)
            by_steps(act, groups, step, 4)

        @block.vector
        def _(dve):
            o = m.dve_order

            def pick(src, dst):
                for c in range(K):
                    o.mark(nc.vector.scalar_tensor_tensor(out=picked[c % 2][:], in0=number[:], scalar=float(c + 1),
                                                          in1=src[:], op0=ALU.is_equal, op1=ALU.mult))
                    if c:
                        dve.wait_ge(o.sem, o.made - 1)
                        o.mark(nc.vector.tensor_reduce(dst[:, c - 1, :], picked[(c - 1) % 2][:], AX_X, ALU.add))
                        o.wait(dve)
                o.wait(dve)
                o.link(dve, nc.vector.tensor_reduce(dst[:, K - 1, :], picked[(K - 1) % 2][:], AX_X, ALU.add))

            norm_vector(m, dve, n)
            m.wait_weights(dve, "routing")
            m.wait_weights(dve, "consts")
            o.mark(nc.vector.memset(probs[:, :, routed:], -1.0))
            o.mark(nc.vector.memset(before[:, 0, :], 0.0))
            o.mark(nc.vector.tensor_scalar(limits[:], iota[:, 0:TILES], float(P), None, ALU.mult))
            o.mark(nc.vector.tensor_scalar(earlier[:], iota[:, 0:TILES], float(K), None, ALU.mult))
            o.mark(nc.vector.tensor_scalar(turns[:], iota[:, 0:GROUPS], float(GROUP), None, ALU.mult))
            dve.wait_ge(routed_ready, 1)
            o.link(dve, nc.vector.tensor_reduce(row[:], logits[:, :, 0:routed], AX_X, ALU.max))
            nc.vector.tensor_tensor(probs[:, :, 0:routed], logits[:, :, 0:routed],
                                    row[:].unsqueeze(2).to_broadcast([P, TILES, routed]), ALU.subtract).then_inc(less_max, 1)
            dve.wait_ge(exps, 1)
            o.link(dve, nc.vector.tensor_reduce(row[:], probs[:, :, 0:routed], AX_X, ALU.add))
            o.link(dve, nc.vector.reciprocal(row[:], row[:]))
            o.link(dve, nc.vector.tensor_tensor(probs[:, :, 0:routed], probs[:, :, 0:routed],
                                                row[:].unsqueeze(2).to_broadcast([P, TILES, routed]), ALU.mult))
            for t in range(TILES):
                o.mark(nc.vector.max(best[:, t, :], probs[:, t, :]))
            o.wait(dve)
            o.link(dve, nc.vector.memset(best[:, :, top:], -1.0))
            for t in range(TILES):
                o.mark(nc.vector.match_replace(out=rest[:, t, :], in_to_replace=best[:, t, :], in_values=probs[:, t, :],
                                               imm_value=GONE))
            o.wait(dve)
            o.link(dve, nc.vector.tensor_scalar(goes[:, :, 0:routed], rest[:, :, 0:routed], GONE, None, ALU.is_equal))
            for t in range(TILES):
                o.link(dve, nc.vector.tensor_tensor(before[:, t + 1, :], before[:, t, :], goes[:, t, :], ALU.add))
            dve.sem_inc(goes_ready, 1)
            o.link(dve, nc.vector.tensor_tensor(combine[:, :, 0:routed], probs[:, :, 0:routed], goes[:, :, 0:routed],
                                                ALU.mult))
            flat = lambda a: a[:].rearrange("p t e -> p (t e)")
            o.link(dve, nc.vector.tensor_tensor_scan(flat(number), flat(goes), flat(goes), 0.0, ALU.add, ALU.max))
            o.link(dve, nc.vector.tensor_tensor(number[:], number[:], earlier[:].unsqueeze(2).to_broadcast([P, TILES, E]),
                                                ALU.subtract))
            o.link(dve, nc.vector.tensor_tensor(number[:], number[:], goes[:], ALU.mult))
            dve.wait_ge(counted, 1)
            o.link(dve, nc.vector.tensor_tensor(over[:], counts.unsqueeze(2).to_broadcast([P, E, TILES]),
                                                limits[:].unsqueeze(1).to_broadcast([P, E, TILES]), ALU.is_gt))
            o.link(dve, nc.vector.tensor_reduce(blocks[:], over[:], AX_X, ALU.add))
            o.link(dve, nc.vector.tensor_tensor_scan(ends[:], blocks[:], blocks[:], 0.0, ALU.add, ALU.max))
            o.link(dve, nc.vector.tensor_scalar(starts[:], ends[:], token[:, 0:1], None, ALU.is_le))
            o.link(dve, nc.vector.tensor_reduce(owner[:], starts[:], AX_X, ALU.add))
            o.link(dve, nc.vector.tensor_scalar(owner[:], owner[:], float(E - 1), None, ALU.min))
            nc.vector.tensor_scalar(owners_diag[:], m.ident[:], owner[:, 0:1], None, ALU.mult).then_inc(owner_ready, 1)
            o.link(dve, nc.vector.tensor_scalar(turns[:], turns[:], ends[:, E - 1:E], None, ALU.is_lt))
            o.link(dve, nc.vector.tensor_reduce(groups_f[:], turns[:], AX_X, ALU.add))
            o.link(dve, nc.vector.tensor_scalar(more_turns[:, 0:1], groups_f[0:1, :], float(FEWEST), None, ALU.subtract))
            dve.sem_inc(lists_ready, 1)
            dve.wait_ge(owners_filled, 1)
            nc.vector.tensor_copy(owners[:], owner_row[0:1, :]).then_inc(lists_ready, 1)
            o.link(dve, nc.vector.tensor_tensor(starts[:], ends[:], blocks[:], ALU.subtract))
            o.link(dve, nc.vector.tensor_scalar(starts[:], starts[:], float(P), None, ALU.mult))
            o.link(dve, nc.vector.tensor_tensor(slots[:], rank.rearrange("p (t e) -> p t e", e=E),
                                                starts[:].unsqueeze(1).to_broadcast([P, TILES, E]), ALU.add))
            pick(slots, slot)
            o.link(dve, nc.vector.tensor_scalar(block_of[:], slot[:], 1.0 / P, -(P - 1) / (2.0 * P), ALU.mult, ALU.add))
            o.link(dve, nc.vector.tensor_scalar(block_of[:], block_of[:], ROUND, None, ALU.add))
            o.link(dve, nc.vector.tensor_scalar(block_of[:], block_of[:], ROUND, None, ALU.subtract))
            o.link(dve, nc.vector.scalar_tensor_tensor(out=lane_of[:], in0=block_of[:], scalar=-float(P), in1=slot[:],
                                                       op0=ALU.mult, op1=ALU.add))
            for c in range(K):
                if c >= 2:
                    dve.wait_ge(tabled, c - 1)
                nc.vector.tensor_tensor(block_hot[c % 2][:], iota[:, 0:BLOCKS].unsqueeze(1).to_broadcast([P, TILES, BLOCKS]),
                                        block_of[:, c, :].unsqueeze(2).to_broadcast([P, TILES, BLOCKS]),
                                        ALU.is_equal).then_inc(blocks_ready, 1)
                if shared:
                    number_tokens(dve, nc.vector, c)
                nc.vector.tensor_tensor(lane_hot[c % 2][:], iota[:].unsqueeze(1).to_broadcast([P, TILES, P]),
                                        lane_of[:, c, :].unsqueeze(2).to_broadcast([P, TILES, P]),
                                        ALU.is_equal).then_inc(lanes_ready, 1)
            dve.wait_ge(tabled, K)
            nc.vector.tensor_copy(token_of[:], table).then_inc(table_ready, 1)
            o.link(dve, nc.vector.tensor_copy(slot_index[:], slot[:]))
            if normalize:
                o.link(dve, nc.vector.tensor_reduce(row[:], combine[:, :, 0:routed], AX_X, ALU.add))
                if floor is not None:
                    o.link(dve, nc.vector.tensor_scalar(row[:], row[:], floor, None, ALU.max))
                o.link(dve, nc.vector.reciprocal(row[:], row[:]))
                o.link(dve, nc.vector.tensor_tensor(combine[:, :, 0:routed], combine[:, :, 0:routed],
                                                    row[:].unsqueeze(2).to_broadcast([P, TILES, routed]), ALU.mult))
            pick(combine, weight)
            groups = group_count(dve)
            dve.sem_inc(y_ready, 1)

            def step(base, s, first, last):
                if (not first or s >= 2) and (not last or s < 2):
                    d = s - 2
                    dve.wait_ge(g_turned, base + (d + 1))
                    if not first or d >= 2:
                        dve.wait_ge(down_done, base + (d - 1))
                    nc.vector.tensor_copy(gatedT[d % 2][:], gT_ps[d % 2]).then_inc(gT_ready, 1)
                if (not first or s >= 1) and (not last or s < 1):
                    d = s - 1
                    dve.wait_ge(silu_done, base + (d + 1))
                    if not first or d >= 2:
                        dve.wait_ge(g_turned, base + (d - 1))
                    nc.vector.tensor_tensor(gated[d % 2][:], silu[d % 2][:], in_ps[d % 2][:, F:2 * F],
                                            ALU.mult).then_inc(gate_done, 1)
                if not first or s >= 3:
                    d = s - 3
                    dve.wait_ge(down_done, base + (d + 1))
                    if not first:
                        dve.wait_ge(y_stored[d % GROUP], base * (16 // GROUP) + (d // GROUP + 1) * 16)
                    nc.vector.tensor_copy(y[d % GROUP][:], y_ps[d % 2]).then_inc(y_ready, 1)
            by_steps(dve, groups, step, 3)
            with dve.Fori(0, K) as c:
                for t in range(TILES):
                    dve.wait_ge(back_loaded[t], c * 16 + 16)
                    dve.wait_ge(accumulated, c * TILES)
                    nc.vector.scalar_tensor_tensor(
                        out=m.resid[:, t, :], in0=back[t][:], scalar=weight[:, bass.ds(c, 1), t], in1=m.resid[:, t, :],
                        op0=ALU.mult, op1=ALU.add).then_inc(accumulated, 1)



def rotate(m, dve, jobs, name, swapped, cos, sin, tmp, out, bias=(None, None)):
    nc, o = m.nc, m.dve_order
    for x, table, t, b in ((name, cos, tmp[0], bias[0]), (swapped, sin, tmp[1], bias[1])):
        jobs.wait_filled(dve, x)
        src = jobs.pair(x).rearrange("p (b s) -> p b s", s=S)
        if b is None:
            ins = nc.vector.tensor_tensor(t, src, table, ALU.mult)
        else:
            ins = nc.vector.scalar_tensor_tensor(out=t, in0=src, scalar=b, in1=table, op0=ALU.add, op1=ALU.mult)
        ins.then_inc(jobs.empty(x), 1)
        dve.wait_ge(jobs.empty(x), jobs.takers[:jobs.at(x) + 1].count("vector"))
    o.link(dve, nc.vector.tensor_tensor(out, tmp[0], tmp[1], ALU.add))



class Attention:

    SCORES = 4
    Q_PARTS = (0, 0, 1, 0, 2, 1)
    K_PARTS = (0, 1, 0, 2, 0, 1)

    def __init__(self, m, tag, heads, causal):
        self.m, self.causal = m, causal
        self.hpc = heads // KD
        self.hd = D // heads
        self.units = 2 * heads
        self.groups = 2 * KD
        self.rows = len(self.Q_PARTS) * self.hd
        self.side = 1 if self.rows <= 64 else 0
        self.tiles = heads // (1 + self.side)
        sb, sem = m.sb, lambda s: m.sem(tag + s)
        self.rotated = [sb(tag + f"rotated{i}", [P, T]) for i in range(2)]
        self.residue = sb(tag + "residue", [P, T])
        self.parts = [sb(tag + f"parts{i}", [P, 3, T], BF16) for i in range(2)]
        self.packed = {x: [sb(tag + f"{x}_packed{u}", [P, self.tiles, S], BF16) for u in range(2)] for x in "qk"}
        self.v = sb(tag + "v", [P, B * KD * 2 * P + P])
        self.prob = [sb(tag + f"prob{i}", [P, 2, S]) for i in range(self.SCORES)]
        self.probT = [sb(tag + f"probT{i}", [P, 2, 2, P]) for i in range(2)]
        self.neg_max = [sb(tag + f"neg_max{i}", [P, 2]) for i in range(self.SCORES)]
        self.sums = [sb(tag + f"sums{i}", [P, 2, self.hpc]) for i in range(KD)]
        self.inv = [sb(tag + f"inv{i}", [P, 2, self.hpc]) for i in range(KD)]
        self.out = sb(tag + "out", [P, B, KD, 2 * P])
        self.scratch = m.nc.dram_tensor(tag + "parts", (2, 3, KD, P, T), BF16).ap()
        if causal:
            self.ident, self.after = (sb(tag + x, [P, P], BF16) for x in ("ident", "after"))
        (self.inputs, self.rot_ready, self.high, self.residue_ready, self.middle, self.split, self.scored,
         self.max_ready, self.exp_done, self.turned, self.probT_ready, self.mixed, self.inv_ready, self.out_ready,
         self.outT_filled, self.outT_ready) = (
            sem(s) for s in ("inputs", "rot_ready", "high", "residue", "middle", "split", "scored",
                             "max_ready", "exp_done", "turned", "probT_ready", "mixed", "inv_ready", "out_ready",
                             "outT_filled", "outT_ready"))
        self.stored = [sem(f"stored{i}") for i in range(2)]
        self.loaded = [[sem(f"loaded{u}{c}") for c in range(KD)] for u in range(2)]

    def values(self):
        return self.v[:, 0:B * KD * 2 * P].rearrange("p (b c k f) -> p b c k f", b=B, c=KD, f=P)

    def bank(self, i):
        return self.m.psum[:, i * 512:(i + 1) * 512]

    def place(self, c, hh):
        return (64 * c, hh) if self.side else (0, c * self.hpc + hh)

    def split_scalar(self, act, i, scale):
        x, parts = self.rotated[i % 2], self.parts[i % 2]
        act.wait_ge(self.rot_ready, i + 1)
        if i >= 2:
            act.wait_ge(self.stored[i % 2], i // 2 * 16)
        self.m.nc.scalar.activation(parts[:, 0, :], x[:], ACT.Copy, scale=scale).then_inc(self.high, 1)
        act.wait_ge(self.residue_ready, i + 1)
        self.m.nc.scalar.activation(parts[:, 1, :], self.residue[:], ACT.Copy).then_inc(self.middle, 1)

    def split_vector(self, dve, i, scale):
        nc, x, parts = self.m.nc, self.rotated[i % 2], self.parts[i % 2]
        dve.wait_ge(self.high, i + 1)
        if i:
            dve.wait_ge(self.split, i)
        nc.vector.scalar_tensor_tensor(out=self.residue[:], in0=x[:], scalar=scale, in1=parts[:, 0, :], op0=ALU.mult,
                                       op1=ALU.subtract).then_inc(self.residue_ready, 1)
        dve.wait_ge(self.middle, i + 1)
        nc.vector.tensor_tensor(parts[:, 2, :], self.residue[:], parts[:, 1, :], ALU.subtract).then_inc(self.split, 1)

    def pack(self, sp):
        def load(u, c, seq):
            base, tile = self.place(c, 0)
            for x, order in ((0, self.Q_PARTS), (1, self.K_PARTS)):
                for r, part in enumerate(order):
                    rows = slice(base + r * self.hd, base + (r + 1) * self.hd)
                    src = self.scratch[x, part, c].rearrange("(h f) (b s) -> f h b s", f=self.hd, s=S)
                    sp.dma_start(self.packed["qk"[x]][u][rows, tile:tile + self.hpc, :],
                                 src[:, :, bass.ds(seq, 1), :].rearrange("f h o s -> f h (o s)")).then_inc(
                                     self.loaded[u][c], 16)

        for c in range(KD):
            for x in range(2):
                sp.wait_ge(self.split, KD * c + x + 1)
                sp.dma_start(self.scratch[x, :, c].rearrange("k p t -> p k t"), self.parts[x][:]).then_inc(
                    self.stored[x], 16)
            for stored in self.stored:
                sp.wait_ge(stored, (c + 1) * 16)
            load(0, c, 0)
        for c in range(KD):
            load(1, c, 1)
        with sp.Fori(1, B // 2) as i:
            for u in range(2):
                sp.wait_ge(self.scored, i * self.units + (u - 1) * (self.units // 2))
                for c in range(KD):
                    load(u, c, i * 2 + u)

    def tensor(self, pe):
        nc, m, n, hpc = self.m.nc, self.m, self.units, self.hpc
        pe.sem_inc(self.turned, self.SCORES)
        pe.sem_inc(self.mixed, 2)
        with pe.Fori(0, B // 2) as i:
            def score(h):
                g, hh = divmod(h, hpc)
                u, c = divmod(g, KD)
                if hh == 0:
                    pe.wait_ge(self.loaded[u][c], i * (32 * len(self.Q_PARTS)) + 32 * len(self.Q_PARTS))
                pe.wait_ge(self.exp_done, i * n + (h + 1))
                out = self.bank(h % self.SCORES)
                base, tile = self.place(c, hh)
                q, k = (self.packed[x][u][base:base + self.rows, tile, :] for x in "qk")
                for qt in range(2):
                    lhs = q[:, qt * P:(qt + 1) * P]
                    if not self.causal:
                        ins = nc.tensor.matmul(out[:, qt * S:(qt + 1) * S], lhsT=lhs, rhs=k, start=True, stop=True)
                        continue
                    for kt in range(qt + 1):
                        cols = out[:, qt * S + kt * P:qt * S + (kt + 1) * P]
                        ins = nc.tensor.matmul(cols, lhsT=lhs, rhs=k[:, kt * P:(kt + 1) * P], start=True, stop=kt < qt)
                    ins = nc.tensor.matmul(cols, lhsT=self.ident[:], rhs=self.after[:], start=False, stop=True)
                ins.then_inc(self.scored, 1)

            def turn(h):
                pe.wait_ge(self.exp_done, i * n + (h + 1 + self.SCORES))
                pe.wait_ge(self.probT_ready, i * n + (h + 1))
                for kt in range(2):
                    for qt in range(2):
                        if self.causal and kt > qt:
                            continue
                        at = (kt * 2 + qt) * P
                        ins = nc.tensor.transpose(self.bank(4 + h % 2)[:, at:at + P],
                                                  self.prob[h % self.SCORES][:, qt, kt * P:(kt + 1) * P], m.ident[:])
                ins.then_inc(self.turned, 1)

            def mix(h):
                g, hh = divmod(h, hpc)
                u, c = divmod(g, KD)
                pe.wait_ge(self.probT_ready, i * n + (h + 3))
                if hh == 0:
                    pe.wait_ge(self.out_ready, i * self.groups + (g + 1))
                for qt in range(2):
                    kts = range(qt + 1) if self.causal else range(2)
                    for kt in kts:
                        v = self.v[:, bass.ds(i * (2 * KD * 2 * P) + ((u * KD + c) * 2 + kt) * P + hh * self.hd, P)]
                        at = qt * 2 * P + hh * self.hd
                        ins = nc.tensor.matmul(self.bank(6 + c)[:, at:at + P], lhsT=self.probT[h % 2][:, kt, qt, :],
                                               rhs=v, start=(kt == 0), stop=(kt == kts[-1]))
                ins.then_inc(self.mixed, 1)

            for h in range(n + 3):
                if h < n:
                    score(h)
                if 2 <= h <= n + 1:
                    turn(h - 2)
                if h >= 3:
                    mix(h - 3)

    def scalar(self, act):
        nc, n, hpc = self.m.nc, self.units, self.hpc
        act.sem_inc(self.exp_done, self.SCORES)
        with act.Fori(0, B // 2) as i:
            for h in range(n):
                g, hh = divmod(h, hpc)
                if hh == 0:
                    act.wait_ge(self.inv_ready, i * self.groups + (g + 1))
                act.wait_ge(self.max_ready, i * n + (h + 1))
                act.wait_ge(self.turned, i * n + (h + 1))
                for qt in range(2):
                    keys = (qt + 1) * P if self.causal else S
                    ins = nc.scalar.activation(self.prob[h % self.SCORES][:, qt, 0:keys],
                                               self.bank(h % self.SCORES)[:, qt * S:qt * S + keys], ACT.Exp,
                                               bias=self.neg_max[h % self.SCORES][:, qt:qt + 1],
                                               accum_out=self.sums[g % 2][:, qt, hh:hh + 1])
                ins.then_inc(self.exp_done, 1)

    def vector(self, dve):
        nc, n, hpc = self.m.nc, self.units, self.hpc
        dve.sem_inc(self.out_ready, KD)
        dve.sem_inc(self.inv_ready, KD)
        dve.sem_inc(self.probT_ready, 2)
        with dve.Fori(0, B // 2) as i:
            def maximum(h):
                dve.wait_ge(self.scored, i * n + (h + 1))
                dve.wait_ge(self.exp_done, i * n + (h + 1))
                bank, neg_max = self.bank(h % self.SCORES), self.neg_max[h % self.SCORES]
                if self.causal:
                    for qt in range(2):
                        ins = nc.vector.tensor_reduce(neg_max[:, qt:qt + 1], bank[:, qt * S:qt * S + (qt + 1) * P], AX_X,
                                                      ALU.max, negate=True)
                else:
                    ins = nc.vector.tensor_reduce(neg_max[:], bank.rearrange("p (q k) -> p q k", k=S), AX_X, ALU.max,
                                                  negate=True)
                ins.then_inc(self.max_ready, 1)

            def move(h):
                dve.wait_ge(self.turned, i * n + (h + 1 + self.SCORES))
                dve.wait_ge(self.mixed, i * n + (h + 1))
                bank = self.bank(4 + h % 2)
                dst = self.probT[h % 2][:].rearrange("p k q s -> p (k q s)")
                if self.causal:
                    nc.vector.tensor_copy(dst[:, 0:2 * P], bank[:, 0:2 * P])
                    ins = nc.vector.tensor_copy(dst[:, 3 * P:4 * P], bank[:, 3 * P:4 * P])
                else:
                    ins = nc.vector.tensor_copy(dst, bank)
                ins.then_inc(self.probT_ready, 1)

            def normalize(g):
                u, c = divmod(g, KD)
                dve.wait_ge(self.exp_done, i * n + ((g + 1) * hpc + self.SCORES))
                nc.vector.reciprocal(self.inv[c][:], self.sums[c][:]).then_inc(self.inv_ready, 1)
                dve.wait_ge(self.inv_ready, i * self.groups + (g + 1 + KD))
                dve.wait_ge(self.mixed, i * n + ((g + 1) * hpc + 2))
                out = self.out[:, bass.ds(i * 2 + u, 1), c, :].rearrange("p o (q x d) -> p (o q) x d", q=2, d=self.hd)
                src = self.bank(6 + c).rearrange("p (q w) -> p q w", q=2)[:, :, 0:P].rearrange(
                    "p q (x d) -> p q x d", d=self.hd)
                scale = self.inv[c][:].unsqueeze(3).to_broadcast([P, 2, hpc, self.hd])
                nc.vector.tensor_tensor(out, src, scale, ALU.mult).then_inc(self.out_ready, 1)

            for h in range(n + 2):
                if h < n:
                    maximum(h)
                if h >= 2:
                    move(h - 2)
                if h > hpc and h % hpc == 4:
                    normalize(h // hpc - 1)
            normalize(self.groups - 1)


def softmax_attention(m, n, j, tag, heads, causal):
    nc = m.nc
    self_attn = causal
    w = lambda name: m.w[tag + name]
    a = Attention(m, tag, heads, causal)
    scales = (a.hd ** -0.5, 1.0) * KD
    names = [] if self_attn else ["angle"]
    for c in range(KD):
        names += [f"q{c}", f"q{c}s", f"k{c}", f"k{c}s"]
    jobs = Jobs(m, tag + "in", 2, [(x, "vector") for x in names] + [("v0", "scalar"), ("v1", "scalar")])
    ends = Jobs(m, tag + "end", 2, [("out0", "vector"), ("out1", "vector")])
    tmp = [m.sb(tag + f"rot{i}", [P, B, S]) for i in range(2)]
    if self_attn:
        tables = [w(x)[:].unsqueeze(1).to_broadcast([P, B, S]) for x in ("cos", "sin")]
    else:
        turns = [m.sb(tag + f"turns{i}", [P, T]) for i in range(2)]
        whole = a.rotated
        tables = [t[:].rearrange("p (b s) -> p b s", s=S) for t in turns]
        turns_ready, table_ready = m.sem(tag + "turns"), m.sem(tag + "table")
    with nc.Block(name=tag + "block") as block:
        @block.sync
        def _(sp):
            a.pack(sp)

        @block.gpsimd
        def _(pool):
            norm_gpsimd(m, pool, n)
            nc.gpsimd.memset(a.v[:, B * KD * 2 * P:], 0.0).then_inc(a.inputs, 1)

        @block.tensor
        def _(pe):
            norm_tensor(m, pe, n)
            m.wait_weights(pe, tag)
            hT = feature_rhs(m.hT)
            keys = hT if self_attn else lambda k, cols: m.ctxT[:, cols]
            kc = KD if self_attn else 1
            if not self_attn:
                project(m, pe, jobs, "angle", lambda k: w("freq")[:], lambda k, cols: w("pos")[:, cols], 1)
            for c in range(KD):
                project(m, pe, jobs, f"q{c}", wcols(w("q"), c), hT, KD, turn=None if c else j)
                project(m, pe, jobs, f"q{c}s", wcols(w("q"), KD + c), hT, KD)
                project(m, pe, jobs, f"k{c}", wcols(w("k"), c), keys, kc)
                project(m, pe, jobs, f"k{c}s", wcols(w("k"), KD + c), keys, kc)
            src = m.hT if self_attn else m.ctxT[:].unsqueeze(1)
            project_tokens(m, pe, jobs, ("v0", "v1"), lambda k, t: src[:, k, t * P:(t + 1) * P],
                           lambda k, t: w("v")[:, k, :], kc)
            pe.wait_ge(a.inputs, 4)
            a.tensor(pe)
            pe.wait_ge(a.out_ready, KD + B * KD)
            for q in range(2):
                for t in range(4 * q, 4 * q + 4):
                    for c in range(KD):
                        ins = nc.tensor.transpose(m.pair(c)[:, t * P:(t + 1) * P], a.out[:, t // 2, c, t % 2 * P:(t % 2 + 1) * P],
                                                  m.ident[:])
                ins.then_inc(a.outT_filled, 1)
            pe.wait_ge(a.outT_ready, 4)
            project_tokens(m, pe, ends, ("out0", "out1"), lambda k, t: m.hT[:, k, t * P:(t + 1) * P],
                           lambda k, t: w("o")[:, k, :], KD)

        @block.scalar
        def _(act):
            norm_scalar(m, act, j)
            if not self_attn:
                act.wait_ge(turns_ready, 2)
                for i in range(2):
                    nc.scalar.activation(turns[i][:], turns[i][:], ACT.Sin, scale=SIN_SCALE).then_inc(table_ready, 1)
            for i, scale in enumerate(scales):
                a.split_scalar(act, i, scale)
            for q in range(2):
                name = f"v{q}"
                jobs.wait_filled(act, name)
                for b in range(2):
                    for qt in range(2):
                        src = jobs.pair(name)[:, (2 * b + qt) * D:(2 * b + qt + 1) * D].rearrange("p (c f) -> p c f", c=KD)
                        ins = nc.scalar.activation(a.values()[:, 2 * q + b, :, qt, :], src, ACT.Copy)
                ins.then_inc(jobs.empty(name), 1)
            act.wait_ge(jobs.emptied["scalar"], 2)
            act.sem_inc(a.inputs, 1)
            a.scalar(act)
            for q in range(2):
                act.wait_ge(a.outT_filled, q + 1)
                for c in range(KD):
                    cols = slice(q * HALF, (q + 1) * HALF)
                    nc.scalar.activation(m.hT[:, c, cols], m.pair(c)[:, cols], ACT.Copy).then_inc(a.outT_ready, 1)

        @block.vector
        def _(dve):
            o = m.dve_order
            norm_vector(m, dve, n)
            m.wait_weights(dve, tag)
            if self_attn:
                nc.vector.tensor_copy(a.ident[:], m.ident[:])
                o.mark(nc.vector.tensor_copy(a.after[:], m.w["causal"][:]))
            if not self_attn:
                jobs.wait_filled(dve, "angle")
                ps = jobs.pair("angle")
                o.mark(nc.vector.tensor_scalar(turns[0][:], ps, 0.25, None, ALU.add))
                nc.vector.tensor_copy(turns[1][:], ps).then_inc(jobs.empty("angle"), 1)
                dve.wait_ge(jobs.emptied["vector"], 1)
                for i in range(2):
                    o.mark(nc.vector.tensor_scalar(whole[i][:], turns[i][:], ROUND, -ROUND, ALU.add, ALU.add))
                o.wait(dve)
                for i in range(2):
                    nc.vector.tensor_tensor(turns[i][:], turns[i][:], whole[i][:], ALU.subtract).then_inc(turns_ready, 1)
                dve.wait_ge(table_ready, 2)
            for i, scale in enumerate(scales):
                x = ("q", "k")[i % 2] + str(i // 2)
                if i >= 2:
                    dve.wait_ge(a.split, i - 1)
                rotate(m, dve, jobs, x, x + "s", tables[0], tables[1], [t[:] for t in tmp],
                       a.rotated[i % 2][:].rearrange("p (b s) -> p b s", s=S))
                dve.sem_inc(a.rot_ready, 1)
                a.split_vector(dve, i, scale)
            dve.sem_inc(a.inputs, 2)
            a.vector(dve)
            add_tokens(m, dve, ends, ("out0", "out1"), bias=None if self_attn else w("o_b")[:])



def feature_attention(m, n, j):
    nc = m.nc
    tag = "l2a_"
    w = lambda name: m.w[tag + name]
    HPC, HD = 8, 16
    chunks = [("q", 0), ("q", 1), ("k", 0)]
    jobs = Jobs(m, tag + "in", 2, [(f"{x}{c}{s}", "vector") for x, c in chunks for s in ("", "s")]
                + [("v", "vector"), ("norm", "scalar")] + [(f"p{x}{c}", "vector") for x, c in chunks]
                + [("t0", "scalar"), ("t1", "scalar"), ("out0", "vector"), ("out1", "vector")])
    tmp = [m.sb(tag + f"rot{i}", [P, B, S]) for i in range(2)]
    x = {f"{k}{c}": m.sb(tag + f"{k}{c}", [P, T]) for k, c in chunks}
    sq = {f"{k}{c}": m.sb(tag + f"sq_{k}{c}", [P, T]) for k, c in chunks}
    feats = sq
    v = m.sb(tag + "v", [P, TILES, P])
    norm = m.sb(tag + "norm", [P, len(chunks), TILES, HPC])
    whole = m.sb(tag + "whole", [P, T])
    pair_prod = [m.sb(tag + f"pair_prod{c}", [P, HPC, HPC, HD]) for c in range(KD)]
    value_prod = [m.sb(tag + f"value_prod{c}", [P, HPC, HD, HPC]) for c in range(KD)]
    weight = [m.sb(tag + f"weight{c}", [P, HPC, HPC]) for c in range(KD)]
    att = m.sb(tag + "att", [P, TILES, D])
    (rotated, turns_ready, feats_ready, v_ready, pair_done, weight_done, value_done, att_done) = (
        m.sem(tag + s) for s in ("rotated", "turns", "feats", "v_ready", "pair", "weight", "value", "att"))

    def head_products(eng, ops, c, t, step, done):
        if step == 0:
            q = feats[f"q{c}"][:, t * P:(t + 1) * P].rearrange("p (h f) -> p h f", f=HD)
            k = feats["k0"][:, t * P:(t + 1) * P].rearrange("p (h f) -> p h f", f=HD)
            ops.tensor_tensor(pair_prod[c][:], q.unsqueeze(1).to_broadcast([P, HPC, HPC, HD]),
                              k.unsqueeze(2).to_broadcast([P, HPC, HPC, HD]), ALU.mult).then_inc(done, 1)
        else:
            g = weight[c][:].rearrange("p k q -> p q k").unsqueeze(2).to_broadcast([P, HPC, HD, HPC])
            vt = v[:, t, :].rearrange("p (k d) -> p d k", d=HD).unsqueeze(1).to_broadcast([P, HPC, HD, HPC])
            ops.tensor_tensor(value_prod[c][:], g, vt, ALU.mult).then_inc(done, 1)

    pool_pair, pool_value = m.sem(tag + "pool_pair"), m.sem(tag + "pool_value")
    stored = [m.sem(tag + f"stored{b}") for b in range(B)]
    att_back = m.sem(tag + "att_back")
    scratch = nc.dram_tensor(tag + "scratch", (B, 2 * HPC, S, HD), F32).ap()
    with nc.Block(name=tag + "block") as block:
        @block.sync
        def _(sp):
            for t in range(TILES):
                sp.wait_ge(att_done, 2 * t + 2)
                dst = scratch[t // 2, :, t % 2 * P:(t % 2 + 1) * P, :].rearrange("h s d -> s h d")
                sp.dma_start(dst, att[:, t, :].rearrange("p (h d) -> p h d", d=HD)).then_inc(stored[t // 2], 16)
            rows = scratch.rearrange("b h (s r) d -> b (h s) (r d)", r=HD).rearrange("b (q p) f -> b p q f", p=P)
            for b in range(B):
                sp.wait_ge(stored[b], 32)
                sp.dma_start(m.h[:, 2 * b:2 * b + 2, :], rows[b]).then_inc(att_back, 16)

        @block.gpsimd
        def _(pool):
            norm_gpsimd(m, pool, n)
            pool.wait_ge(feats_ready, 3)
            pool.wait_ge(v_ready, 1)
            head_products(pool, nc.gpsimd, 1, 0, 0, pool_pair)
            for t in range(TILES):
                if t + 1 < TILES:
                    pool.wait_ge(weight_done, 2 * t + 2)
                    head_products(pool, nc.gpsimd, 1, t + 1, 0, pool_pair)
                pool.wait_ge(weight_done, 2 * t + 2)
                if t:
                    pool.wait_ge(att_done, 2 * t)
                head_products(pool, nc.gpsimd, 1, t, 1, pool_value)

        @block.tensor
        def _(pe):
            norm_tensor(m, pe, n)
            m.wait_weights(pe, tag)
            hT = feature_rhs(m.hT)
            for i, (k, c) in enumerate(chunks):
                half = w(k)[:].shape[2] // (2 * P)
                project(m, pe, jobs, f"{k}{c}", wcols(w(k), c), hT, KD, turn=None if i else j)
                project(m, pe, jobs, f"{k}{c}s", wcols(w(k), half + c), hT, KD)
            jobs.wait_room(pe, "v")
            for t in range(TILES):
                for k in range(KD):
                    ins = nc.tensor.matmul(jobs.pair("v")[:, t * P:(t + 1) * P], lhsT=m.hT[:, k, t * P:(t + 1) * P],
                                           rhs=w("v")[:, k, :], start=(k == 0), stop=(k == KD - 1))
            ins.then_inc(jobs.filled, 1)
            jobs.wait_room(pe, "norm")
            for i, (k, c) in enumerate(chunks):
                pe.wait_ge(rotated, i + 1)
                for t in range(TILES):
                    at = (i * TILES + t) * HPC
                    ins = nc.tensor.matmul(jobs.pair("norm")[:, at:at + HPC], lhsT=sq[f"{k}{c}"][:, t * P:(t + 1) * P],
                                           rhs=w("ones")[:], start=True, stop=True)
            ins.then_inc(jobs.filled, 1)
            for k, c in chunks:
                name = f"p{k}{c}"
                jobs.wait_room(pe, name)
                for t in range(TILES):
                    ins = nc.tensor.matmul(jobs.pair(name)[:, t * P:(t + 1) * P], lhsT=x[f"{k}{c}"][:, t * P:(t + 1) * P],
                                           rhs=w("rand")[:], start=True, stop=True)
                ins.then_inc(jobs.filled, 1)
            pe.wait_ge(att_back, 16 * B)
            for c in range(KD):
                jobs.wait_room(pe, f"t{c}")
                for t in range(TILES):
                    ins = nc.tensor.transpose(jobs.pair(f"t{c}")[:, t * P:(t + 1) * P], m.h[:, t, c * P:(c + 1) * P],
                                              m.ident[:])
                ins.then_inc(jobs.filled, 1)
            pe.wait_ge(jobs.emptied["scalar"], 3)
            project_tokens(m, pe, jobs, ("out0", "out1"), lambda k, t: m.hT[:, k, t * P:(t + 1) * P],
                           lambda k, t: w("o")[:, k, :], KD)

        @block.scalar
        def _(act):
            norm_scalar(m, act, j)
            jobs.wait_filled(act, "norm")
            nc.scalar.activation(norm[:].rearrange("p a t h -> p (a t h)"),
                                 jobs.pair("norm")[:, 0:len(chunks) * TILES * HPC], ACT.Sqrt).then_inc(jobs.empty("norm"), 1)
            for i, (k, c) in enumerate(chunks):
                act.wait_ge(turns_ready, i + 1)
                f = feats[f"{k}{c}"][:]
                nc.scalar.activation(f, f, ACT.Sin, scale=SIN_SCALE).then_inc(feats_ready, 1)
            for c in range(KD):
                jobs.wait_filled(act, f"t{c}")
                nc.scalar.activation(m.hT[:, c, :], jobs.pair(f"t{c}"), ACT.Copy, scale=2.0 / HD).then_inc(jobs.empty(f"t{c}"), 1)

        @block.vector
        def _(dve):
            o = m.dve_order
            norm_vector(m, dve, n)
            m.wait_weights(dve, tag)
            tables = [w(t)[:].unsqueeze(1).to_broadcast([P, B, S]) for t in ("cos", "sin")]
            for k, c in chunks:
                b = w(k + "_b")
                half = b[:].shape[1] // 2
                rotate(m, dve, jobs, f"{k}{c}", f"{k}{c}s", tables[0], tables[1], [t[:] for t in tmp],
                       x[f"{k}{c}"][:].rearrange("p (b s) -> p b s", s=S),
                       bias=(b[:, c:c + 1], b[:, half + c:half + c + 1]))
                nc.vector.tensor_tensor(sq[f"{k}{c}"][:], x[f"{k}{c}"][:], x[f"{k}{c}"][:], ALU.mult).then_inc(rotated, 1)
            jobs.wait_filled(dve, "v")
            nc.vector.tensor_tensor(v[:], jobs.pair("v").rearrange("p (t d) -> p t d", d=P),
                                    w("v_b")[:].unsqueeze(1).to_broadcast([P, TILES, P]), ALU.add).then_inc(jobs.empty("v"), 1)
            dve.wait_ge(jobs.empty("v"), 2 * len(chunks) + 1)
            dve.sem_inc(v_ready, 1)
            dve.wait_ge(jobs.empty("norm"), 1)
            flat = norm[:].rearrange("p a t h -> p (a t h)")
            o.link(dve, nc.vector.tensor_scalar(flat, flat, 1e-6, None, ALU.max))
            o.link(dve, nc.vector.reciprocal(flat, flat))
            o.link(dve, nc.vector.tensor_scalar(flat, flat, float(1 / TWO_PI), None, ALU.mult))
            for i, (k, c) in enumerate(chunks):
                name = f"p{k}{c}"
                jobs.wait_filled(dve, name)
                f = feats[f"{k}{c}"][:]
                heads = lambda a: a.rearrange("p (x f) -> p x f", f=HD)
                r = norm[:, i, :, :].rearrange("p t h -> p (t h)").unsqueeze(2).to_broadcast([P, TILES * HPC, HD])
                nc.vector.tensor_tensor(heads(f), heads(jobs.pair(name)), r, ALU.mult).then_inc(jobs.empty(name), 1)
                dve.wait_ge(jobs.empty(name), jobs.takers[:jobs.at(name) + 1].count("vector"))
                o.link(dve, nc.vector.tensor_scalar(heads(f)[:, :, 8:16], heads(f)[:, :, 8:16], 0.25, None, ALU.add))
                o.link(dve, nc.vector.tensor_scalar(whole[:], f, ROUND, -ROUND, ALU.add, ALU.add))
                nc.vector.tensor_tensor(f, f, whole[:], ALU.subtract).then_inc(turns_ready, 1)
                dve.wait_ge(turns_ready, i + 1)
            dve.wait_ge(feats_ready, 3)

            def sum_values(c, t):
                dve.wait_ge((value_done, pool_value)[c], t + 1)
                out = att[:, t, c * P:(c + 1) * P].rearrange("p (h d) -> p h d", d=HD)
                nc.vector.tensor_reduce(out, value_prod[c][:], AX_X, ALU.add).then_inc(att_done, 1)

            for t in range(TILES):
                head_products(dve, nc.vector, 0, t, 0, pair_done)
                for c in range(KD):
                    dve.wait_ge((pair_done, pool_pair)[c], t + 1)
                    if c and t:
                        dve.wait_ge(pool_value, t)
                    nc.vector.tensor_reduce(weight[c][:], pair_prod[c][:], AX_X, ALU.add).then_inc(weight_done, 1)
                if t:
                    sum_values(1, t - 1)
                dve.wait_ge(weight_done, 2 * t + 1)
                head_products(dve, nc.vector, 0, t, 1, value_done)
                sum_values(0, t)
            sum_values(1, TILES - 1)
            add_tokens(m, dve, jobs, ("out0", "out1"), bias=w("o_b")[:])



def context_mixing(m, n, j):
    nc = m.nc
    tag = "l2x_"
    w = lambda name: m.w[tag + name]
    jobs = Jobs(m, tag + "in", 2, [("q", "scalar"), ("k", "scalar"), ("e0", "scalar"), ("e1", "scalar"),
                                   ("t0", "scalar"), ("t1", "scalar"), ("out0", "vector"), ("out1", "vector")])
    q = m.sb(tag + "q", [P, T])
    k = m.sb(tag + "k", [P, T])
    att = m.sb(tag + "att", [P, TILES, S])
    attT = m.sb(tag + "attT", [P, TILES, S])
    neg_max = m.sb(tag + "neg_max", [P, TILES])
    sums = m.sb(tag + "sums", [P, TILES])
    max_ready, att_ready = m.sem(tag + "max"), m.sem(tag + "att")
    with nc.Block(name=tag + "block") as block:
        @block.gpsimd
        def _(pool):
            norm_gpsimd(m, pool, n)

        @block.tensor
        def _(pe):
            norm_tensor(m, pe, n)
            m.wait_weights(pe, tag)
            ctx = lambda k, cols: m.ctxT[:, cols]
            for x in "qk":
                project(m, pe, jobs, x, lambda k, x=x: w(x)[:], ctx, 1)
            pe.wait_ge(jobs.emptied["scalar"], 2)
            wait_hT(m, pe, j)
            for half in range(2):
                name = f"e{half}"
                jobs.wait_room(pe, name)
                for t in range(4 * half, 4 * half + 4):
                    b = t // 2
                    ins = nc.tensor.matmul(jobs.pair(name)[:, (t % 4) * S:(t % 4 + 1) * S], lhsT=q[:, t * P:(t + 1) * P],
                                           rhs=k[:, b * S:(b + 1) * S], start=True, stop=True)
                ins.then_inc(jobs.filled, 1)
            pe.wait_ge(att_ready, 1)
            for half in range(2):
                name = f"t{half}"
                jobs.wait_room(pe, name)
                for b in range(2 * half, 2 * half + 2):
                    for nt in range(2):
                        for mt in range(2):
                            at = (b % 2 * 2 + nt) * S + mt * P
                            ins = nc.tensor.transpose(jobs.pair(name)[:, at:at + P],
                                                      att[:, 2 * b + mt, nt * P:(nt + 1) * P], m.ident[:])
                ins.then_inc(jobs.filled, 1)
            pe.wait_ge(jobs.emptied["scalar"], 6)
            project_tokens(m, pe, jobs, ("out0", "out1"), lambda k, t: m.hT[:, k, t * P:(t + 1) * P],
                           lambda k, t: attT[:, t // 2 * 2 + k, :], KD)

        @block.scalar
        def _(act):
            norm_scalar(m, act, j)
            m.wait_weights(act, tag)
            for x, dst in (("q", q), ("k", k)):
                jobs.wait_filled(act, x)
                nc.scalar.activation(dst[:], jobs.pair(x), ACT.Identity, bias=w(x + "_b")[:, 0:1]).then_inc(jobs.empty(x), 1)
            for half in range(2):
                name = f"e{half}"
                act.wait_ge(max_ready, half + 1)
                for t in range(4 * half, 4 * half + 4):
                    ins = nc.scalar.activation(att[:, t, :], jobs.pair(name)[:, (t % 4) * S:(t % 4 + 1) * S], ACT.Exp,
                                               bias=neg_max[:, t:t + 1], accum_out=sums[:, t:t + 1])
                ins.then_inc(jobs.empty(name), 1)
            for half in range(2):
                name = f"t{half}"
                jobs.wait_filled(act, name)
                nc.scalar.activation(attT[:, 4 * half:4 * half + 4, :].rearrange("p t s -> p (t s)"), jobs.pair(name),
                                     ACT.Copy).then_inc(jobs.empty(name), 1)

        @block.vector
        def _(dve):
            o = m.dve_order
            norm_vector(m, dve, n)
            for half in range(2):
                name = f"e{half}"
                jobs.wait_filled(dve, name)
                nc.vector.tensor_reduce(neg_max[:, 4 * half:4 * half + 4], jobs.pair(name).rearrange("p (t s) -> p t s", s=S),
                                        AX_X, ALU.max, negate=True).then_inc(max_ready, 1)
            dve.wait_ge(jobs.emptied["scalar"], 4)
            o.link(dve, nc.vector.reciprocal(sums[:], sums[:]))
            nc.vector.tensor_tensor(att[:], att[:], sums[:].unsqueeze(2).to_broadcast([P, TILES, S]),
                                    ALU.mult).then_inc(att_ready, 1)
            add_tokens(m, dve, jobs, ("out0", "out1"))



def gated_recurrence(m, n, j):
    nc = m.nc
    tag = "l3a_"
    w = lambda name: m.w[tag + name]
    kinds = ("in", "decay", "gate")
    jobs = Jobs(m, tag + "in", 2, [(f"{x}{c}", "scalar") for x in kinds for c in range(KD)]
                + [("out0", "vector"), ("out1", "vector")])
    val = {x: m.sb(tag + x, [P, KD, T]) for x in kinds}
    part = m.sb(tag + "part", [P, T])
    att = m.sb(tag + "att", [P, KD, T])
    bias_ready, att_ready = m.sem(tag + "bias"), m.sem(tag + "att")
    with nc.Block(name=tag + "block") as block:
        @block.gpsimd
        def _(pool):
            norm_gpsimd(m, pool, n)
            m.wait_weights(pool, tag)
            nc.gpsimd.tensor_tensor(w("decay_b")[:], w("decay_b")[:], w("decay_b2")[:], ALU.add).then_inc(bias_ready, 1)

        @block.tensor
        def _(pe):
            norm_tensor(m, pe, n)
            m.wait_weights(pe, tag)
            for x in kinds:
                for c in range(KD):
                    project(m, pe, jobs, f"{x}{c}", wcols(w(x), c), feature_rhs(m.hT), KD,
                            turn=j if x == kinds[0] and c == 0 else None)
            pe.wait_ge(att_ready, KD)
            project_tokens(m, pe, jobs, ("out0", "out1"), lambda k, t: att[:, k, t * P:(t + 1) * P],
                           lambda k, t: w("out")[:, k, :], KD)

        @block.scalar
        def _(act):
            norm_scalar(m, act, j)
            act.wait_ge(bias_ready, 1)
            for x in kinds:
                for c in range(KD):
                    name = f"{x}{c}"
                    jobs.wait_filled(act, name)
                    nc.scalar.activation(val[x][:, c, :], jobs.pair(name), ACT.Silu if x == "in" else ACT.Sigmoid,
                                         bias=w(x + "_b")[:, c:c + 1]).then_inc(jobs.empty(name), 1)

        @block.vector
        def _(dve):
            o = m.dve_order
            norm_vector(m, dve, n)
            m.wait_weights(dve, tag)
            for c in range(KD):
                x, d, g = (val[k][:, c, :] for k in kinds)
                dve.wait_ge(jobs.emptied["scalar"], 3 + c)
                o.link(dve, nc.vector.tensor_tensor(part[:], d, x, ALU.mult))
                o.mark(nc.vector.tensor_tensor(x, x, part[:], ALU.subtract))
                o.link(dve, nc.vector.tensor_tensor(d, d, m.w["carry"][:], ALU.mult))
                o.link(dve, nc.vector.tensor_tensor_scan(part[:], d, x, 0.0, ALU.mult, ALU.add))
                dve.wait_ge(jobs.emptied["scalar"], 5 + c)
                nc.vector.tensor_tensor(att[:, c, :], g, part[:], ALU.mult).then_inc(att_ready, 1)
                dve.wait_ge(att_ready, c + 1)
            add_tokens(m, dve, jobs, ("out0", "out1"), bias=w("out_b")[:])



def mx_scale(ops, x, scale):
    n = x.shape[-1] // MX_BLOCK
    blocks = x.rearrange("p (b e) -> p b e", e=MX_BLOCK)
    return ops.tensor_tensor(blocks, blocks, scale.unsqueeze(2).to_broadcast([P, n, MX_BLOCK]), ALU.mult)


def mx_round(m, eng, ops, o, x, work, scale, inv, scaled=True):
    nc = m.nc
    blocks = lambda a: a.rearrange("p (b e) -> p b e", e=MX_BLOCK)
    n = x.shape[-1] // MX_BLOCK
    spread = lambda a: a.unsqueeze(2).to_broadcast([P, n, MX_BLOCK])
    o.link(eng, nc.vector.tensor_reduce(scale, blocks(x), AX_X, ALU.max, apply_absolute_value=True))
    o.link(eng, ops.tensor_scalar(scale, scale, 1.0 / FP8_MAX, 1e-30, ALU.mult, ALU.max))
    o.link(eng, nc.vector.reciprocal(inv, scale))
    o.link(eng, ops.tensor_tensor(blocks(x), blocks(x), spread(inv), ALU.mult))
    o.link(eng, ops.tensor_scalar(work.bitcast(I32), x.bitcast(I32), 0x7F800000, None, ALU.bitwise_and))
    o.link(eng, ops.tensor_scalar(work, work, 2.0 ** -6, 1.5 * 2.0 ** 20, ALU.max, ALU.mult))
    o.link(eng, ops.tensor_tensor(x, x, work, ALU.add))
    ins = ops.tensor_tensor(x, x, work, ALU.subtract)
    if not scaled:
        return ins
    o.link(eng, ins)
    return mx_scale(ops, x, scale)


def mx_feed_forward(m, n, j):
    nc = m.nc
    tag = "l1f_"
    w = lambda name: m.w[tag + name]
    INNER = 1024
    KI = INNER // P
    natural = {x: m.sb(tag + "nat_" + x, [P, 2 * INNER]) for x in ("gate", "up", "down")}
    gateT, upT = (m.sb(tag + x + "T", [P, KD, INNER]) for x in ("gate", "up"))
    downT = m.sb(tag + "downT", [P, KI, D])
    work = m.sb(tag + "work", [P, 2 * INNER])
    scales = [m.sb(tag + f"scale{i}", [P, 2 * INNER // MX_BLOCK]) for i in range(2)]
    scale = scales[0]
    inv = m.sb(tag + "inv", [P, 2 * INNER // MX_BLOCK])
    silu = m.sb(tag + "silu", [P, INNER])
    inner = m.sb(tag + "inner", [P, INNER])
    innerT = m.sb(tag + "innerT", [P, KI, P])
    (nat_in, unscaled, w_rounded, w_turned, w_ready, h_rounded, filled, silu_done, inner_done, inner_rounded, inner_turned,
     innerT_ready, down_filled, added) = (m.sem(tag + s) for s in (
         "nat_in", "unscaled", "w_rounded", "w_turned", "w_ready", "h_rounded", "filled", "silu", "inner", "inner_rounded",
         "inner_turned", "innerT", "down", "added"))
    rounded = [(m.h[:].rearrange("p t d -> p (t d)"), h_rounded)] + [
        (natural[x][:], w_rounded) for x in ("gate", "up", "down")]
    with nc.Block(name=tag + "block") as block:
        @block.sync
        def _(sp):
            for x in ("gate", "up", "down"):
                sp.dma_start(natural[x][:], m.dram[tag + x]).then_inc(nat_in, 16)

        @block.gpsimd
        def _(pool):
            norm_gpsimd(m, pool, n)
            for i, (x, done) in enumerate(rounded):
                pool.wait_ge(unscaled, i + 1)
                mx_scale(nc.gpsimd, x, scales[i % 2][:]).then_inc(done, 1)

        @block.tensor
        def _(pe):
            def turn_weight(i):
                x = ("gate", "up", "down")[i]
                pe.wait_ge(w_rounded, i + 1)
                if i:
                    pe.wait_ge(w_ready, 2 * i)
                for k in range(2):
                    for f in range(KI):
                        if x == "down":
                            chunk, part = 4 * k + f // 2, f % 2
                            src = natural[x][:, part * INNER + chunk * P:part * INNER + (chunk + 1) * P]
                        else:
                            src = natural[x][:, f * D + k * P:f * D + (k + 1) * P]
                        ins = nc.tensor.transpose(m.pair(2 + k)[:, f * P:(f + 1) * P], src, m.ident[:])
                    ins.then_inc(w_turned, 1)

            def up(t):
                if t:
                    pe.wait_ge(inner_done, t)
                for p, wt in enumerate((gateT, upT)):
                    for half in range(2):
                        if t and p and half:
                            turn(t - 1)
                        for k in range(KD):
                            cols = slice(half * 512, (half + 1) * 512)
                            ins = nc.tensor.matmul(m.pair(p)[:, cols], lhsT=m.hT[:, k, t * P:(t + 1) * P], rhs=wt[:, k, cols],
                                                   start=(k == 0), stop=(k == KD - 1))
                    ins.then_inc(filled, 1)

            def turn(t):
                pe.wait_ge(inner_rounded, t + 1)
                if t:
                    pe.wait_ge(innerT_ready, t)
                for f in range(KI):
                    ins = nc.tensor.transpose(m.pair(2)[:, f * P:(f + 1) * P], inner[:, f * P:(f + 1) * P], m.ident[:])
                ins.then_inc(inner_turned, 1)

            def down(t):
                pe.wait_ge(innerT_ready, t + 1)
                if t:
                    pe.wait_ge(added, t)
                for f in range(KI):
                    ins = nc.tensor.matmul(m.pair(3)[:, 0:D], lhsT=innerT[:, f, :], rhs=downT[:, f, :], start=(f == 0),
                                           stop=(f == KI - 1))
                ins.then_inc(down_filled, 1)

            pe.wait_ge(h_rounded, 1)
            for half in range(2):
                for t in range(4 * half, 4 * half + 4):
                    for k in range(KD):
                        ins = nc.tensor.transpose(m.pair(k)[:, t * P:(t + 1) * P], m.h[:, t, k * P:(k + 1) * P], m.ident[:])
                ins.then_inc(m.turned, 1)
            turn_weight(0)
            turn_weight(1)
            wait_hT(m, pe, j)
            pe.wait_ge(w_ready, 4)
            up(0)
            turn_weight(2)
            pe.wait_ge(w_ready, 6)
            for t in range(1, TILES):
                up(t)
                down(t - 1)
            turn(TILES - 1)
            down(TILES - 1)

        @block.scalar
        def _(act):
            def copy_weight(i):
                for k in range(2):
                    act.wait_ge(w_turned, 2 * i + k + 1)
                    dst = (gateT[:, k, :], upT[:, k, :],
                           downT[:, 4 * k:4 * k + 4, :].rearrange("p f d -> p (f d)"))[i]
                    nc.scalar.activation(dst, m.pair(2 + k), ACT.Copy).then_inc(w_ready, 1)

            def copy_inner(t):
                act.wait_ge(inner_turned, t + 1)
                if t:
                    act.wait_ge(down_filled, t)
                nc.scalar.activation(innerT[:].rearrange("p f t -> p (f t)"), m.pair(2), ACT.Copy).then_inc(innerT_ready, 1)

            norm_scalar(m, act, j)
            copy_weight(0)
            copy_weight(1)
            for t in range(TILES):
                act.wait_ge(filled, 2 * t + 1)
                if t:
                    act.wait_ge(inner_done, t)
                nc.scalar.activation(silu[:], m.pair(0), ACT.Silu).then_inc(silu_done, 1)
                if t:
                    copy_inner(t - 1)
                else:
                    copy_weight(2)
            copy_inner(TILES - 1)

        @block.vector
        def _(dve):
            o = m.dve_order
            norm_vector(m, dve, n)
            dve.wait_ge(m.h_ready, TILES * (n + 1))
            for i, (x, done) in enumerate(rounded):
                if i == 1:
                    dve.wait_ge(nat_in, 48)
                if i == 2:
                    dve.wait_ge(h_rounded, 1)
                if i == 3:
                    dve.wait_ge(w_rounded, 1)
                mx_round(m, dve, nc.vector, o, x, work[:], scales[i % 2][:], inv[:], scaled=False).then_inc(unscaled, 1)
                dve.wait_ge(unscaled, i + 1)
            dve.wait_ge(w_rounded, 2)

            def add(t):
                dve.wait_ge(down_filled, t + 1)
                nc.vector.tensor_tensor(m.resid[:, t, :], m.pair(3)[:, 0:D], m.resid[:, t, :], ALU.add).then_inc(added, 1)

            for t in range(TILES):
                dve.wait_ge(silu_done, t + 1)
                dve.wait_ge(filled, 2 * t + 2)
                if t:
                    dve.wait_ge(inner_turned, t)
                nc.vector.tensor_tensor(inner[:], silu[:], m.pair(1), ALU.mult).then_inc(inner_done, 1)
                dve.wait_ge(inner_done, t + 1)
                nb = INNER // MX_BLOCK
                mx_round(m, dve, nc.vector, o, inner[:], work[:, 0:INNER], scale[:, 0:nb],
                         inv[:, 0:nb]).then_inc(inner_rounded, 1)
                dve.wait_ge(inner_rounded, t + 1)
                if t:
                    add(t - 1)
            add(TILES - 1)



def weights(m):
    m.weight("consts", "ident", [P, P])
    m.ident = m.w["ident"]
    m.weight("consts", "carry", [P, T])
    m.weight("consts", "ctxT", [P, T])
    m.ctxT = m.w["ctxT"]
    for name, shape in (("iota", [P, P]), ("token", [P, TILES]), ("earlier", [P, P]), ("ones", [P, P])):
        m.weight("routing", name, shape)
    m.weight("l0_attn", "l0_qkv", [P, KD, 3 * D])
    m.weight("l0_attn", "l0_out", [P, KD, D])
    for layer in (0, 1):
        g = f"l{layer}s_"
        for name, shape in (("in", [P, D]), ("conv", [P, KD, D_CONV]), ("conv_b", [P, KD]), ("x", [P, KD, X_DBL]),
                            ("dt", [DT_RANK, D]), ("dt_b", [P, KD]), ("a", [P, KD, N_STATE]), ("d", [P, KD])):
            m.weight(g, g + name, shape)
    for group, name, shape in LATER_WEIGHTS:
        m.weight(group, name, shape)


LATER_WEIGHTS = [
    ("l0f_", "l0f_router", [P, KD, 16]), ("l2f_", "l2f_router", [P, KD, 9]), ("l3f_", "l3f_router", [P, KD, 64]),
    ("l1a_", "l1a_q", [P, KD, 2 * D]), ("l1a_", "l1a_k", [P, KD, 2 * D]), ("l1a_", "l1a_v", [P, KD, D]),
    ("l1a_", "l1a_o", [P, KD, D]), ("l1a_", "l1a_cos", [P, S]), ("l1a_", "l1a_sin", [P, S]),
    ("l1a_", "causal", [P, P]),
    ("l2a_", "l2a_q", [P, KD, 2 * D]), ("l2a_", "l2a_k", [P, KD, D]), ("l2a_", "l2a_v", [P, KD, P]),
    ("l2a_", "l2a_o", [P, KD, D]), ("l2a_", "l2a_cos", [P, S]), ("l2a_", "l2a_sin", [P, S]),
    ("l2a_", "l2a_q_b", [P, 2 * KD]), ("l2a_", "l2a_k_b", [P, 2]), ("l2a_", "l2a_v_b", [P, P]),
    ("l2a_", "l2a_o_b", [P, D]), ("l2a_", "l2a_rand", [P, P]), ("l2a_", "l2a_ones", [P, 8]),
    ("l2x_", "l2x_q", [P, P]), ("l2x_", "l2x_k", [P, P]), ("l2x_", "l2x_q_b", [P, 1]), ("l2x_", "l2x_k_b", [P, 1]),
    ("l3a_", "l3a_in", [P, KD, D]), ("l3a_", "l3a_decay", [P, KD, D]), ("l3a_", "l3a_gate", [P, KD, D]),
    ("l3a_", "l3a_out", [P, KD, D]), ("l3a_", "l3a_in_b", [P, KD]), ("l3a_", "l3a_decay_b", [P, KD]),
    ("l3a_", "l3a_decay_b2", [P, KD]), ("l3a_", "l3a_gate_b", [P, KD]), ("l3a_", "l3a_out_b", [P, D]),
    ("l3x_", "l3x_q", [P, KD, 2 * D]), ("l3x_", "l3x_k", [P, 1, 2 * D]), ("l3x_", "l3x_v", [P, 1, D]),
    ("l3x_", "l3x_o", [P, KD, D]), ("l3x_", "l3x_o_b", [P, D]), ("l3x_", "l3x_freq", [2, P]),
    ("l3x_", "l3x_pos", [2, T]),
]
FIRST_WEIGHTS = ("consts", "l0_attn")


def decoder(nc, dram, out):
    with ExitStack() as ctx:
        m = Machine(nc, ctx, dram)
        weights(m)
        loaded_x = m.sem("loaded_x")
        m.gather_sems = {tag: ([m.sem(tag + f"x_loaded{i}") for i in range(GROUP)],
                               [m.sem(tag + f"back_loaded{i}") for i in range(TILES)])
                         for tag in ("l0f_", "l2f_", "l3f_")}
        stored = m.sem("stored")
        with nc.Block(name="load_x") as block:
            @block.sync
            def _(sp):
                sp.dma_start(m.resid[:], dram["x"]).then_inc(loaded_x, 16)
                m.load_weights(sp, FIRST_WEIGHTS)
                sp.wait_ge(loaded_x, 16)

            @block.gpsimd
            def _(pool):
                nc.gpsimd.memset(m.minus_half[:], -0.5)

        stages = [
            lambda n, j: linear_attention(m, n, j),
            lambda n, j: state_space(m, 0, n),
            lambda n, j: experts(m, n, j, "l0f_", routed=16, top=6, rows=88, chunks=2),
            lambda n, j: softmax_attention(m, n, j, "l1a_", heads=16, causal=True),
            lambda n, j: state_space(m, 1, n),
            lambda n, j: mx_feed_forward(m, n, j),
            lambda n, j: feature_attention(m, n, j),
            lambda n, j: context_mixing(m, n, j),
            lambda n, j: experts(m, n, j, "l2f_", routed=8, top=2, rows=88, chunks=2, shared=4, normalize=True),
            lambda n, j: gated_recurrence(m, n, j),
            lambda n, j: softmax_attention(m, n, j, "l3x_", heads=32, causal=False),
            lambda n, j: experts(m, n, j, "l3f_", routed=64, top=4, rows=96, chunks=1, normalize=True, floor=1e-12),
        ]
        first = nc.free_semaphores[0]
        m.first_stage_sem = first
        j = 0
        for n, stage in enumerate(stages):
            with ExitStack() as scope:
                outer, m.ctx, m.stage_sems = m.ctx, scope, 0
                stage(n, j)
                if n not in (1, 4):
                    j += 1
                with nc.Block(name=f"clear{n}") as block:
                    @block.sync
                    def _(sp):
                        sp.sem_clear(range(first, first + m.stage_sems))
                m.ctx, m.stage_sems = outer, None

        with nc.Block(name="store") as block:
            @block.sync
            def _(sp):
                for group in m.w_loaded:
                    m.wait_weights(sp, group)
                sp.dma_start(out, m.resid[:]).then_inc(stored, 16)
                sp.wait_ge(stored, 16)


def rows_to_chunks(a):
    return np.ascontiguousarray(a.reshape(-1, P, a.shape[-1]).transpose(1, 0, 2))


def column(a):
    return np.ascontiguousarray(a.reshape(-1, P).T)


def constants():
    c = {}
    c["ident"] = np.eye(P, dtype=np.float32)
    carry = np.ones((P, T), np.float32)
    carry[:, ::S] = 0
    c["carry"] = carry
    c["iota"] = np.broadcast_to(np.arange(P, dtype=np.float32), (P, P)).copy()
    c["token"] = (np.arange(P)[:, None] + P * np.arange(TILES)[None, :]).astype(np.float32)
    c["earlier"] = np.triu(np.ones((P, P), np.float32), 1)
    c["ones"] = np.ones((P, P), np.float32)
    f = np.arange(P)
    c["causal"] = np.where(np.arange(P)[None, :] > np.arange(P)[:, None], np.float32(-1e30), np.float32(0))
    step = np.arange(S, dtype=np.float32)
    inv = (np.float32(10000.0) ** (-(np.arange(0, 16, 2, dtype=np.float32) / np.float32(16)))).astype(np.float32)
    ang = inv[f % 16 // 2][:, None] * step[None, :]
    c["l1a_cos"] = np.cos(ang)
    c["l1a_sin"] = np.sin(ang) * np.where(f % 2, 1, -1).astype(np.float32)[:, None]
    ang = inv[f % 8][:, None] * step[None, :]
    c["l2a_cos"] = np.cos(ang)
    c["l2a_sin"] = np.sin(ang) * np.where(f % 16 < 8, -1, 1).astype(np.float32)[:, None]
    same = (f[:, None] // 16 == f[None, :] // 16).astype(np.float32)
    c["l2a_ones"] = np.ascontiguousarray(same[:, ::16])
    freq = 10000.0 ** -(np.arange(2) / 2)
    axis, which = f % 8 // 4, f % 4 // 2
    turns = freq[which] / TWO_PI * np.where(f % 2, 1, -1)
    c["l3x_freq"] = np.where(axis[None, :] == np.arange(2)[:, None], turns[None, :], 0).astype(np.float32)
    return c


def layouts(i):
    d = {}
    tok = lambda a: np.ascontiguousarray(a.reshape(TILES, P, -1).transpose(1, 0, 2))
    d["x"] = tok(i["x"])
    d["ctxT"] = np.ascontiguousarray(i["ctx_1024"].reshape(T, CTX).T)
    d["l0_qkv"] = rows_to_chunks(i["L0_attn_W_qkv"].T)
    d["l0_out"] = rows_to_chunks(i["L0_attn_W_out"].T)
    for layer in (0, 1):
        g, s = f"l{layer}s_", f"L{layer}_xattn_"
        d[g + "in"] = np.ascontiguousarray(i[s + "in_proj_w"].T)
        d[g + "conv"] = rows_to_chunks(i[s + "conv_w"].reshape(D, D_CONV))
        d[g + "conv_b"] = column(i[s + "conv_b"])
        d[g + "x"] = rows_to_chunks(i[s + "x_proj_w"].T)
        d[g + "dt"] = np.ascontiguousarray(i[s + "dt_proj_w"].T)
        d[g + "dt_b"] = column(i[s + "dt_proj_b"])
        d[g + "a"] = rows_to_chunks(i[s + "A_log"])
        d[g + "d"] = column(i[s + "D"])
    across = lambda a: np.ascontiguousarray(np.broadcast_to(a[None, :], (P, a.shape[0])))
    pairs = np.arange(D) ^ 1
    halves = np.arange(D) ^ 8
    both = lambda a, order: rows_to_chunks(np.concatenate([a, a[:, order]], axis=1))
    for x in "qk":
        d["l1a_" + x] = both(i["L1_attn_w" + x].T, pairs)
    d["l1a_v"] = rows_to_chunks(i["L1_attn_wv"].T)
    d["l1a_o"] = rows_to_chunks(i["L1_attn_wo"].T)
    for x in "qk":
        b = i["L2_attn_b" + x]
        d["l2a_" + x] = both(i["L2_attn_W" + x].T, halves[:len(b)])
        d[f"l2a_{x}_b"] = column(np.concatenate([b, b[halves[:len(b)]]]))
    d["l2a_v"] = rows_to_chunks(i["L2_attn_Wv"].T)
    d["l2a_v_b"] = across(i["L2_attn_bv"])
    d["l2a_o"] = rows_to_chunks(i["L2_attn_Wo"].T)
    d["l2a_o_b"] = across(i["L2_attn_bo"])
    rand = np.zeros((P, P), np.float32)
    for h in range(8):
        for part in range(2):
            rand[16 * h:16 * h + 16, 16 * h + 8 * part:16 * h + 8 * part + 8] = i["L2_attn_rand_matrix"].T
    d["l2a_rand"] = rand
    for x in "qk":
        d["l2x_" + x] = np.ascontiguousarray(i["L2_xattn_W" + x].T)
        d[f"l2x_{x}_b"] = column(i["L2_xattn_b" + x])
    for x in ("in", "decay", "gate", "out"):
        d["l3a_" + x] = rows_to_chunks(i["L3_attn_W_" + x])
    for x in ("in", "decay", "gate"):
        d[f"l3a_{x}_b"] = column(i["L3_attn_b_" + x])
    d["l3a_decay_b2"] = column(i["L3_attn_decay_bias"])
    d["l3a_out_b"] = across(i["L3_attn_b_out"])
    d["l3x_q"] = both(i["L3_xattn_Wq"], pairs)
    d["l3x_k"] = both(i["L3_xattn_Wkv"][:, :D], pairs)
    d["l3x_v"] = rows_to_chunks(i["L3_xattn_Wkv"][:, D:])
    d["l3x_o"] = rows_to_chunks(i["L3_xattn_Wout"])
    d["l3x_o_b"] = across(i["L3_xattn_bout"])
    d["l3x_pos"] = np.ascontiguousarray(i["fside_BxSx2_0"].reshape(T, 2).T)
    for x in ("gate", "up", "down"):
        d["l1f_" + x] = np.ascontiguousarray(rows_to_chunks(i[f"L1_ffn_{x}_w"]).reshape(P, -1))
    up_rows = lambda a: np.ascontiguousarray(a.reshape(a.shape[0], KD, P, -1).transpose(0, 2, 1, 3)).reshape(
        a.shape[0], P, -1)
    down_rows = lambda a, n: np.ascontiguousarray(a.reshape(a.shape[0], n, -1, D).transpose(0, 2, 1, 3)).reshape(
        a.shape[0], a.shape[1] // n, -1)
    d["l0f_router"] = rows_to_chunks(i["L0_ffn_gate_w"].T)
    d["l0f_w_in"] = up_rows(np.concatenate([i["L0_ffn_w_gate"], i["L0_ffn_w_up"]], axis=1).transpose(0, 2, 1))
    d["l0f_w_down"] = down_rows(i["L0_ffn_w_down"].transpose(0, 2, 1), 2)
    d["l2f_router"] = rows_to_chunks(np.concatenate([i["L2_ffn_gate_w"].T, i["L2_ffn_shared_gate_w"]], axis=1))
    cut = lambda a: a.reshape(D, 4, -1).transpose(1, 0, 2)
    gate = np.concatenate([i["L2_ffn_w_gate"], cut(i["L2_ffn_sw_gate"])])
    up = np.concatenate([i["L2_ffn_w_up"], cut(i["L2_ffn_sw_up"])])
    d["l2f_w_in"] = up_rows(np.concatenate([gate, up], axis=2))
    d["l2f_w_down"] = down_rows(np.concatenate([i["L2_ffn_w_down"], i["L2_ffn_sw_down"].reshape(4, -1, D)]), 2)
    d["l3f_router"] = rows_to_chunks(i["L3_ffn_gate_weight"].T)
    d["l3f_w_in"] = up_rows(i["L3_ffn_gate_up_proj"].transpose(0, 2, 1))
    d["l3f_w_down"] = down_rows(i["L3_ffn_down_proj"].transpose(0, 2, 1), 1)
    return d


def kernel(**inputs):
    import concourse.bacc as bacc
    from concourse.bass_utils import run_bass_kernel_spmd

    arrays = {**constants(), **layouts({k: np.asarray(v) for k, v in inputs.items()})}
    nc = bacc.Bacc("TRN2", target_bir_lowering=False, num_devices=1)
    dram = {n: nc.dram_tensor("in_" + n, a.shape, mybir.dt.from_np(a.dtype), kind="ExternalInput").ap()
            for n, a in arrays.items()}
    out = nc.dram_tensor("out_0", (P, TILES, D), F32, kind="ExternalOutput").ap()
    decoder(nc, dram, out)
    r = run_bass_kernel_spmd(nc, [{"in_" + n: a for n, a in arrays.items()}], core_ids=[0])
    y = r.results[0]["out_0"]
    return np.ascontiguousarray(y.transpose(1, 0, 2)).reshape(B, S, D)
```
